# Optimizing a Trainium2 kernel written in Bass

```python
import numpy as np
import jax
import jax.numpy as jnp

def _softmax(x, axis=-1):
    return jax.nn.softmax(x, axis=axis)

def _gelu(x):
    return jax.nn.gelu(x, approximate=True)

def _silu(x):
    return jax.nn.silu(x)

def _sigmoid(x):
    return jax.nn.sigmoid(x)

def _layernorm(x, axis=-1, eps=1e-05):
    m = jnp.mean(x, axis=axis, keepdims=True)
    v = jnp.var(x, axis=axis, keepdims=True)
    return (x - m) / jnp.sqrt(v + eps)

def _scatter_add(tgt, idx, src, axis=0):
    return tgt.at[idx].add(src)

def _segment_sum(src, seg, n):
    return jax.ops.segment_sum(src, seg, n)
kernel_name = 'mk_gps_d1_gnn_r8_ea4e23'

def setup_inputs(seed: int=0):
    np.random.seed(seed)
    _w = jnp.asarray

    def _rec_inputs():
        import jax
        import jax.numpy as jnp
        _gk = jax.random.key(seed)
        x = -0.0002117 + 1 * jax.random.normal(jax.random.fold_in(_gk, 1), (12500, 256), jnp.float32)
        _s = jax.random.randint(jax.random.fold_in(_gk, 2), (100000,), 0, 12500, jnp.int32)
        _d = jax.random.randint(jax.random.fold_in(_gk, 3), (100000,), 0, 12500, jnp.int32)
        _loop = jnp.arange(12500, dtype=jnp.int32)
        src = jnp.concatenate([_s, _d, _loop])
        dst = jnp.concatenate([_d, _s, _loop])
        _o = jnp.argsort(dst, stable=True)
        src = src[_o]
        dst = dst[_o]
        edge_weight = jax.random.uniform(jax.random.fold_in(_gk, 12), (212500,), jnp.float32, 0.0, 1)
        return (x, src, dst, edge_weight)
    x, src, dst, edge_weight = _rec_inputs()

    def _L0_gnn_setup():
        import jax, jax.numpy as jnp
        import numpy as np
        N_NODES = 12500
        N_EDGES = 400000
        D_IN = 256
        D_OUT = 256
        key = jax.random.key(seed)
        k1, k2, k3, k4, k5 = jax.random.split(key, 5)
        x = jax.random.normal(k1, (N_NODES, D_IN), dtype=jnp.float32)
        weight = jax.random.normal(k2, (D_IN, D_OUT), dtype=jnp.float32) * (1.0 / np.sqrt(D_IN))
        adj_val = jax.random.uniform(k3, (N_EDGES,), dtype=jnp.float32)
        edge_row = jax.random.randint(k4, (N_EDGES,), 0, N_NODES, dtype=jnp.int32)
        edge_col = jax.random.randint(k5, (N_EDGES,), 0, N_NODES, dtype=jnp.int32)
        return {'x': x, 'weight': weight, 'adj_val': adj_val, 'edge_row': edge_row, 'edge_col': edge_col}
    _L0_gnn_all = _L0_gnn_setup()
    _L0_gnn_in = {k: v for k, v in _L0_gnn_all.items() if k in ('weight',)}
    del _L0_gnn_all

    def _L0_mix_setup():
        import jax, jax.numpy as jnp
        import numpy as np
        N, F, C, H = (32, 512, 256, 8)
        D = C // H
        EPS_ATTN = 1e-06
        EPS_LN = 1e-05

        def layer_norm(x, g, b):
            mu = jnp.mean(x, axis=-1, keepdims=True)
            var = jnp.var(x, axis=-1, keepdims=True)
            return (x - mu) * jax.lax.rsqrt(var + EPS_LN) * g + b
        key = jax.random.key(seed)
        ks = jax.random.split(key, 8)
        s = 1.0 / np.sqrt(C)
        return {'x': jax.random.normal(ks[0], (N, F, C), jnp.float32), 'Wqkv': jax.random.uniform(ks[1], (3 * C, C), jnp.float32, -s, s), 'ln1_g': jnp.ones((C,), jnp.float32), 'ln1_b': jnp.zeros((C,), jnp.float32), 'W1': jax.random.uniform(ks[2], (C, C), jnp.float32, -s, s), 'b1': jax.random.uniform(ks[3], (C,), jnp.float32, -s, s), 'W2': jax.random.uniform(ks[4], (C, C), jnp.float32, -s, s), 'b2': jax.random.uniform(ks[5], (C,), jnp.float32, -s, s), 'ln2_g': jnp.ones((C,), jnp.float32), 'ln2_b': jnp.zeros((C,), jnp.float32)}
    _L0_mix_all = _L0_mix_setup()
    _L0_mix_in = {k: v for k, v in _L0_mix_all.items() if k in ('Wqkv', 'ln1_g', 'ln1_b', 'W1', 'b1', 'W2', 'b2', 'ln2_g', 'ln2_b')}
    del _L0_mix_all

    def _L0_ffn_setup():
        import jax, jax.numpy as jnp
        import numpy as np
        B, S, D = (8, 512, 256)
        H = 4 * D
        CAPACITY = 0.5
        key = jax.random.key(seed)
        ks = jax.random.split(key, 6)
        x = jax.random.normal(ks[0], (B, S, D), dtype=jnp.float32)
        attention_mask = jnp.zeros((B, 1, 1, S), dtype=jnp.float32)
        wr = jax.random.normal(ks[1], (D, 1), dtype=jnp.float32) * 0.02
        br = jnp.zeros((1,), dtype=jnp.float32)
        w1 = jax.random.normal(ks[2], (D, H), dtype=jnp.float32) * 0.02
        b1 = jnp.zeros((H,), dtype=jnp.float32)
        w2 = jax.random.normal(ks[3], (H, D), dtype=jnp.float32) * 0.02
        b2 = jnp.zeros((D,), dtype=jnp.float32)
        return {'x': x, 'attention_mask': attention_mask, 'wr': wr, 'br': br, 'w1': w1, 'b1': b1, 'w2': w2, 'b2': b2}
    _L0_ffn_all = _L0_ffn_setup()
    _L0_ffn_in = {k: v for k, v in _L0_ffn_all.items() if k in ('attention_mask', 'wr', 'br', 'w1', 'b1', 'w2', 'b2')}
    del _L0_ffn_all
    return {'x': x, 'src': src, 'dst': dst, 'edge_weight': edge_weight, 'L0_gnn_weight': _L0_gnn_in['weight'], 'L0_mix_Wqkv': _L0_mix_in['Wqkv'], 'L0_mix_ln1_g': _L0_mix_in['ln1_g'], 'L0_mix_ln1_b': _L0_mix_in['ln1_b'], 'L0_mix_W1': _L0_mix_in['W1'], 'L0_mix_b1': _L0_mix_in['b1'], 'L0_mix_W2': _L0_mix_in['W2'], 'L0_mix_b2': _L0_mix_in['b2'], 'L0_mix_ln2_g': _L0_mix_in['ln2_g'], 'L0_mix_ln2_b': _L0_mix_in['ln2_b'], 'L0_ffn_attention_mask': _L0_ffn_in['attention_mask'], 'L0_ffn_wr': _L0_ffn_in['wr'], 'L0_ffn_br': _L0_ffn_in['br'], 'L0_ffn_w1': _L0_ffn_in['w1'], 'L0_ffn_b1': _L0_ffn_in['b1'], 'L0_ffn_w2': _L0_ffn_in['w2'], 'L0_ffn_b2': _L0_ffn_in['b2']}

def reference(x, src, dst, edge_weight, L0_gnn_weight, L0_mix_Wqkv, L0_mix_ln1_g, L0_mix_ln1_b, L0_mix_W1, L0_mix_b1, L0_mix_W2, L0_mix_b2, L0_mix_ln2_g, L0_mix_ln2_b, L0_ffn_attention_mask, L0_ffn_wr, L0_ffn_br, L0_ffn_w1, L0_ffn_b1, L0_ffn_w2, L0_ffn_b2):
    import jax
    import jax.numpy as jnp

    def _L0_gnn_ref(x, weight, adj_val, edge_row, edge_col):
        import jax, jax.numpy as jnp
        import numpy as np
        N_NODES = 12500
        N_EDGES = 400000
        D_IN = 256
        D_OUT = 256
        support = jnp.matmul(x, weight)
        msgs = adj_val[:, None] * support[edge_col]
        out = jax.ops.segment_sum(msgs, edge_row, num_segments=x.shape[0])
        return out

    def _L0_mix_ref(x, Wqkv, ln1_g, ln1_b, W1, b1, W2, b2, ln2_g, ln2_b):
        import jax, jax.numpy as jnp
        import numpy as np
        N, F, C, H = (32, 512, 256, 8)
        D = C // H
        EPS_ATTN = 1e-06
        EPS_LN = 1e-05

        def layer_norm(x, g, b):
            mu = jnp.mean(x, axis=-1, keepdims=True)
            var = jnp.var(x, axis=-1, keepdims=True)
            return (x - mu) * jax.lax.rsqrt(var + EPS_LN) * g + b
        n, f, c = x.shape
        qkv = jnp.einsum('nfc,oc->nfo', x, Wqkv)
        q, k, v = jnp.split(qkv, 3, axis=-1)
        q = q.reshape(n, f, H, D)
        k = k.reshape(n, f, H, D)
        v = v.reshape(n, f, H, D)
        q = jax.nn.elu(q) + 1.0
        k = jax.nn.elu(k) + 1.0
        kv = jnp.einsum('nshd,nshm->nhmd', k, v)
        ksum = jnp.sum(k, axis=1)
        z = 1.0 / (jnp.einsum('nlhd,nhd->nlh', q, ksum) + EPS_ATTN)
        t = jnp.einsum('nlhd,nhmd,nlh->nlhm', q, kv, z)
        t = t.reshape(n, f, c)
        x1 = layer_norm(t + x, ln1_g, ln1_b)
        h = jax.nn.gelu(jnp.einsum('nfc,oc->nfo', x1, W1) + b1, approximate=False)
        y = jnp.einsum('nfc,oc->nfo', h, W2) + b2
        return layer_norm(y + x1, ln2_g, ln2_b)

    def _L0_ffn_ref(x, attention_mask, wr, br, w1, b1, w2, b2):
        import jax, jax.numpy as jnp
        import numpy as np
        B, S, D = (8, 512, 256)
        H = 4 * D
        CAPACITY = 0.5
        b, s, d = x.shape
        weights = (jnp.einsum('bsd,do->bso', x, wr) + br)[..., 0]
        k = max(1, int(CAPACITY * s))
        kk = k - 1 if k > 1 else 1
        _, idx = jax.lax.top_k(weights, k)
        sel_idx = idx[:, :kk]
        sel = jnp.take_along_axis(x, sel_idx[:, :, None], axis=1)
        h = jax.nn.gelu(jnp.einsum('bkd,dh->bkh', sel, w1) + b1)
        y = jnp.einsum('bkh,hd->bkd', h, w2) + b2
        w_sel = jnp.take_along_axis(weights, sel_idx, axis=1)
        y = y * w_sel[..., None]
        batch_idx = jnp.arange(b)[:, None]
        processed = jnp.zeros_like(x).at[batch_idx, sel_idx].set(y)
        return processed + x
    xn = _layernorm(x, axis=-1)
    x = x + _L0_gnn_ref(xn, L0_gnn_weight, edge_weight, src, dst) + _L0_mix_ref(xn[None], L0_mix_Wqkv, L0_mix_ln1_g, L0_mix_ln1_b, L0_mix_W1, L0_mix_b1, L0_mix_W2, L0_mix_b2, L0_mix_ln2_g, L0_mix_ln2_b)[0]
    x = x + _L0_ffn_ref(_layernorm(x, axis=-1)[None], L0_ffn_attention_mask, L0_ffn_wr, L0_ffn_br, L0_ffn_w1, L0_ffn_b1, L0_ffn_w2, L0_ffn_b2)[0]
    return x

_drawn_inputs = setup_inputs


def setup_inputs(seed=0):
    import zlib

    import numpy as np

    out = dict(_drawn_inputs(seed))
    spreads = {'L0_mix_ln1_g': (1.0, 0.2),
     'L0_mix_ln1_b': (0.0, 0.1),
     'L0_mix_ln2_g': (1.0, 0.2),
     'L0_mix_ln2_b': (0.0, 0.1),
     'L0_ffn_b1': (0.0, 0.8),
     'L0_ffn_b2': (0.0, 0.8)}
    factors = {'L0_mix_Wqkv': 8.0,
     'L0_mix_b1': 8.0,
     'L0_mix_b2': 4.975,
     'L0_ffn_wr': 7.492,
     'L0_ffn_w1': 7.657,
     'L0_ffn_w2': 7.162}
    for name, (base, spread) in spreads.items():
        noise = np.random.default_rng([zlib.crc32(name.encode()), seed]).standard_normal(out[name].shape)
        drawn = base * np.exp(spread * noise) if base else spread * noise
        out[name] = jnp.asarray(drawn.astype(out[name].dtype))
    for name, factor in factors.items():
        out[name] = (out[name] * factor).astype(out[name].dtype)
    return out
```

```python
import concourse.bass as bass
from concourse import mybir
from contextlib import ExitStack
import numpy as np

N, C, E, HEADS, HID, NQKV = 12500, 256, 212500, 8, 1024, 768
P = 128
CC = C // P
NT = (N + P - 1) // P
LASTROWS = N - (NT - 1) * P
KEEP = max(1, int(0.5 * N)) - 1
EPS_LN, EPS_ATTN = 1e-5, 1e-6

BT = 4
BE = BT * P
KB = 4
EQ = -(-E // (BE * KB))
NB = EQ * KB
ET = NB * BT
EJ = ET // P
EPAD = ET * P

GS = 256
RW = C + 2
RG = 8
NGMAX = (EPAD + NT * (GS - 1)) // GS
NGROUPS = 1 + NGMAX + RG + 1
GJ = -(-NGROUPS // P)

G = 7
NG = NT // G


def gps_layer_kernel(nc, x, src, dst, edge_weight, gnn_w, wqkv, ln1_g, ln1_b, w1, b1, w2, b2,
                     ln2_g, ln2_b, wr, br, fw1, fb1, fw2, fb2, out):
    F32, BF16, F16, I32, U32 = (mybir.dt.float32, mybir.dt.bfloat16, mybir.dt.float16, mybir.dt.int32,
                                mybir.dt.uint32)
    ALU, ACT, AX = mybir.AluOpType, mybir.ActivationFunctionType, mybir.AxisListType
    ds = bass.ds
    SIGN = -2147483648
    LOW = 2048
    NEWTON = 2 + 4 * 3

    src_d = nc.dram_tensor("src_pad", [EPAD], I32).ap()
    dst_d = nc.dram_tensor("dst_pad", [EPAD], I32).ap()
    ew_d = nc.dram_tensor("weight_pad", [EPAD], F32).ap()
    xn_d = nc.dram_tensor("xn_rows", [NT * P, C], F32).ap()
    xnT_d = nc.dram_tensor("xn_transposed", [NT, P, C], F32).ap()
    sup_d = nc.dram_tensor("support_rows", [(NT + 1) * P, C], F32).ap()
    qT_d = nc.dram_tensor("q_transposed", [NT, P, C], F32).ap()
    rows_d = nc.dram_tensor("sorted_rows", [NGROUPS * GS, RW], F32).ap()
    gb_d = nc.dram_tensor("group_bucket", [GJ * P], I32).ap()

    with ExitStack() as ctx:
        def sb(name, shape, dt=F32):
            return ctx.enter_context(nc.sbuf_tensor(name, shape, dt))

        def sem(name):
            return ctx.enter_context(nc.semaphore(name))

        acc = sb("acc", [P, NT * C])
        tabs = sb("tabs", [P, 4 * ET])
        ws_t = tabs[:, 0:2 * ET].rearrange("p (t k) -> p t k", k=2)
        bkt_t = tabs[:, 2 * ET:3 * ET]
        dst_t = tabs[:, 3 * ET:4 * ET].bitcast(U32)
        fw1_s = tabs[:, 0:CC * HID].rearrange("p (c h) -> p c h", c=CC)
        fw2_s = tabs[:, CC * HID:2 * CC * HID].rearrange("p (k c) -> p k c", c=C)
        rel = sb("rel", [EQ, KB * BE], F16)
        d0_row = sb("d0_row", [1, NB], I32)
        wqkvT = sb("wqkvT", [P, CC, NQKV])
        gw_s = sb("gw_s", [P, CC, C])
        w1T = sb("w1T", [P, CC, C])
        w2T = sb("w2T", [P, CC, C])
        vec = sb("vec", [P, 7, C])
        LN1G, LN1B, LN2G, LN2B, B2, FB2, WR = range(7)
        b1_c = sb("b1_c", [P, CC])
        fb1_c = sb("fb1_c", [P, HID // P])
        br_c = sb("br_c", [P, 1])
        ident = sb("ident", [P, P])
        ident_h = sb("ident_h", [P, P], F16)
        ident_hi = sb("ident_hi", [P, P], F16)
        onecol = sb("onecol", [P, 2 * EQ], BF16)
        first_lo = sb("first_lo", [EQ, BT * NT], F16)
        first_hi = sb("first_hi", [EQ, BT * NT], F16)
        before = sb("before", [P, P], BF16)
        ones_b = sb("ones_b", [P, P], BF16)
        zeros_b = sb("zeros_b", [P, 512], BF16)
        onesf = sb("onesf", [P, P])
        lane = sb("lane", [P, 1])
        cols = sb("cols", [P, P])
        kvb = sb("kvb", [P, CC, P + 4])
        maskc = sb("maskc", [P, NT])
        meta = sb("meta", [P, 4], I32)
        gb_row = sb("gb_row", [1, GJ * P], I32)
        rowbuf = sb("rowbuf", [P, KB * BT, RW])
        oht = sb("oht", [P, 2, BE])
        win = sb("win", [P, KB, C])
        ohb = sb("ohb", [P, KB, BT * NT], BF16)
        posf = sb("posf", [P, KB * BT])
        posu = sb("posu", [P, KB * BT], U32)
        dsg = sb("dsg", [P, BT], U32)
        scr = sb("scr", [P, BT * NT])
        node = sb("node", [P, 14 * C])
        stats = sb("stats", [P, G, 6])
        mvs = sb("mvs", [P, G, 2])
        newt = sb("newt", [P, 3, NT])
        rs = sb("rs", [P, G])
        rz = sb("rz", [P, 2 * HEADS])
        wts = sb("wts", [P, NT])
        wcol = sb("wcol", [P, G])
        mv = sb("mv", [P, NT, 2])
        rstd = sb("rstd", [P, NT])
        tk = sb("tk", [P, 8])
        tki = tk[:, :].bitcast(I32)
        bits = sb("bits", [P, 32], I32)
        cntb = sb("cntb", [P, 1], BF16)

        def part(at, *shape, of=acc):
            n = int(np.prod(shape))
            ap = of[:, at:at + n]
            if len(shape) == 1:
                return ap
            if len(shape) == 2:
                return ap.rearrange("p (a b) -> p a b", a=shape[0])
            return ap.rearrange("p (a b c) -> p a b c", a=shape[0], b=shape[1])

        GC = G * C
        x_g = [part(s * GC, G, C) for s in range(2)]
        xnT_g = [part((2 + s) * GC, G, C) for s in range(2)]
        sup_g = [part((4 + s) * GC, G, C) for s in range(2)]
        raw0 = 6 * GC
        rsrc, rdst, rew, fbkt, floc, fdst = (part(raw0 + k * ET, ET) for k in range(6))
        rrel = part(raw0 + 6 * ET, KB * BE)
        wraw = part(0, 10, C)
        offs = part(raw0, 16, BT * NT)
        bcmp = part(raw0 + 7000, GJ, NT)
        beforef = part(raw0 + 8000, P)
        xnT_b = [part(k * C, C) for k in range(2)]
        eq, rq, qTb, ek, rk, kk = (part((2 + 2 * k) * C, 2, C) for k in range(6))
        vext = part(14 * C, 2, CC, P + 1)
        qTm, xnb, xb, tmp, x1, x1T, hT = (part(2 * C * k, 2, C, of=node) for k in range(7))
        x3, x3T, fo = (part(4 * C * k, 2, 2 * C, of=node) for k in range(3))
        fhT = rowbuf[:, :, :].rearrange("p a b -> p (a b)")[:, 0:2 * 8 * 2 * P].rearrange(
            "p (s m r) -> p s m r", s=2, m=HID // P)
        zrow = node[:, 0:2 * RW]
        padi = node[0:1, 600:600 + EPAD - E].bitcast(I32)
        pf_row = node[0:1, 1200:1200 + NT + RG - 1].bitcast(I32)
        last_dst = node[0:1, 1420:1421].bitcast(I32)
        padj = node[0:1, 1500:1500 + EPAD - E].bitcast(I32)
        gb_pj = node[:, 1400:1400 + GJ].bitcast(I32)

        ps = ctx.enter_context(nc.psum_tensor("ps", [P, 8, 512], F32))
        RANK, RELB, MSG, KVA, QPS, KVPS = 0, 1, 2, 4, 5, 6
        TPS, XTPS, HPS, YPS = 4, 6, 7, 4
        GRP = 4

        (padsrc, padded, w_in, raw_in, wraw_in, d0_in, iotas, consts, dstep, pstep) = (sem(n) for n in (
            "padsrc", "padded", "w_in", "raw_in", "wraw_in", "d0_in", "iotas", "consts", "dstep", "pstep"))
        (raw_ready, tab_mm, tab_read, viol_ready, viol_mm, flag_ready) = (sem(n) for n in (
            "raw_ready", "tab_mm", "tab_read", "viol_ready", "viol_mm", "flag_ready"))
        (hist_oh, hist_mm, base_ready, base_mm, meta_ready, gb_ready, gb_out, gb_in, cleared) = (sem(n) for n in (
            "hist_oh", "hist_mm", "base_ready", "base_mm", "meta_ready", "gb_ready", "gb_out", "gb_in", "cleared"))
        xg_in = [sem(f"xg_in{s}") for s in range(2)]
        xg_out = [sem(f"xg_out{s}") for s in range(2)]
        (xn_ready, tr_mm, xnT_ready, sup_mm, sup_ready) = (sem(n) for n in (
            "xn_ready", "tr_mm", "xnT_ready", "sup_mm", "sup_ready"))
        (oh_ready, rank_mm, rank_read, relb_mm, oht_ready, main_mm, row_ready, pos_ready, ws_ready) = (
            sem(n) for n in ("oh_ready", "rank_mm", "rank_read", "relb_mm", "oht_ready", "main_mm",
                             "row_ready", "pos_ready", "ws_ready"))
        win_in = [sem(f"win_in{k}") for k in range(KB)]
        scat = [sem(f"scattered{k}") for k in range(KB)]
        dsg_ready, gath = sem("dsg_ready"), sem("gathered")
        xnTb_in = [sem(f"xnTb_in{u}") for u in range(2)]
        (q_mm, kv_mm, elu_a, elu_v, kv_acc, q_out, kvb_ready) = (sem(n) for n in (
            "q_mm", "kv_mm", "elu_parts", "elu_done", "kv_acc", "q_out", "kvb_ready"))
        (qxn_in, x_in, t_mm, x1_ready, x1T_mm, x1T_ready, h_mm, h_ready, y_mm, mix_done) = (sem(n) for n in (
            "qxn_in", "x_in", "t_mm", "x1_ready", "x1T_mm", "x1T_ready", "h_mm", "h_ready", "y_mm", "mix_done"))
        fw_in, last_in = sem("fw_in"), sem("last_in")
        passed = sem("passed")
        r_in = [sem(f"rows_in{k}") for k in range(KB)]
        (ohw_ready, grp_mm, acc_done, cnt_ready, cnt_mm, final_cnt, final_mm) = (sem(n) for n in (
            "ohw_ready", "grp_mm", "acc_done", "cnt_ready", "cnt_mm", "final_cnt", "final_mm"))
        (x3_ready, x3T_mm, x3T_ready, fh_mm, fh_ready, fy_mm, o_ready) = (sem(n) for n in (
            "x3_ready", "x3T_mm", "x3T_ready", "fh_mm", "fh_ready", "fy_mm", "o_ready"))
        o_out, q_free, fo_free, rows_left = (sem(n) for n in ("o_out", "q_free", "fo_free", "rows_left"))

        MAIN0, ROW0, OHT0, RANK0, RREAD0, MIX0 = 2 * KB, 2, 1, 1, 1, 1
        ELUA0, ELUV0, KVACC0 = 10, 6, 2
        XNT0, SUP0 = 2, 2
        GRP0, ACC0 = 2 * KB, 4
        XT0, FH0 = 1, 2
        QFREE0, FO0, LEFT0 = 1, 2, KB
        TAB = 16 + 6

        block = ctx.enter_context(nc.Block())
        tiles_of = lambda d: d.rearrange("(t p) c -> t p c", p=P)
        lanes = lambda d: d.rearrange("t p c -> p t c")
        xr = tiles_of(x[0:(NT - 1) * P, :])

        @block.sync
        def _(sp):
            sp.sem_inc(q_free, QFREE0)
            sp.sem_inc(fo_free, FO0)
            row = lambda d: d.rearrange("(a b) -> a b", a=1)
            sp.dma_start(last_dst, row(dst[E - 1:E])).then_inc(last_in, 16)
            for k, (a, n) in enumerate(((wqkv, 6), (w1, 2), (w2, 2))):
                at = (0, 6, 8)[k]
                sp.dma_start(wraw[:, at:at + n, :], a.rearrange("(k p) c -> p k c", p=P)).then_inc(wraw_in, 16)
            sp.dma_start(src_d[0:E], src).then_inc(padded, 16)
            sp.dma_start(dst_d[0:E], dst).then_inc(padded, 16)
            sp.dma_start(ew_d[0:E], edge_weight).then_inc(padded, 16)
            sp.wait_ge(padsrc, 2)
            sp.dma_start(row(src_d[E:EPAD]), padi).then_inc(padded, 16)
            sp.dma_start(row(ew_d[E:EPAD]), zrow[0:1, 0:EPAD - E]).then_inc(padded, 16)
            sp.wait_ge(padsrc, 3)
            sp.dma_start(row(dst_d[E:EPAD]), padj).then_inc(padded, 16)
            sp.dma_start(sup_d[NT * P:, :], zrow[:, 0:C]).then_inc(w_in, 16)
            sp.dma_start(gw_s[:, :, :], gnn_w.rearrange("(k p) c -> p k c", p=P)).then_inc(w_in, 16)
            sp.wait_ge(padded, 96)
            for a, d in ((rsrc, src_d), (rdst, dst_d)):
                sp.dma_start(a.bitcast(I32).rearrange("r (j e) -> r j e", e=P),
                             d.rearrange("(j r e) -> r j e", r=P, e=P)).then_inc(raw_in, 16)
            sp.dma_start(rew.rearrange("r (j e) -> r j e", e=P),
                         ew_d.rearrange("(j r e) -> r j e", r=P, e=P)).then_inc(raw_in, 16)
            sp.dma_start(rrel[0:EQ, :].bitcast(I32), dst_d.rearrange("(q f) -> q f", q=EQ)).then_inc(raw_in, 16)
            sp.dma_start(d0_row[0:1, :], dst_d.rearrange("(a b e) -> a b e", a=1, e=BE)[:, :, 0],
                         allow_slow_non_contiguous=True).then_inc(d0_in, 16)
            for k, v in enumerate((ln1_g, ln1_b, ln2_g, ln2_b, b2, fb2, wr.rearrange("a b -> (a b)"))):
                sp.dma_start(vec[:, k, :], v.partition_broadcast(P)).then_inc(w_in, 16)
            sp.dma_start(b1_c[:, :], b1.rearrange("(k p) -> p k", p=P),
                         allow_slow_non_contiguous=True).then_inc(w_in, 16)
            sp.dma_start(fb1_c[:, :], fb1.rearrange("(k p) -> p k", p=P),
                         allow_slow_non_contiguous=True).then_inc(w_in, 16)
            sp.dma_start(br_c[:, :], br.partition_broadcast(P)).then_inc(w_in, 16)

            sp.wait_ge(tab_read, 6)

            def x_load(s, g):
                sp.dma_start(x_g[s][:, 0:G - 1, :], lanes(xr[ds(g * G, G - 1)])).then_inc(xg_in[s], 16)
                sp.dma_start(x_g[s][:, G - 1, :], x[ds((g * G + G - 1) * P, P), :]).then_inc(xg_in[s], 16)

            def x_load_last(s):
                sp.dma_start(x_g[s][:, 0:G - 1, :], lanes(xr[(NG - 1) * G:NT - 1])).then_inc(xg_in[s], 16)
                sp.dma_start(x_g[s][0:LASTROWS, G - 1, :], x[(NT - 1) * P:N, :]).then_inc(xg_in[s], 16)

            def stage_out(s, g):
                sp.wait_ge(xn_ready, G * (g + 1))
                sp.dma_start(lanes(tiles_of(xn_d)[ds(g * G, G)]), x_g[s]).then_inc(xg_out[s], 16)
                sp.wait_ge(xnT_ready, XNT0 + G * (g + 1))
                sp.dma_start(lanes(xnT_d[ds(g * G, G)]), xnT_g[s]).then_inc(xg_out[s], 16)
                sp.wait_ge(sup_ready, SUP0 + G * (g + 1))
                sp.dma_start(lanes(tiles_of(sup_d[0:NT * P])[ds(g * G, G)]), sup_g[s]).then_inc(xg_out[s], 16)

            x_load(0, 0)
            x_load(1, 1)
            with sp.Fori(0, NG // 2 - 2) as i:
                for s in range(2):
                    stage_out(s, 2 * i + s)
                    sp.wait_ge(xg_out[s], 48 * (i + 1))
                    x_load(s, 2 * i + 2 + s)
            for s in range(2):
                stage_out(s, NG - 4 + s)
                sp.wait_ge(xg_out[s], 48 * (NG // 2 - 1))
                if s == 0:
                    x_load(0, NG - 2)
                else:
                    x_load_last(1)
            for s in range(2):
                stage_out(s, NG - 2 + s)

            sp.wait_ge(meta_ready, 1)
            with sp.Fori(0, NT + RG - 1) as i:
                at = sp.value_load(pf_row[0:1, ds(i, 1)], min_val=0, max_val=(NGROUPS - 1) * GS)
                sp.dma_start(rows_d[ds(at, GS), :].rearrange("(p k) f -> p (k f)", p=P),
                             zrow[:, :]).then_inc(cleared, 16)
            sp.wait_ge(gb_ready, 1)
            sp.dma_start(gb_d.rearrange("(j p) -> p j", p=P), gb_pj,
                         allow_slow_non_contiguous=True).then_inc(gb_out, 16)
            sp.wait_ge(gb_out, 16)
            sp.dma_start(gb_row[0:1, :], row(gb_d)).then_inc(gb_in, 16)
            for s in range(2):
                sp.wait_ge(xg_out[s], 48 * (NG // 2))
            sp.wait_ge(d0_in, 16)

            def window(i, k):
                b = KB * i + k
                sp.wait_ge(main_mm, 2 * b + 2)
                first = sp.value_load(d0_row[0:1, ds(b, 1)], min_val=0, max_val=N - 1)
                sp.dma_start(win[:, k, :], sup_d[ds(first, P), :]).then_inc(win_in[k], 16)

            def att_load(u, n):
                sp.dma_start(xnT_b[u], xnT_d[ds(n, 1)].rearrange("a p c -> (a p) c")).then_inc(xnTb_in[u], 16)

            def att_step(i, more):
                for k in range(KB):
                    window(i, k)
                if more:
                    sp.wait_ge(kv_mm, 2 * (i + 1))
                    for u in range(2):
                        att_load(u, 2 * i + 2 + u)
                sp.wait_ge(elu_v, ELUV0 + 6 * i + 5)
                sp.dma_start(lanes(qT_d[ds(2 * i, 2)]), qTb).then_inc(q_out, 16)
                sp.wait_ge(q_out, 16 * (i + 1))
                sp.sem_inc(q_free, 1)

            for u in range(2):
                att_load(u, u)
            with sp.Fori(0, NT // 2 - 1) as i:
                att_step(i, True)
            att_step(NT // 2 - 1, False)
            sp.wait_ge(q_out, 16 * (NT // 2))
            sp.wait_ge(cleared, 16 * (NT + RG - 1))

            def mix_load(i, last=False):
                sp.dma_start(qTm, lanes(qT_d[ds(2 * i, 2)])).then_inc(qxn_in, 16)
                sp.dma_start(xnb, lanes(tiles_of(xn_d)[ds(2 * i, 2)])).then_inc(qxn_in, 16)
                sp.dma_start(xb[:, 0, :], x[ds(2 * P * i, P), :]).then_inc(x_in, 16)
                if last:
                    sp.dma_start(xb[0:LASTROWS, 1, :], x[(NT - 1) * P:N, :]).then_inc(x_in, 16)
                else:
                    sp.dma_start(xb[:, 1, :], x[ds(2 * P * i + P, P), :]).then_inc(x_in, 16)

            def mix_step(i, then):
                for k in range(KB):
                    window(NT // 2 + i, k)
                if then:
                    sp.wait_ge(mix_done, MIX0 + i + 1)
                    mix_load(i + 1, last=then == "last")

            mix_load(0)
            with sp.Fori(0, NT // 2 - 2) as i:
                mix_step(i, "next")
            mix_step(NT // 2 - 2, "last")
            mix_step(NT // 2 - 1, None)
            with sp.Fori(2 * (NT // 2), EQ) as i:
                for k in range(KB):
                    window(i, k)

            for k in range(KB):
                sp.wait_ge(scat[k], 16 * BT * EQ)
            sp.wait_ge(rank_mm, RANK0 + NB)
            sp.dma_start(fw1_s, fw1.rearrange("(k p) c -> p k c", p=P)).then_inc(fw_in, 16)
            sp.dma_start(fw2_s, fw2.rearrange("(k p) c -> p k c", p=P)).then_inc(fw_in, 16)
            steps = sp.value_load(meta[0:1, 1:2], min_val=1, max_val=NGMAX // RG + 1)
            with sp.Fori(0, steps) as i:
                for k in range(KB):
                    sp.wait_ge(grp_mm, RG * i + 2 * k + 2)
                    sp.dma_start(rowbuf[:, k * BT:(k + 1) * BT, :].rearrange("p (g k) f -> p g (k f)", g=2),
                                 rows_d[ds((RG * i + 2 * k + 1) * GS, 2 * GS), :].rearrange(
                                     "(g p k) f -> p g (k f)", g=2, p=P)).then_inc(r_in[k], 16)

            def out_store(i, s):
                sp.wait_ge(o_ready, i + 1)
                sp.dma_start(lanes(tiles_of(out[0:(NT - 1) * P, :])[ds(2 * i, 2)]),
                             fo[:, s, :].rearrange("p (u c) -> p u c", u=2)).then_inc(o_out, 16)
                sp.wait_ge(o_out, 16 * (i + 1))
                sp.sem_inc(fo_free, 1)

            with sp.Fori(0, NT // 4) as i:
                out_store(2 * i, 0)
                out_store(2 * i + 1, 1)
            sp.wait_ge(o_ready, NT // 2)
            sp.dma_start(out[(NT - 2) * P:(NT - 1) * P, :], fo[:, 0, 0:C]).then_inc(o_out, 16)
            sp.dma_start(out[(NT - 1) * P:N, :], fo[0:LASTROWS, 0, C:2 * C]).then_inc(o_out, 16)
            sp.wait_ge(o_out, 16 * 2 * (NT // 4) + 32)

        @block.gpsimd
        def _(pool):
            g = nc.gpsimd
            g.memset(zrow, 0.0).then_inc(padsrc, 1)
            g.memset(padi, NT * P - 1).then_inc(padsrc, 1)
            pool.wait_ge(last_in, 16)
            g.tensor_copy(padj, last_dst.to_broadcast([1, EPAD - E])).then_inc(padsrc, 1)
            g.iota(lane[:, :], [[0, 1]], base=0, channel_multiplier=1,
                   allow_small_or_imprecise_dtypes=True).then_inc(iotas, 1)
            g.iota(cols[:, :], [[1, P]], base=0, channel_multiplier=0,
                   allow_small_or_imprecise_dtypes=True).then_inc(iotas, 1)
            g.memset(zeros_b[:, :], 0.0).then_inc(iotas, 1)
            g.memset(ones_b[:, :], 1.0).then_inc(iotas, 1)
            g.memset(onesf[:, :], 1.0).then_inc(iotas, 1)
            g.memset(maskc[:, :], 1.0).then_inc(iotas, 1)
            g.memset(kvb[:, :, :], 0.0).then_inc(iotas, 1)
            g.iota(bits[:, :], [[1, 32]], base=0, channel_multiplier=0).then_inc(iotas, 1)

            pool.wait_ge(cleared, 16 * (NT + RG - 1))
            pool.wait_ge(flag_ready, 1)
            wide = pool.value_load(meta[0:1, 2:3], min_val=0, max_val=EQ)

            def scatter(i, k, first=False):
                b = KB * i + k
                pool.wait_ge(pos_ready, b + 1)
                pool.wait_ge(ws_ready, b + 1)
                pool.wait_ge(row_ready, ROW0 + 2 * b + 2)
                pool.sem_inc(passed, 1)
                with pool.If(wide > 0):
                    g.tensor_copy(dsg[:, :], dst_t[:, ds(BT * b, BT)]).then_inc(dsg_ready, 1)
                    pool.wait_ge(dsg_ready, b + 1)
                    pool.sem_inc(passed, 1)
                    for t in range(BT):
                        g.indirect_dma_start(rowbuf[:, BT * k + t, 0:C], None, sup_d,
                                             bass.IndirectOffsetOnAxis(dsg[:, t:t + 1], 0)).then_inc(gath, 16)
                    pool.wait_ge(gath, 16 * BT * (b + 1))
                    pool.sem_inc(passed, 1)
                for t in range(BT):
                    s = BT * k + t
                    g.indirect_dma_start(rows_d, bass.IndirectOffsetOnAxis(posu[:, s:s + 1], 0),
                                         rowbuf[:, s, :], None).then_inc(scat[k], 16)
                if not first:
                    pool.wait_ge(scat[(k - 1) % KB], 16 * BT * (i + (k > 0)))
                    pool.sem_inc(rows_left, 1)

            pool.sem_inc(rows_left, LEFT0)
            for k in range(KB):
                scatter(0, k, first=k == 0)
            with pool.Fori(1, EQ) as i:
                for k in range(KB):
                    scatter(i, k)

        @block.tensor
        def _(pe):
            mm, tp = nc.tensor.matmul, nc.tensor.transpose
            pe.sem_inc(main_mm, MAIN0)
            pe.sem_inc(rank_mm, RANK0)
            pe.sem_inc(kv_acc, KVACC0)
            pe.sem_inc(grp_mm, GRP0)
            pe.wait_ge(consts, 5)
            pe.wait_ge(iotas, 8)

            def blocks(job, items):
                if job >= 8:
                    pe.wait_ge(tab_read, job - 7)
                for k, a in enumerate(items):
                    last = tp(ps[:, job % 8, k * P:(k + 1) * P], a, ident[:, :])
                last.then_inc(tab_mm, 1)

            pe.wait_ge(wraw_in, 48)
            for job, (rows, c) in enumerate((([0, 1, 2, 3], 0), ([4, 5], 0), ([0, 1, 2, 3], 1), ([4, 5], 1))):
                blocks(job, [wraw[:, r, c * P:(c + 1) * P] for r in rows])
            for job, at in ((4, 6), (5, 8)):
                blocks(job, [wraw[:, at + r, c * P:(c + 1) * P] for c in range(CC) for r in range(2)])
            pe.wait_ge(raw_in, 64)
            for k, tab in enumerate((fbkt, floc, rew, fdst)):
                pe.wait_ge(raw_ready, (2, 4, 4, 5)[k])
                for q in range(4):
                    n = min(4, EJ - 4 * q)
                    blocks(6 + 4 * k + q, [tab[:, (4 * q + r) * P:(4 * q + r + 1) * P] for r in range(n)])
            pe.wait_ge(tab_read, TAB)
            pe.wait_ge(viol_ready, 1)
            mm(ps[0:1, 3, 0:1], tk[0:EQ, 0:1], onesf[0:EQ, 0:1], start=True, stop=True).then_inc(viol_mm, 1)

            hist = ps[0:EQ, RANK, 0:BT * NT]
            mm(hist, zeros_b[:, 0:EQ], zeros_b[:, 0:BT * NT], start=True, stop=False)
            with pe.Fori(0, EQ) as i:
                for k in range(KB):
                    pe.wait_ge(hist_oh, KB * i + k + 1)
                    pe.sem_inc(passed, 1)
                    mm(hist, onecol[:, ds(EQ - 1 - i, EQ)], ohb[:, k, :], start=False, stop=False).then_inc(hist_mm, 1)
            mm(hist, zeros_b[:, 0:EQ], zeros_b[:, 0:BT * NT], start=False, stop=True).then_inc(hist_mm, 1)
            pe.wait_ge(base_ready, 1)
            mm(ps[:, 1, 0:BT * NT], onesf[0:EQ, :], offs[0:EQ, 1, :], start=True, stop=True)
            mm(ps[0:EQ, 2, 0:BT * NT], beforef[0:EQ, 0:EQ], offs[0:EQ, 1, :], start=True, stop=True).then_inc(base_mm, 1)

            pe.wait_ge(w_in, 16 * 12)
            pe.wait_ge(flag_ready, 1)
            pe.wait_ge(meta_ready, 1)
            with pe.Fori(0, NG // 2) as i:
                for n in range(2 * G):
                    s, t = n // G, n % G
                    tile = 2 * G * i + n
                    pe.wait_ge(xn_ready, tile + 1)
                    pe.wait_ge(xnT_ready, tile + 1)
                    for c in range(CC):
                        last = tp(ps[:, 4 + n % 2, c * P:(c + 1) * P], x_g[s][:, t, c * P:(c + 1) * P], ident[:, :])
                    last.then_inc(tr_mm, 1)
                    pe.wait_ge(xnT_ready, XNT0 + tile + 1)
                    pe.wait_ge(sup_ready, tile + 1)
                    for c in range(CC):
                        last = mm(ps[:, 6 + n % 2, 0:C], xnT_g[s][:, t, c * P:(c + 1) * P], gw_s[:, c, :],
                                  start=c == 0, stop=c == CC - 1)
                    last.then_inc(sup_mm, 1)
            pe.wait_ge(sup_ready, SUP0 + NT)
            mm(ps[:, KVA, 0:CC * (P + 1)], zeros_b[:, 0:P], zeros_b[:, 0:CC * (P + 1)], start=True, stop=False)

            def edges(i, k):
                b = KB * i + k
                pe.wait_ge(oht_ready, b + 1)
                mm(ps[:, RELB, :], ident_h[0:EQ, ds(i, 1)].to_broadcast([EQ, P]), rel[:, k * BE:(k + 1) * BE],
                   start=True, stop=True).then_inc(relb_mm, 1)
                pe.wait_ge(rank_read, RREAD0 + BT * b)
                rank = ps[:, RANK, 0:BT * NT]
                mm(rank, ident_h[0:EQ, ds(i, 1)].to_broadcast([EQ, P]), first_lo[:, :], start=True, stop=False)
                mm(rank, ident_hi[0:EQ, ds(i, 1)].to_broadcast([EQ, P]), first_hi[:, :], start=False, stop=False)
                for j in range(k):
                    mm(rank, ones_b[:, :], ohb[:, j, :], start=False, stop=False)
                pe.wait_ge(oh_ready, b + 1)
                mm(rank, before[:, :], ohb[:, k, :], start=False, stop=True).then_inc(rank_mm, 1)
                pe.wait_ge(oht_ready, OHT0 + b + 1)
                pe.wait_ge(win_in[k], 16 * (i + 1))
                for h in range(2):
                    pe.wait_ge(row_ready, 2 * b + h + 1)
                    for t in range(2):
                        last = mm(ps[:, MSG + h, t * C:(t + 1) * C], oht[:, k % 2, (2 * h + t) * P:(2 * h + t + 1) * P],
                                  win[:, k, :], start=True, stop=True)
                    last.then_inc(main_mm, 1)

            def qkv(i, u):
                n = 2 * i + u
                pe.wait_ge(xnTb_in[u], 16 * (i + 1))
                pe.wait_ge(elu_a, 5 * n + 7)
                for m in range(CC):
                    for c in range(CC):
                        last = mm(ps[:, QPS, u * C + m * P:u * C + (m + 1) * P], wqkvT[:, c, m * P:(m + 1) * P],
                                  xnT_b[u][:, c * P:(c + 1) * P], start=c == 0, stop=c == CC - 1)
                last.then_inc(q_mm, 1)
                for c in range(CC):
                    last = mm(ps[:, KVPS + u, :], xnT_b[u][:, c * P:(c + 1) * P], wqkvT[:, c, C:3 * C],
                              start=c == 0, stop=c == CC - 1)
                last.then_inc(kv_mm, 1)

            def kv_sum(i, u):
                n = 2 * i + u
                pe.wait_ge(elu_v, ELUV0 + 3 * n + 3)
                pe.wait_ge(elu_a, ELUA0 + 5 * n + 5)
                for c in range(CC):
                    last = mm(ps[:, KVA, c * (P + 1):(c + 1) * (P + 1)], kk[:, u, c * P:(c + 1) * P],
                              vext[:, u, c, :], start=False, stop=False)
                last.then_inc(kv_acc, 1)

            with pe.Fori(0, NT // 2) as i:
                edges(i, 0)
                qkv(i, 0)
                edges(i, 1)
                qkv(i, 1)
                edges(i, 2)
                kv_sum(i, 0)
                edges(i, 3)
                kv_sum(i, 1)
            mm(ps[:, KVA, 0:CC * (P + 1)], zeros_b[:, 0:P], zeros_b[:, 0:CC * (P + 1)], start=False,
               stop=True).then_inc(kv_acc, 1)
            pe.wait_ge(kvb_ready, 1)
            pe.wait_ge(elu_a, ELUA0 + 5 * NT)
            pe.wait_ge(w_in, 16 * 12)

            def attend(i):
                pe.wait_ge(qxn_in, 32 * (i + 1))
                pe.wait_ge(mix_done, MIX0 + i)
                for u in range(2):
                    for c in range(CC):
                        last = mm(ps[:, TPS + u, c * (P + 4):(c + 1) * (P + 4)], qTm[:, u, c * P:(c + 1) * P],
                                  kvb[:, c, :], start=True, stop=True)
                last.then_inc(t_mm, 1)

            def mlp_up(i):
                pe.wait_ge(x1_ready, 2 * (i + 1))
                for c in range(CC):
                    for u in range(2):
                        last = tp(ps[:, XTPS, (2 * c + u) * P:(2 * c + u + 1) * P], x1[:, u, c * P:(c + 1) * P],
                                  ident[:, :])
                last.then_inc(x1T_mm, 1)
                pe.wait_ge(x1T_ready, i + 1)
                for m in range(CC):
                    for c in range(CC):
                        last = mm(ps[:, HPS, m * C:(m + 1) * C], w1T[:, c, m * P:(m + 1) * P], x1T[:, c, :],
                                  start=c == 0, stop=c == CC - 1)
                last.then_inc(h_mm, 1)

            def mlp_down(i):
                pe.wait_ge(h_ready, 2 * (i + 1))
                for u in range(2):
                    for m in range(CC):
                        mm(ps[:, YPS, u * C:(u + 1) * C], hT[:, m, u * P:(u + 1) * P], w2T[:, m, :],
                           start=m == 0, stop=False)
                    last = mm(ps[:, YPS, u * C:(u + 1) * C], onesf[0:1, :], vec[0:1, B2, :], start=False, stop=True)
                last.then_inc(y_mm, 1)

            with pe.Fori(0, NT // 2) as i:
                attend(i)
                edges(NT // 2 + i, 0)
                edges(NT // 2 + i, 1)
                mlp_up(i)
                edges(NT // 2 + i, 2)
                mlp_down(i)
                edges(NT // 2 + i, 3)
            with pe.Fori(2 * (NT // 2), EQ) as i:
                for k in range(KB):
                    edges(i, k)

            pe.wait_ge(mix_done, MIX0 + NT // 2)
            pe.wait_ge(row_ready, ROW0 + 2 * NB)
            steps = pe.value_load(meta[0:1, 1:2], min_val=1, max_val=NGMAX // RG + 1)
            with pe.Fori(0, steps) as i:
                for k in range(KB):
                    pe.wait_ge(r_in[k], 16 * (i + 1))
                    for h in range(2):
                        grp = RG * i + 2 * k + h
                        pe.wait_ge(acc_done, grp + 1)
                        for t in range(2):
                            pe.wait_ge(ohw_ready, 2 * grp + t + 1)
                            s = 2 * h + t
                            last = mm(ps[:, GRP + (2 * k + h) % 4, 0:C], oht[:, k % 2, s * P:(s + 1) * P],
                                      rowbuf[:, BT * k + s, 0:C], start=t == 0, stop=t == 1)
                        last.then_inc(grp_mm, 1)

            with pe.Fori(0, 32) as i:
                pe.wait_ge(cnt_ready, i + 1)
                mm(ps[:, 0, 0:1], ones_b[:, :], cntb[:, :], start=True, stop=True).then_inc(cnt_mm, 1)
            pe.wait_ge(final_cnt, 1)
            mm(ps[:, 0, 0:NT], ones_b[:, :], ohb[:, 0, 0:NT], start=True, stop=True)
            mm(ps[:, 1, 0:NT], ones_b[:, :], ohb[:, 1, 0:NT], start=True, stop=True)
            mm(ps[:, 2, 0:NT], before[:, :], ohb[:, 1, 0:NT], start=True, stop=True).then_inc(final_mm, 1)

            pe.wait_ge(fw_in, 32)
            pe.wait_ge(x3_ready, 1)

            def ffn(i, s, first=False):
                pe.wait_ge(x3_ready, 2 * (i + 1))
                pe.wait_ge(x3T_ready, i + 1)
                for c in range(CC):
                    for u in range(2):
                        last = tp(ps[:, 0, (2 * c + u) * P:(2 * c + u + 1) * P],
                                  x3[:, s, u * C + c * P:u * C + (c + 1) * P], ident[:, :])
                last.then_inc(x3T_mm, 1)
                pe.wait_ge(x3T_ready, XT0 + i + 1)
                for m in range(HID // P):
                    pe.wait_ge(fh_ready, 8 * i + m + 1)
                    for c in range(CC):
                        last = mm(ps[:, 2 + m % 2, 0:C], fw1_s[:, c, m * P:(m + 1) * P],
                                  x3T[:, s, c * 2 * P:(c + 1) * 2 * P], start=c == 0, stop=c == CC - 1)
                    last.then_inc(fh_mm, 1)
                pe.wait_ge(fh_ready, FH0 + 8 * (i + 1))
                if not first:
                    pe.wait_ge(o_ready, i - 1)
                for u in range(2):
                    for m in range(HID // P):
                        mm(ps[:, 4 + s, u * C:(u + 1) * C], fhT[:, s, m, u * P:(u + 1) * P], fw2_s[:, m, :],
                           start=m == 0, stop=False)
                    last = mm(ps[:, 4 + s, u * C:(u + 1) * C], onesf[0:1, :], vec[0:1, FB2, :], start=False,
                              stop=True)
                last.then_inc(fy_mm, 1)

            ffn(0, 0, first=True)
            ffn(1, 1, first=True)
            with pe.Fori(1, NT // 4) as i:
                ffn(2 * i, 0)
                ffn(2 * i + 1, 1)
            ffn(NT // 2 - 1, 0)

        @block.scalar
        def _(act):
            A = nc.scalar.activation
            act.sem_inc(xnT_ready, XNT0)
            act.sem_inc(sup_ready, SUP0)
            act.sem_inc(row_ready, ROW0)
            act.sem_inc(elu_a, ELUA0)
            act.sem_inc(x3T_ready, XT0)
            act.sem_inc(fh_ready, FH0)
            outs = [wqkvT[:, 0, 0:512], wqkvT[:, 0, 512:768], wqkvT[:, 1, 0:512], wqkvT[:, 1, 512:768],
                    w1T[:, :, :].rearrange("p c o -> p (c o)"), w2T[:, :, :].rearrange("p c o -> p (c o)")]
            for tab in (bkt_t, ws_t[:, :, 1], ws_t[:, :, 0], dst_t):
                for q in range(4):
                    outs.append(tab[:, 4 * q * P:min(4 * q + 4, EJ) * P])
            for job, o in enumerate(outs):
                act.wait_ge(tab_mm, job + 1)
                A(o, ps[:, job % 8, 0:o.shape[1]], ACT.Copy).then_inc(tab_read, 1)
            with act.Fori(0, NG // 2) as i:
                for n in range(2 * G):
                    s, t = n // G, n % G
                    tile = 2 * G * i + n
                    act.wait_ge(tr_mm, tile + 1)
                    A(xnT_g[s][:, t, :], ps[:, 4 + n % 2, 0:C], ACT.Copy).then_inc(xnT_ready, 1)
                    act.wait_ge(sup_mm, tile + 1)
                    A(sup_g[s][:, t, :], ps[:, 6 + n % 2, 0:C], ACT.Copy).then_inc(sup_ready, 1)

            def rows(i, k):
                b = KB * i + k
                act.wait_ge(rows_left, b + 1)
                for h in range(2):
                    act.wait_ge(main_mm, MAIN0 + 2 * b + h + 1)
                    s = BT * k + 2 * h
                    A(rowbuf[:, s:s + 2, 0:C], ps[:, MSG + h, :].rearrange("p (t c) -> p t c", t=2),
                      ACT.Copy).then_inc(row_ready, 1)

            def elu_parts(i, u):
                n = 2 * i + u
                act.wait_ge(elu_v, 3 * n + 3)
                act.wait_ge(q_mm, n + 1)
                A(eq[:, u, :], ps[:, QPS, u * C:(u + 1) * C], ACT.Exp).then_inc(elu_a, 1)
                A(rq[:, u, :], ps[:, QPS, u * C:(u + 1) * C], ACT.Relu).then_inc(elu_a, 1)
                act.wait_ge(kv_mm, n + 1)
                A(ek[:, u, :], ps[:, KVPS + u, 0:C], ACT.Exp).then_inc(elu_a, 1)
                A(rk[:, u, :], ps[:, KVPS + u, 0:C], ACT.Relu).then_inc(elu_a, 1)
                act.wait_ge(kv_acc, n + 1)
                A(vext[:, u, :, 0:P], ps[:, KVPS + u, C:2 * C].rearrange("p (c f) -> p c f", c=CC), ACT.Copy,
                  scale=maskc[:, ds(n, 1)]).then_inc(elu_a, 1)

            act.wait_ge(consts, 5)
            for s in range(2):
                act.wait_ge(xg_out[s], 48 * (NG // 2))
            with act.Fori(0, NT // 2) as i:
                rows(i, 0)
                elu_parts(i, 0)
                rows(i, 1)
                elu_parts(i, 1)
                rows(i, 2)
                rows(i, 3)
            act.wait_ge(w_in, 16 * 12)
            with act.Fori(0, NT // 2) as i:
                rows(NT // 2 + i, 0)
                rows(NT // 2 + i, 1)
                act.wait_ge(x1T_mm, i + 1)
                A(x1T.rearrange("p c r -> p (c r)"), ps[:, XTPS, :], ACT.Copy).then_inc(x1T_ready, 1)
                act.wait_ge(h_mm, i + 1)
                for m in range(CC):
                    A(hT[:, m, :], ps[:, HPS, m * C:(m + 1) * C], ACT.Gelu, bias=b1_c[:, m:m + 1]).then_inc(h_ready, 1)
                rows(NT // 2 + i, 2)
                rows(NT // 2 + i, 3)
            with act.Fori(2 * (NT // 2), EQ) as i:
                for k in range(KB):
                    rows(i, k)

            def ffn(i, s):
                act.wait_ge(x3T_mm, i + 1)
                A(x3T[:, s, :], ps[:, 0, :], ACT.Copy).then_inc(x3T_ready, 1)
                for m in range(HID // P):
                    act.wait_ge(fh_mm, 8 * i + m + 1)
                    A(fhT[:, s, m, :], ps[:, 2 + m % 2, 0:C], ACT.Gelu_apprx_tanh,
                      bias=fb1_c[:, m:m + 1]).then_inc(fh_ready, 1)

            steps = act.value_load(meta[0:1, 1:2], min_val=1, max_val=NGMAX // RG + 1)
            act.wait_ge(grp_mm, GRP0 + RG * steps)
            ffn(0, 0)
            ffn(1, 1)
            with act.Fori(1, NT // 4) as i:
                for s in range(2):
                    act.wait_ge(fy_mm, 2 * i + s - 1)
                    ffn(2 * i + s, s)
            act.wait_ge(fy_mm, NT // 2 - 2)
            ffn(NT // 2 - 1, 0)

        @block.vector
        def _(dve):
            v = nc.vector
            chain = Chain(dve, dstep)
            v_link = chain.link

            def newton(var, y, t):
                v_link(v.tensor_scalar(t.bitcast(I32), var.bitcast(I32), 1, None, ALU.logical_shift_right))
                v_link(v.tensor_scalar(y.bitcast(I32), t.bitcast(I32), -1.0, 1597463007.0, ALU.mult, ALU.add))
                for _ in range(4):
                    v_link(v.scalar_tensor_tensor(t, y, -0.5, y, ALU.mult, ALU.mult))
                    v_link(v.tensor_tensor(t, t, var, ALU.mult))
                    v_link(v.scalar_tensor_tensor(y, t, 1.5, y, ALU.add, ALU.mult))

            dve.wait_ge(iotas, 8)
            v.tensor_scalar(ident[:, :], cols[:, :], lane[:, 0:1], None, ALU.is_equal).then_inc(consts, 1)
            v.tensor_scalar(ident_h[:, :], cols[:, :], lane[:, 0:1], None, ALU.is_equal).then_inc(consts, 1)
            v.tensor_scalar(ident_hi[:, :], cols[:, :], lane[:, 0:1], float(LOW), ALU.is_equal,
                            ALU.mult).then_inc(consts, 1)
            v.tensor_scalar(before[:, :], cols[:, :], lane[:, 0:1], None, ALU.is_gt).then_inc(consts, 1)
            v.tensor_scalar(maskc[:, NT - 1:NT], lane[:, 0:1], float(LASTROWS), None, ALU.is_lt).then_inc(consts, 1)
            v_link(v.memset(newt[:, 2, 0:32].bitcast(I32), 1))
            v_link(v.tensor_tensor(bits[:, :], newt[:, 2, 0:32].bitcast(I32), bits[:, :], ALU.logical_shift_left))
            v_link(v.memset(onecol[:, :], 0.0))
            v_link(v.memset(onecol[:, EQ - 1:EQ], 1.0))
            v.sem_inc(oht_ready, OHT0)
            v.sem_inc(elu_v, ELUV0)
            v.sem_inc(acc_done, ACC0)
            v.sem_inc(rank_read, RREAD0)
            v.sem_inc(mix_done, MIX0)

            dve.wait_ge(raw_in, 64)
            si = rsrc.bitcast(I32)
            v.tensor_scalar(fbkt.bitcast(I32), si, 7, None, ALU.logical_shift_right).then_inc(raw_ready, 1)
            dve.wait_ge(raw_ready, 1)
            v.tensor_copy(fbkt, fbkt.bitcast(I32)).then_inc(raw_ready, 1)
            v.tensor_scalar(floc.bitcast(I32), si, P - 1, None, ALU.bitwise_and).then_inc(raw_ready, 1)
            dve.wait_ge(raw_ready, 3)
            v.tensor_copy(floc, floc.bitcast(I32)).then_inc(raw_ready, 1)
            v.tensor_copy(fdst, rdst.bitcast(I32)).then_inc(raw_ready, 1)
            rr = rrel[0:EQ, :].bitcast(I32).rearrange("p (k e) -> p k e", k=KB)
            v_link(v.tensor_tensor(rel[:, :].rearrange("p (k e) -> p k e", k=KB), rr,
                                   rr[:, :, 0:1].to_broadcast([EQ, KB, BE]), ALU.subtract))
            chain.inc(v.tensor_reduce(tk[0:EQ, 1:2], rel[:, :], AX.X, ALU.max))
            chain.inc(v.tensor_reduce(tk[0:EQ, 2:3], rel[:, :], AX.X, ALU.min))
            chain.wait()
            v_link(v.tensor_scalar(tk[0:EQ, 1:2], tk[0:EQ, 1:2], float(P - 1), None, ALU.is_gt))
            v_link(v.tensor_scalar(tk[0:EQ, 2:3], tk[0:EQ, 2:3], 0.0, None, ALU.is_lt))
            v.tensor_tensor(tk[0:EQ, 0:1], tk[0:EQ, 1:2], tk[0:EQ, 2:3], ALU.max).then_inc(viol_ready, 1)

            bidx = cols[:, 0:NT].unsqueeze(1).to_broadcast([P, BT, NT])

            def one_hot(b, k):
                return v.tensor_tensor(ohb[:, k, :].rearrange("p (t n) -> p t n", t=BT),
                                       bkt_t[:, ds(BT * b, BT)].unsqueeze(2).to_broadcast([P, BT, NT]), bidx,
                                       ALU.is_equal)

            dve.wait_ge(tab_read, TAB)
            for k in range(KB):
                one_hot(k, k).then_inc(hist_oh, 1)
            with dve.Fori(1, EQ) as i:
                for k in range(KB):
                    dve.wait_ge(hist_mm, KB * (i - 1) + k + 1)
                    one_hot(KB * i + k, k).then_inc(hist_oh, 1)

            dve.wait_ge(hist_mm, NB + 1)
            base4 = offs[:, 0, :].rearrange("p (t n) -> p t n", t=BT)
            h4 = offs[:, 8, :].rearrange("p (t n) -> p t n", t=BT)
            tot, grp, cs, cs2 = (offs[:, 2 + k, 0:NT] for k in range(4))
            v_link(v.tensor_scalar(beforef, cols[:, :], lane[:, 0:1], None, ALU.is_gt))
            v_link(v.tensor_copy(offs[0:EQ, 1, :], ps[0:EQ, RANK, 0:BT * NT]))
            v.sem_inc(base_ready, 1)
            dve.wait_ge(base_mm, 1)
            v_link(v.tensor_copy(offs[:, 8, :], ps[:, 1, 0:BT * NT]))
            v_link(v.tensor_tensor(tot, h4[:, 0, :], h4[:, 1, :], ALU.add))
            for t in range(2, BT):
                v_link(v.tensor_tensor(tot, tot, h4[:, t, :], ALU.add))
            v_link(v.tensor_scalar(grp.bitcast(I32), tot, float(GS - 1), None, ALU.add))
            v_link(v.tensor_scalar(grp.bitcast(I32), grp.bitcast(I32), 8, None, ALU.logical_shift_right))
            v_link(v.tensor_copy(grp, grp.bitcast(I32)))
            v_link(v.tensor_copy(cs, grp))
            a, b_, d = cs, cs2, 1
            while d < NT:
                v_link(v.tensor_copy(b_[:, 0:d], a[:, 0:d]))
                v_link(v.tensor_tensor(b_[:, d:NT], a[:, d:NT], a[:, 0:NT - d], ALU.add))
                a, b_, d = b_, a, 2 * d
            cs = a
            v_link(v.tensor_tensor(b_, cs, grp, ALU.subtract))
            v_link(v.tensor_scalar(base4[:, 0, :], b_, float(GS), float(GS), ALU.mult, ALU.add))
            for t in range(1, BT):
                v_link(v.tensor_tensor(base4[:, t, :], base4[:, t - 1, :], h4[:, t - 1, :], ALU.add))
            first, fpart = offs[0:EQ, 9, :].bitcast(I32), offs[0:EQ, 10, :].bitcast(I32)
            v_link(v.tensor_tensor(first, ps[0:EQ, 2, 0:BT * NT], offs[0:EQ, 0, :], ALU.add))
            v_link(v.tensor_scalar(fpart, first, LOW - 1, None, ALU.bitwise_and))
            v_link(v.tensor_copy(first_lo[:, :], fpart))
            v_link(v.tensor_scalar(fpart, first, 11, None, ALU.logical_shift_right))
            v_link(v.tensor_copy(first_hi[:, :], fpart))
            v_link(v.tensor_scalar(tk[:, 3:4], cs[:, NT - 1:NT], float(GS), float(GS), ALU.mult, ALU.add))
            v_link(v.tensor_scalar(pf_row[:, 0:NT], cs[0:1, :], float(GS), None, ALU.mult))
            v_link(v.tensor_scalar(pf_row[:, NT:], cols[0:1, 0:RG - 1], float(GS), tk[0:1, 3:4], ALU.mult, ALU.add))
            v_link(v.tensor_copy(meta[:, 0:1], cs[:, NT - 1:NT]))
            v_link(v.tensor_scalar(meta[:, 1:2], cs[:, NT - 1:NT], float(RG - 1), None, ALU.add))
            v_link(v.tensor_scalar(meta[:, 1:2], meta[:, 1:2], 3, None, ALU.logical_shift_right))
            v.sem_inc(meta_ready, 1)
            dve.wait_ge(viol_mm, 1)
            v.tensor_copy(meta[0:1, 2:3], ps[0:1, 3, 0:1]).then_inc(flag_ready, 1)
            gcol = offs[:, 6, 0:GJ]
            v_link(v.tensor_scalar(gcol, cols[:, 0:GJ], float(P), lane[:, 0:1], ALU.mult, ALU.add))
            v_link(v.tensor_tensor(bcmp, cs.unsqueeze(1).to_broadcast([P, GJ, NT]),
                                   gcol.unsqueeze(2).to_broadcast([P, GJ, NT]), ALU.is_lt))
            v_link(v.tensor_reduce(offs[:, 7, 0:GJ], bcmp, AX.X, ALU.add))
            v_link(v.tensor_scalar(gb_pj, offs[:, 7, 0:GJ], float(NT - 1), float(C), ALU.min, ALU.mult))
            v.sem_inc(gb_ready, 1)

            with dve.Fori(0, NG // 2) as i:
                chain.enter(i, 2 * (2 * G + 1 + NEWTON))
                for s in range(2):
                    dve.wait_ge(xg_in[s], 32 * (i + 1))
                    for t in range(G):
                        chain.inc(v.bn_stats(stats[:, t, :], x_g[s][:, t, :]))
                    chain.wait()
                    dve.sem_inc(passed, 1)
                    for t in range(G):
                        chain.inc(v.bn_aggr(mvs[:, t, :], stats[:, t, :]))
                    chain.wait()
                    v_link(v.tensor_scalar(newt[:, 1, 0:G], mvs[:, :, 1], EPS_LN, None, ALU.add))
                    newton(newt[:, 1, 0:G], rs[:, :], newt[:, 0, 0:G])
                    for t in range(G):
                        v.tensor_scalar(x_g[s][:, t, :], x_g[s][:, t, :], mvs[:, t, 0:1], rs[:, t:t + 1],
                                        ALU.subtract, ALU.mult).then_inc(xn_ready, 1)
                    dve.wait_ge(xn_ready, 2 * G * i + G * (s + 1))
            chain.leave(NG // 2)

            def edges(i, k):
                b = KB * i + k
                dve.wait_ge(rank_mm, RANK0 + b)
                one_hot(b, k).then_inc(oh_ready, 1)
                dve.wait_ge(relb_mm, b + 1)
                dve.wait_ge(main_mm, 2 * b + 6)
                v.tensor_scalar(oht[:, k % 2, :], ps[:, RELB, :], lane[:, 0:1], None,
                                ALU.is_equal).then_inc(oht_ready, 1)
                dve.wait_ge(rank_mm, RANK0 + b + 1)
                dve.wait_ge(oh_ready, b + 1)
                for t in range(BT):
                    q = slice(t * NT, (t + 1) * NT)
                    v.tensor_tensor_reduce(out=scr[:, q], in0=ps[:, RANK, q], in1=ohb[:, k, q], scale=1.0, scalar=0.0,
                                           op0=ALU.mult, op1=ALU.add,
                                           accum_out=posf[:, BT * k + t:BT * k + t + 1]).then_inc(rank_read, 1)
                dve.wait_ge(rows_left, b + 1)
                v.tensor_copy(rowbuf[:, BT * k:BT * (k + 1), C:RW], ws_t[:, ds(BT * b, BT), :]).then_inc(ws_ready, 1)
                dve.wait_ge(rank_read, RREAD0 + BT * (b + 1))
                v.tensor_copy(posu[:, BT * k:BT * (k + 1)], posf[:, BT * k:BT * (k + 1)]).then_inc(pos_ready, 1)

            def elu(i, u):
                n = 2 * i + u
                dve.wait_ge(kv_acc, n + 1)
                v.tensor_copy(vext[:, u, :, P:P + 1],
                              maskc[:, ds(n, 1)].unsqueeze(1).to_broadcast([P, CC, 1])).then_inc(elu_v, 1)
                dve.wait_ge(elu_a, ELUA0 + 5 * n + 2)
                dve.wait_ge(q_free, i + 1)
                v.scalar_tensor_tensor(qTb[:, u, :], eq[:, u, :], 1.0, rq[:, u, :], ALU.min,
                                       ALU.add).then_inc(elu_v, 1)
                dve.wait_ge(elu_a, ELUA0 + 5 * n + 4)
                v.scalar_tensor_tensor(kk[:, u, :], ek[:, u, :], 1.0, rk[:, u, :], ALU.min,
                                       ALU.add).then_inc(elu_v, 1)

            for s in range(2):
                dve.wait_ge(xg_out[s], 48 * (NG // 2))
            with dve.Fori(0, NT // 2) as i:
                edges(i, 0)
                edges(i, 1)
                elu(i, 0)
                edges(i, 2)
                elu(i, 1)
                edges(i, 3)

            dve.wait_ge(kv_acc, KVACC0 + NT + 1)
            for c in range(CC):
                for h in range(4):
                    q = slice(32 * h, 32 * h + 32)
                    chain.inc(v.tensor_copy(kvb[q, c, 32 * h:32 * h + 32],
                                            ps[q, KVA, c * (P + 1) + 32 * h:c * (P + 1) + 32 * h + 32]))
                    chain.inc(v.tensor_copy(kvb[q, c, P + h:P + h + 1],
                                            ps[q, KVA, c * (P + 1) + P:c * (P + 1) + P + 1]))
            chain.wait()
            v.sem_inc(kvb_ready, 1)
            dve.wait_ge(w_in, 16 * 12)
            dve.wait_ge(q_out, 16 * (NT // 2))

            def norm_affine(src2, out2, g_, b_, done):
                for u in range(2):
                    chain.inc(v.bn_stats(stats[:, u, :], src2[:, u, :]))
                chain.wait()
                dve.sem_inc(passed, 1)
                for u in range(2):
                    chain.inc(v.bn_aggr(mvs[:, u, :], stats[:, u, :]))
                chain.wait()
                v_link(v.tensor_scalar(newt[:, 1, 0:2], mvs[:, 0:2, 1], EPS_LN, None, ALU.add))
                for u in range(2):
                    chain.inc(v.scalar_tensor_tensor(out2[:, u, :], src2[:, u, :], mvs[:, u, 0:1], vec[:, g_, :],
                                                     ALU.subtract, ALU.mult))
                newton(newt[:, 1, 0:2], rs[:, 0:2], newt[:, 0, 0:2])
                for u in range(2):
                    done(v.scalar_tensor_tensor(out2[:, u, :], out2[:, u, :], rs[:, u:u + 1], vec[:, b_, :],
                                                ALU.mult, ALU.add))

            def mix_front(i):
                dve.wait_ge(t_mm, i + 1)
                den = ps[:, TPS:TPS + 2, 0:CC * (P + 4)].rearrange("p u (c f) -> p u c f", c=CC)
                for u in range(2):
                    chain.inc(v.tensor_scalar(rz[:, 8 * u:8 * u + 8].rearrange("p (c h) -> p c h", c=CC),
                                              den[:, u, :, P:P + 4], EPS_ATTN, None, ALU.add))
                chain.wait()
                v_link(v.reciprocal(rz[:, :], rz[:, :]))
                for u in range(2):
                    chain.inc(v.tensor_tensor(
                        tmp[:, u, :].rearrange("p (c h d) -> p c h d", c=CC, d=32),
                        den[:, u, :, 0:P].rearrange("p c (h d) -> p c h d", d=32),
                        rz[:, 8 * u:8 * u + 8].rearrange("p (c h) -> p c h", c=CC).unsqueeze(3).to_broadcast(
                            [P, CC, 4, 32]), ALU.mult))
                chain.wait()
                v_link(v.tensor_tensor(tmp, tmp, xnb, ALU.add))
                norm_affine(tmp, x1, LN1G, LN1B, lambda ins: ins.then_inc(x1_ready, 1))

            def mix_back(i):
                dve.wait_ge(y_mm, i + 1)
                dve.wait_ge(x1_ready, 2 * (i + 1))
                v_link(v.tensor_tensor(tmp, ps[:, YPS, :].rearrange("p (u c) -> p u c", u=2), x1, ALU.add))
                norm_affine(tmp, x1, LN2G, LN2B, chain.inc)
                chain.wait()
                dve.wait_ge(x_in, 32 * (i + 1))
                v.tensor_tensor(acc[:, ds(2 * C * i, 2 * C)].rearrange("p (u c) -> p u c", u=2), x1, xb,
                                ALU.add).then_inc(mix_done, 1)

            with dve.Fori(0, NT // 2) as i:
                chain.enter(i, 6 + 7 + NEWTON + 1 + 7 + NEWTON + 2)
                edges(NT // 2 + i, 0)
                mix_front(i)
                edges(NT // 2 + i, 1)
                edges(NT // 2 + i, 2)
                mix_back(i)
                edges(NT // 2 + i, 3)
            chain.leave(NT // 2)
            with dve.Fori(2 * (NT // 2), EQ) as i:
                for k in range(KB):
                    edges(i, k)

            dve.wait_ge(gb_in, 16)
            dve.wait_ge(mix_done, MIX0 + NT // 2)
            dve.wait_ge(main_mm, MAIN0 + 2 * NB)
            steps = dve.value_load(meta[0:1, 1:2], min_val=1, max_val=NGMAX // RG + 1)

            def add_groups(i, k):
                for h in range(2):
                    grp_ = RG * i + 2 * k + h
                    at = dve.value_load(gb_row[0:1, ds(grp_ + 1, 1)], min_val=0, max_val=(NT - 1) * C)
                    dve.wait_ge(grp_mm, GRP0 + grp_ + 1)
                    dve.wait_ge(acc_done, ACC0 + grp_)
                    v.tensor_tensor(acc[:, ds(at, C)], acc[:, ds(at, C)], ps[:, GRP + (2 * k + h) % 4, 0:C],
                                    ALU.add).then_inc(acc_done, 1)

            with dve.Fori(0, steps) as i:
                for k in range(KB):
                    dve.wait_ge(r_in[k], 16 * (i + 1))
                    dve.wait_ge(grp_mm, RG * i + 2 * k + 6)
                    for s in range(BT):
                        r = BT * k + s
                        v.tensor_scalar(oht[:, k % 2, s * P:(s + 1) * P], cols[:, :], rowbuf[:, r, C + 1:C + 2],
                                        rowbuf[:, r, C:C + 1], ALU.is_equal, ALU.mult).then_inc(ohw_ready, 1)
                    if k > 0:
                        add_groups(i, k - 1)
                add_groups(i, KB - 1)
            dve.wait_ge(acc_done, ACC0 + RG * steps)
            dve.sem_inc(passed, 1)

            with dve.Fori(0, NG) as i:
                chain.enter(i, 2 * G + 1)
                for t in range(G):
                    chain.inc(v.bn_stats(stats[:, t, :], acc[:, ds(i * GC + t * C, C)]))
                chain.wait()
                dve.sem_inc(passed, 1)
                for t in range(G):
                    chain.inc(v.bn_aggr(mvs[:, t, :], stats[:, t, :]))
                chain.wait()
                v_link(v.tensor_copy(mv[:, ds(G * i, G), :], mvs[:, :, :]))
            chain.leave(NG)
            v_link(v.tensor_scalar(newt[:, 1, :], mv[:, :, 1], EPS_LN, None, ALU.add))
            newton(newt[:, 1, :], rstd[:, :], newt[:, 0, :])

            def normed(out, col, tile):
                return v.tensor_scalar(out, acc[:, ds(col, C)], mv[:, ds(tile, 1), 0], rstd[:, ds(tile, 1)],
                                       ALU.subtract, ALU.mult)

            with dve.Fori(0, NG) as i:
                chain.enter(i, 2 * G + 1)
                for t in range(G):
                    chain.inc(normed(node[:, t * C:(t + 1) * C], i * GC + t * C, G * i + t))
                chain.wait()
                for t in range(G):
                    chain.inc(v.tensor_tensor_reduce(out=node[:, (G + t) * C:(G + t + 1) * C],
                                                     in0=node[:, t * C:(t + 1) * C], in1=vec[:, WR, :], scale=1.0,
                                                     scalar=0.0, op0=ALU.mult, op1=ALU.add,
                                                     accum_out=wcol[:, t:t + 1]))
                chain.wait()
                v_link(v.tensor_scalar(wts[:, ds(G * i, G)], wcol[:, :], br_c[:, 0:1], None, ALU.add))
            chain.leave(NG)

            wm, pen, hit = scr[:, 0:NT], scr[:, NT:2 * NT], scr[:, 2 * NT:3 * NT]
            v_link(v.tensor_scalar(pen, maskc[:, :], -1.0, 3.0e38, ALU.add, ALU.mult))
            v_link(v.tensor_tensor(wm, wts[:, :], maskc[:, :], ALU.mult))
            v_link(v.tensor_tensor(wm, wm, pen, ALU.add))
            key, cand, sign, thr, hitc, take = (tki[:, k:k + 1] for k in range(6))
            v_link(v.memset(key, 0))

            def decode(c):
                v_link(v.tensor_scalar(sign, c, 31, None, ALU.arith_shift_right))
                v_link(v.tensor_scalar(sign, sign, -1, SIGN, ALU.bitwise_xor, ALU.bitwise_or))
                v_link(v.tensor_tensor(thr, c, sign, ALU.bitwise_xor))

            with dve.Fori(0, 32) as i:
                chain.enter(i, 9)
                bit = bits[:, ds(31 - i, 1)]
                v_link(v.tensor_tensor(cand, key, bit, ALU.bitwise_or))
                decode(cand)
                v_link(v.tensor_scalar(hit, wm, tk[:, 3:4], None, ALU.is_ge))
                v_link(v.tensor_reduce(tk[:, 4:5], hit, AX.X, ALU.add))
                v.tensor_copy(cntb[:, :], tk[:, 4:5]).then_inc(cnt_ready, 1)
                dve.wait_ge(cnt_mm, i + 1)
                v_link(v.tensor_scalar(take, ps[:, 0, 0:1], float(KEEP), -1.0, ALU.is_ge, ALU.mult))
                v_link(v.tensor_tensor(take, take, bit, ALU.bitwise_and))
                v_link(v.tensor_tensor(key, key, take, ALU.bitwise_or))
            chain.leave(32)
            decode(key)
            gt, eqm = ohb[:, 0, 0:NT], ohb[:, 1, 0:NT]
            v_link(v.tensor_scalar(gt, wm, tk[:, 3:4], None, ALU.is_gt))
            v.tensor_scalar(eqm, wm, tk[:, 3:4], None, ALU.is_equal).then_inc(final_cnt, 1)
            dve.wait_ge(final_mm, 1)
            v_link(v.tensor_reduce(tk[:, 4:5], ps[:, 0, 0:NT], AX.X, ALU.add))
            v_link(v.tensor_scalar(tk[:, 4:5], tk[:, 4:5], -1.0, float(KEEP), ALU.mult, ALU.add))
            a, b_, d = scr[:, NT:2 * NT], scr[:, 2 * NT:3 * NT], 1
            e0 = scr[:, 3 * NT:4 * NT]
            v_link(v.tensor_copy(e0, ps[:, 1, 0:NT]))
            v_link(v.tensor_copy(a, e0))
            while d < NT:
                v_link(v.tensor_copy(b_[:, 0:d], a[:, 0:d]))
                v_link(v.tensor_tensor(b_[:, d:NT], a[:, d:NT], a[:, 0:NT - d], ALU.add))
                a, b_, d = b_, a, 2 * d
            v_link(v.tensor_tensor(a, a, e0, ALU.subtract))
            v_link(v.tensor_tensor(a, a, ps[:, 2, 0:NT], ALU.add))
            v_link(v.tensor_scalar(a, a, tk[:, 4:5], None, ALU.is_lt))
            v_link(v.tensor_tensor(a, a, eqm, ALU.mult))
            v_link(v.tensor_tensor(a, a, gt, ALU.add))
            v_link(v.tensor_tensor(wts[:, :], wts[:, :], a, ALU.mult))

            def ffn_in(i, s):
                for u in range(2):
                    normed(x3[:, s, u * C:(u + 1) * C], 2 * i * C + u * C, 2 * i + u).then_inc(x3_ready, 1)

            def ffn_out(i, s):
                dve.wait_ge(fy_mm, i + 1)
                dve.wait_ge(x3_ready, 2 * (i + 1))
                for u in range(2):
                    chain.inc(v.scalar_tensor_tensor(fo[:, s, u * C:(u + 1) * C], ps[:, 4 + s, u * C:(u + 1) * C],
                                                     wts[:, ds(2 * i + u, 1)], x3[:, s, u * C:(u + 1) * C],
                                                     ALU.mult, ALU.add))
                chain.wait()
                v.tensor_tensor(fo[:, s, :], fo[:, s, :], acc[:, ds(2 * i * C, 2 * C)], ALU.add).then_inc(o_ready, 1)

            def ffn_step(i, then):
                for s in range(2):
                    dve.wait_ge(fo_free, 2 * i + s + 1)
                    ffn_out(2 * i + s, s)
                    if s < then:
                        ffn_in(2 * i + 2 + s, s)

            ffn_in(0, 0)
            ffn_in(1, 1)
            with dve.Fori(0, NT // 4 - 1) as i:
                chain.enter(i, 4)
                ffn_step(i, 2)
            chain.leave(NT // 4 - 1)
            ffn_step(NT // 4 - 1, 1)
            dve.wait_ge(fo_free, 2 * (NT // 4) + 1)
            ffn_out(NT // 2 - 1, 0)


class Chain:

    def __init__(self, eng, sem):
        self.eng, self.sem, self.n, self.i = eng, sem, 0, None

    def inc(self, ins):
        ins.then_inc(self.sem, 1)
        self.n += 1

    def enter(self, i, per):
        self.before, self.n, self.i, self.per = self.n, 0, i, per

    def leave(self, count):
        assert self.n == self.per, (self.n, self.per)
        self.n, self.i = self.before + count * self.per, None

    def wait(self):
        at = self.n if self.i is None else self.before + self.i * self.per + self.n
        self.eng.wait_ge(self.sem, at)

    def link(self, ins):
        self.inc(ins)
        self.wait()


_INS = ["x", "src", "dst", "edge_weight", "L0_gnn_weight", "L0_mix_Wqkv", "L0_mix_ln1_g", "L0_mix_ln1_b",
        "L0_mix_W1", "L0_mix_b1", "L0_mix_W2", "L0_mix_b2", "L0_mix_ln2_g", "L0_mix_ln2_b", "L0_ffn_wr",
        "L0_ffn_br", "L0_ffn_w1", "L0_ffn_b1", "L0_ffn_w2", "L0_ffn_b2"]


def kernel(**inputs):
    import numpy as _np
    import concourse.bacc as _bacc
    from concourse import mybir as _mybir
    from concourse.bass_utils import run_bass_kernel_spmd as _run

    nc = _bacc.Bacc("TRN2", target_bir_lowering=False, num_devices=1)
    arrays, args = {}, []
    for name in _INS:
        a = _np.ascontiguousarray(inputs[name])
        arrays[f"in_{name}"] = a
        args.append(nc.dram_tensor(f"in_{name}", a.shape, _mybir.dt.from_np(a.dtype), kind="ExternalInput").ap())
    args.append(nc.dram_tensor("out_rows", (N, C), _mybir.dt.float32, kind="ExternalOutput").ap())
    gps_layer_kernel(nc, *args)
    r = _run(nc, [arrays], core_ids=[0])
    return r.results[0]["out_rows"]
```

```python
import concourse.bass as bass
from concourse import mybir
from contextlib import ExitStack
import numpy as np

N, C, E, HEADS, HID, NQKV = 12500, 256, 212500, 8, 1024, 768
P = 128
CC = C // P
NT = (N + P - 1) // P
LASTROWS = N - (NT - 1) * P
KEEP = max(1, int(0.5 * N)) - 1
EPS_LN, EPS_ATTN = 1e-5, 1e-6

BT = 4
BE = BT * P
KB = 4
EQ = -(-E // (BE * KB))
NB = EQ * KB
ET = NB * BT
EJ = ET // P
EPAD = ET * P

GS = 256
RW = C + 2
RG = 8
NGMAX = (EPAD + NT * (GS - 1)) // GS
NGROUPS = 1 + NGMAX + RG + 1
GJ = -(-NGROUPS // P)

G = 7
NG = NT // G


def gps_layer_kernel(nc, x, src, dst, edge_weight, gnn_w, wqkv, ln1_g, ln1_b, w1, b1, w2, b2,
                     ln2_g, ln2_b, wr, br, fw1, fb1, fw2, fb2, out):
    F32, BF16, F16, I32, U32 = (mybir.dt.float32, mybir.dt.bfloat16, mybir.dt.float16, mybir.dt.int32,
                                mybir.dt.uint32)
    ALU, ACT, AX = mybir.AluOpType, mybir.ActivationFunctionType, mybir.AxisListType
    ds = bass.ds
    SIGN = -2147483648
    LOW = 2048
    NEWTON = 2 + 3 * 3

    src_d = nc.dram_tensor("src_pad", [EPAD], I32).ap()
    dst_d = nc.dram_tensor("dst_pad", [EPAD], I32).ap()
    ew_d = nc.dram_tensor("weight_pad", [EPAD], F32).ap()
    xn_d = nc.dram_tensor("xn_rows", [NT * P, C], F32).ap()
    xnT_d = nc.dram_tensor("xn_transposed", [NT, P, C], F32).ap()
    sup_d = nc.dram_tensor("support_rows", [(NT + 1) * P, C], F32).ap()
    qT_d = nc.dram_tensor("q_transposed", [NT, P, C], F32).ap()
    rows_d = nc.dram_tensor("sorted_rows", [NGROUPS * GS, RW], F32).ap()
    gb_d = nc.dram_tensor("group_bucket", [GJ * P], I32).ap()

    with ExitStack() as ctx:
        def sb(name, shape, dt=F32):
            return ctx.enter_context(nc.sbuf_tensor(name, shape, dt))

        def sem(name):
            return ctx.enter_context(nc.semaphore(name))

        acc = sb("acc", [P, NT * C])
        tabs = sb("tabs", [P, 4 * ET])
        ws_t = tabs[:, 0:2 * ET].rearrange("p (t k) -> p t k", k=2)
        bkt_t = tabs[:, 2 * ET:3 * ET]
        dst_t = tabs[:, 3 * ET:4 * ET].bitcast(U32)
        fw1_s = tabs[:, 0:CC * HID].rearrange("p (c h) -> p c h", c=CC)
        fw2_s = tabs[:, CC * HID:2 * CC * HID].rearrange("p (k c) -> p k c", c=C)
        rel = sb("rel", [EQ, KB * BE], F16)
        d0_row = sb("d0_row", [1, NB], I32)
        wqkvT = sb("wqkvT", [P, CC, NQKV])
        gw_s = sb("gw_s", [P, CC, C])
        w1T = sb("w1T", [P, CC, C])
        w2T = sb("w2T", [P, CC, C])
        vec = sb("vec", [P, 7, C])
        LN1G, LN1B, LN2G, LN2B, B2, FB2, WR = range(7)
        b1_c = sb("b1_c", [P, CC])
        fb1_c = sb("fb1_c", [P, HID // P])
        br_c = sb("br_c", [P, 1])
        ident = sb("ident", [P, P])
        ident_h = sb("ident_h", [P, P], F16)
        ident_hi = sb("ident_hi", [P, P], F16)
        onecol = sb("onecol", [P, 2 * EQ], BF16)
        first_lo = sb("first_lo", [EQ, BT * NT], F16)
        first_hi = sb("first_hi", [EQ, BT * NT], F16)
        before = sb("before", [P, P], BF16)
        ones_b = sb("ones_b", [P, P], BF16)
        zeros_b = sb("zeros_b", [P, 512], BF16)
        onesf = sb("onesf", [P, P])
        lane = sb("lane", [P, 1])
        cols = sb("cols", [P, P])
        kvb = sb("kvb", [P, CC, P + 4])
        maskc = sb("maskc", [P, NT])
        meta = sb("meta", [P, 4], I32)
        gb_row = sb("gb_row", [1, GJ * P], I32)
        rowbuf = sb("rowbuf", [P, KB * BT, RW])
        oht = sb("oht", [P, 2, BE])
        win = sb("win", [P, KB, C])
        ohb = sb("ohb", [P, KB, BT * NT], BF16)
        posf = sb("posf", [P, KB * BT])
        posu = sb("posu", [P, KB * BT], U32)
        dsg = sb("dsg", [P, BT], U32)
        scr = sb("scr", [P, BT * NT])
        node = sb("node", [P, 14 * C])
        stats = sb("stats", [P, G, 6])
        mvs = sb("mvs", [P, G, 2])
        newt = sb("newt", [P, 3, NT])
        rs = sb("rs", [P, G])
        rz = sb("rz", [P, 2 * HEADS])
        wts = sb("wts", [P, NT])
        wcol = sb("wcol", [P, G])
        mv = sb("mv", [P, NT, 2])
        rstd = sb("rstd", [P, NT])
        tk = sb("tk", [P, 8])
        tki = tk[:, :].bitcast(I32)
        minus_lane = sb("minus_lane", [P, 1])
        one = sb("one", [P, 1])
        spare = sb("spare", [P, 1])
        bits = sb("bits", [P, 16, 6], I32)
        cands = sb("cands", [P, 4, 3])
        candi = cands[:, :, :].bitcast(I32)
        cntb = sb("cntb", [P, 3], BF16)

        def part(at, *shape, of=acc):
            n = int(np.prod(shape))
            ap = of[:, at:at + n]
            if len(shape) == 1:
                return ap
            if len(shape) == 2:
                return ap.rearrange("p (a b) -> p a b", a=shape[0])
            return ap.rearrange("p (a b c) -> p a b c", a=shape[0], b=shape[1])

        GC = G * C
        x_g = [part(s * GC, G, C) for s in range(2)]
        xnT_g = [part((2 + s) * GC, G, C) for s in range(2)]
        sup_g = [part((4 + s) * GC, G, C) for s in range(2)]
        raw0 = 6 * GC
        rsrc, rdst, rew, fbkt, floc, fdst = (part(raw0 + k * ET, ET) for k in range(6))
        rrel = part(raw0 + 6 * ET, KB * BE)
        wraw = part(0, 10, C)
        offs = part(raw0, 16, BT * NT)
        bcmp = part(raw0 + 7000, GJ, NT)
        beforef = part(raw0 + 8000, P)
        xnT_b = [part(k * C, C) for k in range(2)]
        eq, rq, qTb, ek, rk, kk = (part((2 + 2 * k) * C, 2, C) for k in range(6))
        vext = part(14 * C, 2, CC, P + 1)
        qTm, xnb, xb, tmp, x1, x1T, hT = (part(2 * C * k, 2, C, of=node) for k in range(7))
        sums = part(0, KB, 2 * C, of=node)
        x3, x3T, fo = (part(4 * C * k, 2, 2 * C, of=node) for k in range(3))
        y2 = wqkvT[:, 0, 0:2 * C].rearrange("p (u c) -> p u c", u=2)
        fhT = rowbuf[:, :, :].rearrange("p a b -> p (a b)")[:, 0:2 * 8 * 2 * P].rearrange(
            "p (s m r) -> p s m r", s=2, m=HID // P)
        zrow = node[:, 0:2 * RW]
        padi = node[0:1, 600:600 + EPAD - E].bitcast(I32)
        pf_row = node[0:1, 1200:1200 + NT + RG - 1].bitcast(I32)
        last_dst = node[0:1, 1420:1421].bitcast(I32)
        padj = node[0:1, 1500:1500 + EPAD - E].bitcast(I32)
        gb_pj = node[:, 1400:1400 + GJ].bitcast(I32)

        ps = ctx.enter_context(nc.psum_tensor("ps", [P, 8, 512], F32))
        RANK, RELB, MSG, KVA, QPS, KVPS = 0, 1, 2, 4, 5, 6
        TPS, XTPS, HPS, YPS = 4, 6, 7, 6
        GRP = 4

        (padsrc, padded, w_in, raw_in, wraw_in, d0_in, iotas, consts, dstep, pstep) = (sem(n) for n in (
            "padsrc", "padded", "w_in", "raw_in", "wraw_in", "d0_in", "iotas", "consts", "dstep", "pstep"))
        (raw_ready, tab_mm, tab_read, viol_ready, viol_mm, flag_ready) = (sem(n) for n in (
            "raw_ready", "tab_mm", "tab_read", "viol_ready", "viol_mm", "flag_ready"))
        (hist_oh, hist_mm, base_ready, base_mm, meta_ready, gb_ready, gb_out, gb_in, cleared) = (sem(n) for n in (
            "hist_oh", "hist_mm", "base_ready", "base_mm", "meta_ready", "gb_ready", "gb_out", "gb_in", "cleared"))
        xg_in = [sem(f"xg_in{s}") for s in range(2)]
        xg_out = [sem(f"xg_out{s}") for s in range(2)]
        (xn_ready, tr_mm, xnT_ready, sup_mm, sup_ready) = (sem(n) for n in (
            "xn_ready", "tr_mm", "xnT_ready", "sup_mm", "sup_ready"))
        (oh_ready, rank_mm, rank_read, relb_mm, oht_ready, main_mm, row_ready, pos_ready, ws_ready) = (
            sem(n) for n in ("oh_ready", "rank_mm", "rank_read", "relb_mm", "oht_ready", "main_mm",
                             "row_ready", "pos_ready", "ws_ready"))
        win_in = [sem(f"win_in{k}") for k in range(KB)]
        scat = [sem(f"scattered{k}") for k in range(KB)]
        dsg_ready, gath = sem("dsg_ready"), sem("gathered")
        xnTb_in = [sem(f"xnTb_in{u}") for u in range(2)]
        (q_mm, kv_mm, elu_a, elu_v, kv_acc, q_out, kvb_ready) = (sem(n) for n in (
            "q_mm", "kv_mm", "elu_parts", "elu_done", "kv_acc", "q_out", "kvb_ready"))
        (qxn_in, x_in, t_mm, x1_ready, x1T_mm, x1T_ready, h_mm, h_ready, y_mm, mix_done) = (sem(n) for n in (
            "qxn_in", "x_in", "t_mm", "x1_ready", "x1T_mm", "x1T_ready", "h_mm", "h_ready", "y_mm", "mix_done"))
        abs_done = sem("abs_done")
        fw_in, last_in, t_read, xnb_read = (sem(n) for n in ("fw_in", "last_in", "t_read", "xnb_read"))
        passed = sem("passed")
        r_in = [sem(f"rows_in{k}") for k in range(KB)]
        (ohw_ready, grp_mm, acc_done, cnt_ready, cnt_mm, final_cnt, final_mm) = (sem(n) for n in (
            "ohw_ready", "grp_mm", "acc_done", "cnt_ready", "cnt_mm", "final_cnt", "final_mm"))
        (x3_ready, x3T_mm, x3T_ready, fh_mm, fh_ready, fy_mm, o_ready) = (sem(n) for n in (
            "x3_ready", "x3T_mm", "x3T_ready", "fh_mm", "fh_ready", "fy_mm", "o_ready"))
        sums_ready = sem("sums_ready")
        o_out, q_free, fo_free, rows_left = (sem(n) for n in ("o_out", "q_free", "fo_free", "rows_left"))

        MAIN0, ROW0, OHT0, RANK0, RREAD0, MIX0 = 2 * KB, 2, 1, 1, 1, 1
        ELUA0, ELUV0, KVACC0 = 10, 6, 2
        XNT0, SUP0 = 2, 2
        GRP0, SUM0, ACC0 = 2 * KB, KB, 2 * KB
        XT0, FH0 = 1, 2
        TREAD0, QFREE0, FO0, LEFT0 = 2, 1, 2, KB
        TAB = 16 + 6

        block = ctx.enter_context(nc.Block())
        tiles_of = lambda d: d.rearrange("(t p) c -> t p c", p=P)
        lanes = lambda d: d.rearrange("t p c -> p t c")
        xr = tiles_of(x[0:(NT - 1) * P, :])

        @block.sync
        def _(sp):
            sp.sem_inc(q_free, QFREE0)
            sp.sem_inc(fo_free, FO0)
            row = lambda d: d.rearrange("(a b) -> a b", a=1)
            sp.dma_start(last_dst, row(dst[E - 1:E])).then_inc(last_in, 16)
            for k, (a, n) in enumerate(((wqkv, 6), (w1, 2), (w2, 2))):
                at = (0, 6, 8)[k]
                sp.dma_start(wraw[:, at:at + n, :], a.rearrange("(k p) c -> p k c", p=P)).then_inc(wraw_in, 16)
            sp.dma_start(src_d[0:E], src).then_inc(padded, 16)
            sp.dma_start(dst_d[0:E], dst).then_inc(padded, 16)
            sp.dma_start(ew_d[0:E], edge_weight).then_inc(padded, 16)
            sp.wait_ge(padsrc, 2)
            sp.dma_start(row(src_d[E:EPAD]), padi).then_inc(padded, 16)
            sp.dma_start(row(ew_d[E:EPAD]), zrow[0:1, 0:EPAD - E]).then_inc(padded, 16)
            sp.wait_ge(padsrc, 3)
            sp.dma_start(row(dst_d[E:EPAD]), padj).then_inc(padded, 16)
            sp.dma_start(sup_d[NT * P:, :], zrow[:, 0:C]).then_inc(w_in, 16)
            sp.dma_start(gw_s[:, :, :], gnn_w.rearrange("(k p) c -> p k c", p=P)).then_inc(w_in, 16)
            sp.wait_ge(padded, 96)
            for a, d in ((rsrc, src_d), (rdst, dst_d)):
                sp.dma_start(a.bitcast(I32).rearrange("r (j e) -> r j e", e=P),
                             d.rearrange("(j r e) -> r j e", r=P, e=P)).then_inc(raw_in, 16)
            sp.dma_start(rew.rearrange("r (j e) -> r j e", e=P),
                         ew_d.rearrange("(j r e) -> r j e", r=P, e=P)).then_inc(raw_in, 16)
            sp.dma_start(rrel[0:EQ, :].bitcast(I32), dst_d.rearrange("(q f) -> q f", q=EQ)).then_inc(raw_in, 16)
            sp.dma_start(d0_row[0:1, :], dst_d.rearrange("(a b e) -> a b e", a=1, e=BE)[:, :, 0],
                         allow_slow_non_contiguous=True).then_inc(d0_in, 16)
            for k, v in enumerate((ln1_g, ln1_b, ln2_g, ln2_b, b2, fb2, wr.rearrange("a b -> (a b)"))):
                sp.dma_start(vec[:, k, :], v.partition_broadcast(P)).then_inc(w_in, 16)
            sp.dma_start(b1_c[:, :], b1.rearrange("(k p) -> p k", p=P),
                         allow_slow_non_contiguous=True).then_inc(w_in, 16)
            sp.dma_start(fb1_c[:, :], fb1.rearrange("(k p) -> p k", p=P),
                         allow_slow_non_contiguous=True).then_inc(w_in, 16)
            sp.dma_start(br_c[:, :], br.partition_broadcast(P)).then_inc(w_in, 16)

            sp.wait_ge(tab_read, 6)

            def x_load(s, g):
                sp.dma_start(x_g[s][:, 0:G - 1, :], lanes(xr[ds(g * G, G - 1)])).then_inc(xg_in[s], 16)
                sp.dma_start(x_g[s][:, G - 1, :], x[ds((g * G + G - 1) * P, P), :]).then_inc(xg_in[s], 16)

            def x_load_last(s):
                sp.dma_start(x_g[s][:, 0:G - 1, :], lanes(xr[(NG - 1) * G:NT - 1])).then_inc(xg_in[s], 16)
                sp.dma_start(x_g[s][0:LASTROWS, G - 1, :], x[(NT - 1) * P:N, :]).then_inc(xg_in[s], 16)

            def stage_out(s, g):
                sp.wait_ge(xn_ready, G * (g + 1))
                sp.dma_start(lanes(tiles_of(xn_d)[ds(g * G, G)]), x_g[s]).then_inc(xg_out[s], 16)
                sp.wait_ge(xnT_ready, XNT0 + G * (g + 1))
                sp.dma_start(lanes(xnT_d[ds(g * G, G)]), xnT_g[s]).then_inc(xg_out[s], 16)
                sp.wait_ge(sup_ready, SUP0 + G * (g + 1))
                sp.dma_start(lanes(tiles_of(sup_d[0:NT * P])[ds(g * G, G)]), sup_g[s]).then_inc(xg_out[s], 16)

            x_load(0, 0)
            x_load(1, 1)
            with sp.Fori(0, NG // 2 - 2) as i:
                for s in range(2):
                    stage_out(s, 2 * i + s)
                    sp.wait_ge(xg_out[s], 48 * (i + 1))
                    x_load(s, 2 * i + 2 + s)
            for s in range(2):
                stage_out(s, NG - 4 + s)
                sp.wait_ge(xg_out[s], 48 * (NG // 2 - 1))
                if s == 0:
                    x_load(0, NG - 2)
                else:
                    x_load_last(1)
            for s in range(2):
                stage_out(s, NG - 2 + s)

            sp.wait_ge(gb_ready, 1)
            sp.dma_start(gb_d.rearrange("(j p) -> p j", p=P), gb_pj,
                         allow_slow_non_contiguous=True).then_inc(gb_out, 16)
            sp.wait_ge(gb_out, 16)
            sp.dma_start(gb_row[0:1, :], row(gb_d)).then_inc(gb_in, 16)
            for s in range(2):
                sp.wait_ge(xg_out[s], 48 * (NG // 2))
            sp.wait_ge(d0_in, 16)

            def window(i, k):
                b = KB * i + k
                sp.wait_ge(main_mm, 2 * b + 2)
                first = sp.value_load(d0_row[0:1, ds(b, 1)], min_val=0, max_val=N - 1)
                sp.dma_start(win[:, k, :], sup_d[ds(first, P), :]).then_inc(win_in[k], 16)

            def att_load(u, n):
                sp.dma_start(xnT_b[u], xnT_d[ds(n, 1)].rearrange("a p c -> (a p) c")).then_inc(xnTb_in[u], 16)

            def att_step(i, more):
                for k in range(KB):
                    if k == 3:
                        sp.wait_ge(elu_v, ELUV0 + 6 * i + 5)
                        sp.dma_start(lanes(qT_d[ds(2 * i, 2)]), qTb).then_inc(q_out, 16)
                    window(i + 1, k)
                    if more and k < 2:
                        sp.wait_ge(kv_mm, 2 * i + k + 1)
                        att_load(k, 2 * i + 2 + k)
                sp.wait_ge(q_out, 16 * (i + 1))
                sp.sem_inc(q_free, 1)

            for k in range(KB):
                window(0, k)
                if k < 2:
                    att_load(k, k)
            with sp.Fori(0, NT // 2 - 1) as i:
                att_step(i, True)
            att_step(NT // 2 - 1, False)
            sp.wait_ge(q_out, 16 * (NT // 2))
            sp.wait_ge(cleared, 16 * (NT + RG - 1))

            def front_load(i):
                sp.dma_start(qTm, lanes(qT_d[ds(2 * i, 2)])).then_inc(qxn_in, 16)
                sp.dma_start(xnb, lanes(tiles_of(xn_d)[ds(2 * i, 2)])).then_inc(qxn_in, 16)

            def x_back(i, last=False):
                sp.dma_start(xb[:, 0, :], x[ds(2 * P * i, P), :]).then_inc(x_in, 16)
                if last:
                    sp.dma_start(xb[0:LASTROWS, 1, :], x[(NT - 1) * P:N, :]).then_inc(x_in, 16)
                else:
                    sp.dma_start(xb[:, 1, :], x[ds(2 * P * i + P, P), :]).then_inc(x_in, 16)

            def mix_step(i, front=True, last=False):
                e = NT // 2 + i
                window(e + 1, 0)
                if front:
                    sp.wait_ge(t_mm, i + 1)
                    sp.wait_ge(xnb_read, i + 1)
                    front_load(i + 1)
                window(e + 1, 1)
                window(e + 1, 2)
                window(e + 1, 3)
                sp.wait_ge(mix_done, MIX0 + i)
                x_back(i, last)

            front_load(0)
            with sp.Fori(0, NT // 2 - 1) as i:
                mix_step(i)
            mix_step(NT // 2 - 1, front=False, last=True)
            with sp.Fori(2 * (NT // 2) + 1, EQ) as i:
                for k in range(KB):
                    window(i, k)

            for k in range(KB):
                sp.wait_ge(scat[k], 16 * BT * EQ)
            sp.wait_ge(rank_mm, RANK0 + NB)
            sp.dma_start(fw1_s, fw1.rearrange("(k p) c -> p k c", p=P)).then_inc(fw_in, 16)
            sp.dma_start(fw2_s, fw2.rearrange("(k p) c -> p k c", p=P)).then_inc(fw_in, 16)
            steps = sp.value_load(meta[0:1, 1:2], min_val=1, max_val=NGMAX // RG + 1)
            with sp.Fori(0, steps) as i:
                for k in range(KB):
                    sp.wait_ge(grp_mm, RG * i + 2 * k + 2)
                    sp.dma_start(rowbuf[:, k * BT:(k + 1) * BT, :].rearrange("p (g k) f -> p g (k f)", g=2),
                                 rows_d[ds((RG * i + 2 * k + 1) * GS, 2 * GS), :].rearrange(
                                     "(g p k) f -> p g (k f)", g=2, p=P)).then_inc(r_in[k], 16)

            def out_store(i, s):
                sp.wait_ge(o_ready, i + 1)
                sp.dma_start(lanes(tiles_of(out[0:(NT - 1) * P, :])[ds(2 * i, 2)]),
                             fo[:, s, :].rearrange("p (u c) -> p u c", u=2)).then_inc(o_out, 16)
                sp.wait_ge(o_out, 16 * (i + 1))
                sp.sem_inc(fo_free, 1)

            with sp.Fori(0, NT // 4) as i:
                out_store(2 * i, 0)
                out_store(2 * i + 1, 1)
            sp.wait_ge(o_ready, NT // 2)
            sp.dma_start(out[(NT - 2) * P:(NT - 1) * P, :], fo[:, 0, 0:C]).then_inc(o_out, 16)
            sp.dma_start(out[(NT - 1) * P:N, :], fo[0:LASTROWS, 0, C:2 * C]).then_inc(o_out, 16)
            sp.wait_ge(o_out, 16 * 2 * (NT // 4) + 32)

        @block.gpsimd
        def _(pool):
            g = nc.gpsimd
            g.memset(zrow, 0.0).then_inc(padsrc, 1)
            g.memset(padi, NT * P - 1).then_inc(padsrc, 1)
            pool.wait_ge(last_in, 16)
            g.tensor_copy(padj, last_dst.to_broadcast([1, EPAD - E])).then_inc(padsrc, 1)
            g.iota(lane[:, :], [[0, 1]], base=0, channel_multiplier=1,
                   allow_small_or_imprecise_dtypes=True).then_inc(iotas, 1)
            g.iota(cols[:, :], [[1, P]], base=0, channel_multiplier=0,
                   allow_small_or_imprecise_dtypes=True).then_inc(iotas, 1)
            g.memset(zeros_b[:, :], 0.0).then_inc(iotas, 1)
            g.memset(ones_b[:, :], 1.0).then_inc(iotas, 1)
            g.memset(onesf[:, :], 1.0).then_inc(iotas, 1)
            g.memset(maskc[:, :], 1.0).then_inc(iotas, 1)
            g.memset(kvb[:, :, :], 0.0).then_inc(iotas, 1)
            g.iota(bits[:, :, :], [[2, 16], [0, 6]], base=0, channel_multiplier=0).then_inc(iotas, 1)

            pool.wait_ge(meta_ready, 1)
            with pool.Fori(0, NT + RG - 1) as i:
                at = pool.value_load(pf_row[0:1, ds(i, 1)], min_val=0, max_val=(NGROUPS - 1) * GS)
                pool.dma_start(rows_d[ds(at, GS), :].rearrange("(p k) f -> p (k f)", p=P),
                             zrow[:, :]).then_inc(cleared, 16)
            pool.wait_ge(cleared, 16 * (NT + RG - 1))
            pool.wait_ge(flag_ready, 1)
            wide = pool.value_load(meta[0:1, 2:3], min_val=0, max_val=EQ)

            def scatter(i, k, first=False):
                b = KB * i + k
                pool.wait_ge(pos_ready, b + 1)
                pool.wait_ge(ws_ready, b + 1)
                pool.wait_ge(row_ready, ROW0 + 2 * b + 2)
                pool.sem_inc(passed, 1)
                with pool.If(wide > 0):
                    g.tensor_copy(dsg[:, :], dst_t[:, ds(BT * b, BT)]).then_inc(dsg_ready, 1)
                    pool.wait_ge(dsg_ready, b + 1)
                    pool.sem_inc(passed, 1)
                    for t in range(BT):
                        g.indirect_dma_start(rowbuf[:, BT * k + t, 0:C], None, sup_d,
                                             bass.IndirectOffsetOnAxis(dsg[:, t:t + 1], 0)).then_inc(gath, 16)
                    pool.wait_ge(gath, 16 * BT * (b + 1))
                    pool.sem_inc(passed, 1)
                for t in range(BT):
                    s = BT * k + t
                    g.indirect_dma_start(rows_d, bass.IndirectOffsetOnAxis(posu[:, s:s + 1], 0),
                                         rowbuf[:, s, :], None).then_inc(scat[k], 16)
                if not first:
                    pool.wait_ge(scat[(k - 1) % KB], 16 * BT * (i + (k > 0)))
                    pool.sem_inc(rows_left, 1)

            pool.sem_inc(rows_left, LEFT0)
            for k in range(KB):
                scatter(0, k, first=k == 0)
            with pool.Fori(1, EQ) as i:
                for k in range(KB):
                    scatter(i, k)

            pool.sem_inc(acc_done, ACC0)
            pool.wait_ge(gb_in, 16)
            pool.wait_ge(mix_done, MIX0 + NT // 2)
            steps = pool.value_load(meta[0:1, 1:2], min_val=1, max_val=NGMAX // RG + 1)
            with pool.Fori(0, steps) as i:
                for k in range(KB):
                    for h in range(2):
                        group = RG * i + 2 * k + h
                        at = pool.value_load(gb_row[0:1, ds(group + 1, 1)], min_val=0, max_val=(NT - 1) * C)
                        pool.wait_ge(sums_ready, SUM0 + KB * i + k + 1)
                        pool.wait_ge(acc_done, ACC0 + group)
                        g.tensor_tensor(acc[:, ds(at, C)], acc[:, ds(at, C)], sums[:, k, h * C:(h + 1) * C],
                                        ALU.add).then_inc(acc_done, 1)

        @block.tensor
        def _(pe):
            mm, tp = nc.tensor.matmul, nc.tensor.transpose
            pe.sem_inc(main_mm, MAIN0)
            pe.sem_inc(rank_mm, RANK0)
            pe.sem_inc(kv_acc, KVACC0)
            pe.sem_inc(grp_mm, GRP0)
            pe.wait_ge(consts, 5)
            pe.wait_ge(iotas, 8)

            def blocks(job, items):
                if job >= 8:
                    pe.wait_ge(tab_read, job - 7)
                for k, a in enumerate(items):
                    last = tp(ps[:, job % 8, k * P:(k + 1) * P], a, ident[:, :])
                last.then_inc(tab_mm, 1)

            pe.wait_ge(wraw_in, 48)
            for job, (rows, c) in enumerate((([0, 1, 2, 3], 0), ([4, 5], 0), ([0, 1, 2, 3], 1), ([4, 5], 1))):
                blocks(job, [wraw[:, r, c * P:(c + 1) * P] for r in rows])
            for job, at in ((4, 6), (5, 8)):
                blocks(job, [wraw[:, at + r, c * P:(c + 1) * P] for c in range(CC) for r in range(2)])
            pe.wait_ge(raw_in, 64)
            for k, tab in enumerate((fbkt, floc, rew, fdst)):
                pe.wait_ge(raw_ready, (2, 4, 4, 5)[k])
                for q in range(4):
                    n = min(4, EJ - 4 * q)
                    blocks(6 + 4 * k + q, [tab[:, (4 * q + r) * P:(4 * q + r + 1) * P] for r in range(n)])
            pe.wait_ge(tab_read, TAB)
            pe.wait_ge(viol_ready, 1)
            mm(ps[0:1, 3, 0:1], tk[0:EQ, 0:1], onesf[0:EQ, 0:1], start=True, stop=True).then_inc(viol_mm, 1)

            hist = ps[0:EQ, RANK, 0:BT * NT]
            mm(hist, zeros_b[:, 0:EQ], zeros_b[:, 0:BT * NT], start=True, stop=False)
            with pe.Fori(0, EQ) as i:
                for k in range(KB):
                    pe.wait_ge(hist_oh, KB * i + k + 1)
                    pe.sem_inc(passed, 1)
                    mm(hist, onecol[:, ds(EQ - 1 - i, EQ)], ohb[:, k, :], start=False, stop=False).then_inc(hist_mm, 1)
            mm(hist, zeros_b[:, 0:EQ], zeros_b[:, 0:BT * NT], start=False, stop=True).then_inc(hist_mm, 1)
            pe.wait_ge(base_ready, 1)
            mm(ps[:, 1, 0:BT * NT], onesf[0:EQ, :], offs[0:EQ, 1, :], start=True, stop=True)
            mm(ps[0:EQ, 2, 0:BT * NT], beforef[0:EQ, 0:EQ], offs[0:EQ, 1, :], start=True, stop=True).then_inc(base_mm, 1)

            pe.wait_ge(w_in, 16 * 12)
            pe.wait_ge(flag_ready, 1)
            pe.wait_ge(meta_ready, 1)
            with pe.Fori(0, NG // 2) as i:
                for n in range(2 * G):
                    s, t = n // G, n % G
                    tile = 2 * G * i + n
                    pe.wait_ge(xn_ready, tile + 1)
                    pe.wait_ge(xnT_ready, tile + 1)
                    for c in range(CC):
                        last = tp(ps[:, 4 + n % 2, c * P:(c + 1) * P], x_g[s][:, t, c * P:(c + 1) * P], ident[:, :])
                    last.then_inc(tr_mm, 1)
                    pe.wait_ge(xnT_ready, XNT0 + tile + 1)
                    pe.wait_ge(sup_ready, tile + 1)
                    for c in range(CC):
                        last = mm(ps[:, 6 + n % 2, 0:C], xnT_g[s][:, t, c * P:(c + 1) * P], gw_s[:, c, :],
                                  start=c == 0, stop=c == CC - 1)
                    last.then_inc(sup_mm, 1)
            pe.wait_ge(sup_ready, SUP0 + NT)
            mm(ps[:, KVA, 0:CC * (P + 1)], zeros_b[:, 0:P], zeros_b[:, 0:CC * (P + 1)], start=True, stop=False)

            def relb(i, k):
                pe.wait_ge(oht_ready, KB * i + k + 1)
                mm(ps[:, RELB, :], ident_h[0:EQ, ds(i, 1)].to_broadcast([EQ, P]), rel[:, k * BE:(k + 1) * BE],
                   start=True, stop=True).then_inc(relb_mm, 1)

            def ranks(i, k, more=True):
                b = KB * i + k
                pe.wait_ge(oht_ready, OHT0 + b + 1)
                if more:
                    relb(*((i, k + 1) if k + 1 < KB else (i + 1, 0)))
                pe.wait_ge(rank_read, RREAD0 + BT * b)
                rank = ps[:, RANK, 0:BT * NT]
                mm(rank, ident_h[0:EQ, ds(i, 1)].to_broadcast([EQ, P]), first_lo[:, :], start=True, stop=False)
                mm(rank, ident_hi[0:EQ, ds(i, 1)].to_broadcast([EQ, P]), first_hi[:, :], start=False, stop=False)
                for j in range(k):
                    mm(rank, ones_b[:, :], ohb[:, j, :], start=False, stop=False)
                pe.wait_ge(oh_ready, b + 1)
                mm(rank, before[:, :], ohb[:, k, :], start=False, stop=True).then_inc(rank_mm, 1)

            def messages(i, k):
                b = KB * i + k
                pe.wait_ge(win_in[k], 16 * (i + 1))
                for h in range(2):
                    pe.wait_ge(row_ready, 2 * b + h + 1)
                    for t in range(2):
                        last = mm(ps[:, MSG + h, t * C:(t + 1) * C], oht[:, k % 2, (2 * h + t) * P:(2 * h + t + 1) * P],
                                  win[:, k, :], start=True, stop=True)
                    last.then_inc(main_mm, 1)

            def edges(i, k, more=True):
                ranks(i, k, more)
                messages(i, k)

            def qkv(i, u):
                n = 2 * i + u
                pe.wait_ge(xnTb_in[u], 16 * (i + 1))
                pe.wait_ge(elu_a, 5 * n + 7)
                for m in range(CC):
                    for c in range(CC):
                        last = mm(ps[:, QPS, u * C + m * P:u * C + (m + 1) * P], wqkvT[:, c, m * P:(m + 1) * P],
                                  xnT_b[u][:, c * P:(c + 1) * P], start=c == 0, stop=c == CC - 1)
                last.then_inc(q_mm, 1)
                for c in range(CC):
                    last = mm(ps[:, KVPS + u, :], xnT_b[u][:, c * P:(c + 1) * P], wqkvT[:, c, C:3 * C],
                              start=c == 0, stop=c == CC - 1)
                last.then_inc(kv_mm, 1)

            def kv_sum(i, u):
                n = 2 * i + u
                pe.wait_ge(elu_v, ELUV0 + 3 * n + 3)
                pe.wait_ge(elu_a, ELUA0 + 5 * n + 5)
                for c in range(CC):
                    last = mm(ps[:, KVA, c * (P + 1):(c + 1) * (P + 1)], kk[:, u, c * P:(c + 1) * P],
                              vext[:, u, c, :], start=False, stop=False)
                last.then_inc(kv_acc, 1)

            relb(0, 0)
            with pe.Fori(0, NT // 2) as i:
                edges(i, 0)
                qkv(i, 0)
                edges(i, 1)
                qkv(i, 1)
                edges(i, 2)
                kv_sum(i, 0)
                edges(i, 3)
                kv_sum(i, 1)
            mm(ps[:, KVA, 0:CC * (P + 1)], zeros_b[:, 0:P], zeros_b[:, 0:CC * (P + 1)], start=False,
               stop=True).then_inc(kv_acc, 1)
            pe.wait_ge(kvb_ready, 1)
            pe.wait_ge(elu_a, ELUA0 + 5 * NT)
            pe.wait_ge(w_in, 16 * 12)

            def attend(i):
                pe.wait_ge(qxn_in, 32 * (i + 1))
                pe.wait_ge(t_read, 2 * i + 2)
                for u in range(2):
                    for c in range(CC):
                        last = mm(ps[:, TPS + u, c * (P + 4):(c + 1) * (P + 4)], qTm[:, u, c * P:(c + 1) * P],
                                  kvb[:, c, :], start=True, stop=True)
                last.then_inc(t_mm, 1)

            def x1_transpose(i):
                pe.wait_ge(x1_ready, 2 * (i + 1))
                for c in range(CC):
                    for u in range(2):
                        last = tp(ps[:, XTPS, (2 * c + u) * P:(2 * c + u + 1) * P], x1[:, u, c * P:(c + 1) * P],
                                  ident[:, :])
                last.then_inc(x1T_mm, 1)

            def mlp_up(i):
                pe.wait_ge(x1T_ready, i + 1)
                for m in range(CC):
                    for c in range(CC):
                        last = mm(ps[:, HPS, m * C:(m + 1) * C], w1T[:, c, m * P:(m + 1) * P], x1T[:, c, :],
                                  start=c == 0, stop=c == CC - 1)
                last.then_inc(h_mm, 1)

            def mlp_down(i):
                pe.wait_ge(h_ready, 2 * (i + 1))
                for u in range(2):
                    for m in range(CC):
                        mm(ps[:, YPS, u * C:(u + 1) * C], hT[:, m, u * P:(u + 1) * P], w2T[:, m, :],
                           start=m == 0, stop=False)
                    last = mm(ps[:, YPS, u * C:(u + 1) * C], onesf[0:1, :], vec[0:1, B2, :], start=False, stop=True)
                last.then_inc(y_mm, 1)

            def mix_step(i, front, back):
                e = NT // 2 + i
                ranks(e, 0)
                if front:
                    attend(i)
                if back:
                    mlp_up(i - 1)
                messages(e, 0)
                ranks(e, 1)
                if back:
                    mlp_down(i - 1)
                messages(e, 1)
                edges(e, 2)
                edges(e, 3)
                if front:
                    x1_transpose(i)

            mix_step(0, True, False)
            with pe.Fori(1, NT // 2) as i:
                mix_step(i, True, True)
            mix_step(NT // 2, False, True)
            with pe.Fori(2 * (NT // 2) + 1, EQ - 1) as i:
                for k in range(KB):
                    edges(i, k)
            for k in range(KB):
                edges(EQ - 1, k, more=k + 1 < KB)

            pe.wait_ge(mix_done, MIX0 + NT // 2)
            pe.wait_ge(row_ready, ROW0 + 2 * NB)
            steps = pe.value_load(meta[0:1, 1:2], min_val=1, max_val=NGMAX // RG + 1)
            with pe.Fori(0, steps) as i:
                for k in range(KB):
                    pe.wait_ge(r_in[k], 16 * (i + 1))
                    pe.wait_ge(sums_ready, KB * i + k + 1)
                    for h in range(2):
                        grp = RG * i + 2 * k + h
                        for t in range(2):
                            pe.wait_ge(ohw_ready, 2 * grp + t + 1)
                            s = 2 * h + t
                            last = mm(ps[:, GRP + k, h * C:(h + 1) * C], oht[:, k % 2, s * P:(s + 1) * P],
                                      rowbuf[:, BT * k + s, 0:C], start=t == 0, stop=t == 1)
                        last.then_inc(grp_mm, 1)

            with pe.Fori(0, 16) as i:
                pe.wait_ge(cnt_ready, i + 1)
                mm(ps[:, 0, 0:3], ones_b[:, :], cntb[:, :], start=True, stop=True).then_inc(cnt_mm, 1)
            pe.wait_ge(final_cnt, 1)
            mm(ps[:, 0, 0:NT], ones_b[:, :], ohb[:, 0, 0:NT], start=True, stop=True)
            mm(ps[:, 1, 0:NT], ones_b[:, :], ohb[:, 1, 0:NT], start=True, stop=True)
            mm(ps[:, 2, 0:NT], before[:, :], ohb[:, 1, 0:NT], start=True, stop=True).then_inc(final_mm, 1)

            pe.wait_ge(fw_in, 32)
            pe.wait_ge(x3_ready, 1)

            def ffn(i, s, first=False):
                pe.wait_ge(x3_ready, 2 * (i + 1))
                pe.wait_ge(x3T_ready, i + 1)
                for c in range(CC):
                    for u in range(2):
                        last = tp(ps[:, 0, (2 * c + u) * P:(2 * c + u + 1) * P],
                                  x3[:, s, u * C + c * P:u * C + (c + 1) * P], ident[:, :])
                last.then_inc(x3T_mm, 1)
                pe.wait_ge(x3T_ready, XT0 + i + 1)
                for m in range(HID // P):
                    pe.wait_ge(fh_ready, 8 * i + m + 1)
                    for c in range(CC):
                        last = mm(ps[:, 2 + m % 2, 0:C], fw1_s[:, c, m * P:(m + 1) * P],
                                  x3T[:, s, c * 2 * P:(c + 1) * 2 * P], start=c == 0, stop=c == CC - 1)
                    last.then_inc(fh_mm, 1)
                pe.wait_ge(fh_ready, FH0 + 8 * (i + 1))
                if not first:
                    pe.wait_ge(o_ready, i - 1)
                for u in range(2):
                    for m in range(HID // P):
                        mm(ps[:, 4 + s, u * C:(u + 1) * C], fhT[:, s, m, u * P:(u + 1) * P], fw2_s[:, m, :],
                           start=m == 0, stop=False)
                    last = mm(ps[:, 4 + s, u * C:(u + 1) * C], onesf[0:1, :], vec[0:1, FB2, :], start=False,
                              stop=True)
                last.then_inc(fy_mm, 1)

            ffn(0, 0, first=True)
            ffn(1, 1, first=True)
            with pe.Fori(1, NT // 4) as i:
                ffn(2 * i, 0)
                ffn(2 * i + 1, 1)
            ffn(NT // 2 - 1, 0)

        @block.scalar
        def _(act):
            A = nc.scalar.activation
            act.sem_inc(xnT_ready, XNT0)
            act.sem_inc(sup_ready, SUP0)
            act.sem_inc(row_ready, ROW0)
            act.sem_inc(elu_a, ELUA0)
            act.sem_inc(x3T_ready, XT0)
            act.sem_inc(fh_ready, FH0)
            act.sem_inc(sums_ready, SUM0)
            outs = [wqkvT[:, 0, 0:512], wqkvT[:, 0, 512:768], wqkvT[:, 1, 0:512], wqkvT[:, 1, 512:768],
                    w1T[:, :, :].rearrange("p c o -> p (c o)"), w2T[:, :, :].rearrange("p c o -> p (c o)")]
            for tab in (bkt_t, ws_t[:, :, 1], ws_t[:, :, 0], dst_t):
                for q in range(4):
                    outs.append(tab[:, 4 * q * P:min(4 * q + 4, EJ) * P])
            for job, o in enumerate(outs):
                act.wait_ge(tab_mm, job + 1)
                A(o, ps[:, job % 8, 0:o.shape[1]], ACT.Copy).then_inc(tab_read, 1)
            with act.Fori(0, NG // 2) as i:
                for n in range(2 * G):
                    s, t = n // G, n % G
                    tile = 2 * G * i + n
                    act.wait_ge(tr_mm, tile + 1)
                    A(xnT_g[s][:, t, :], ps[:, 4 + n % 2, 0:C], ACT.Copy).then_inc(xnT_ready, 1)
                    act.wait_ge(sup_mm, tile + 1)
                    A(sup_g[s][:, t, :], ps[:, 6 + n % 2, 0:C], ACT.Copy).then_inc(sup_ready, 1)

            def rows(i, k):
                b = KB * i + k
                act.wait_ge(rows_left, b + 1)
                for h in range(2):
                    act.wait_ge(main_mm, MAIN0 + 2 * b + h + 1)
                    s = BT * k + 2 * h
                    A(rowbuf[:, s:s + 2, 0:C], ps[:, MSG + h, :].rearrange("p (t c) -> p t c", t=2),
                      ACT.Copy).then_inc(row_ready, 1)
                A(rowbuf[:, BT * k:BT * (k + 1), C:RW], ws_t[:, ds(BT * b, BT), :], ACT.Copy).then_inc(ws_ready, 1)

            def elu_parts(i, u):
                n = 2 * i + u
                act.wait_ge(elu_v, 3 * n + 3)
                act.wait_ge(q_mm, n + 1)
                A(eq[:, u, :], ps[:, QPS, u * C:(u + 1) * C], ACT.Exp).then_inc(elu_a, 1)
                A(rq[:, u, :], ps[:, QPS, u * C:(u + 1) * C], ACT.Relu).then_inc(elu_a, 1)
                act.wait_ge(kv_mm, n + 1)
                A(ek[:, u, :], ps[:, KVPS + u, 0:C], ACT.Exp).then_inc(elu_a, 1)
                A(rk[:, u, :], ps[:, KVPS + u, 0:C], ACT.Relu).then_inc(elu_a, 1)
                act.wait_ge(kv_acc, n + 1)
                A(vext[:, u, :, 0:P], ps[:, KVPS + u, C:2 * C].rearrange("p (c f) -> p c f", c=CC), ACT.Copy,
                  scale=maskc[:, ds(n, 1)]).then_inc(elu_a, 1)

            act.wait_ge(consts, 5)
            for s in range(2):
                act.wait_ge(xg_out[s], 48 * (NG // 2))
            with act.Fori(0, NT // 2) as i:
                rows(i, 0)
                elu_parts(i, 0)
                rows(i, 1)
                elu_parts(i, 1)
                rows(i, 2)
                rows(i, 3)
            act.wait_ge(w_in, 16 * 12)

            def make_oht(i, k):
                b = KB * i + k
                act.wait_ge(relb_mm, b + 1)
                act.wait_ge(main_mm, 2 * b + 6)
                A(oht[:, k % 2, :], ps[:, RELB, :], ACT.Abs, bias=minus_lane[:, :]).then_inc(abs_done, 1)
                act.wait_ge(abs_done, b - KB * (NT // 2))
                A(oht[:, k % 2, :], oht[:, k % 2, :], ACT.Relu, bias=one[:, :], scale=-1.0).then_inc(oht_ready, 1)

            def mix_step(i, front, back):
                e = NT // 2 + i
                if back:
                    act.wait_ge(h_mm, i)
                    for m in range(CC):
                        A(hT[:, m, :], ps[:, HPS, m * C:(m + 1) * C], ACT.Gelu,
                          bias=b1_c[:, m:m + 1]).then_inc(h_ready, 1)
                for k in range(KB):
                    make_oht(*((e, k + 1) if k + 1 < KB else (e + 1, 0)))
                    rows(e, k)
                if front:
                    act.wait_ge(x1T_mm, i + 1)
                    A(x1T.rearrange("p c r -> p (c r)"), ps[:, XTPS, :], ACT.Copy).then_inc(x1T_ready, 1)

            mix_step(0, True, False)
            A(spare[:, :], one[:, :], ACT.Gelu).then_inc(passed, 1)
            with act.Fori(1, NT // 2) as i:
                mix_step(i, True, True)
            mix_step(NT // 2, False, True)
            with act.Fori(2 * (NT // 2) + 1, EQ) as i:
                for k in range(KB):
                    rows(i, k)

            def ffn(i, s):
                act.wait_ge(x3T_mm, i + 1)
                A(x3T[:, s, :], ps[:, 0, :], ACT.Copy).then_inc(x3T_ready, 1)
                for m in range(HID // P):
                    act.wait_ge(fh_mm, 8 * i + m + 1)
                    A(fhT[:, s, m, :], ps[:, 2 + m % 2, 0:C], ACT.Gelu_apprx_tanh,
                      bias=fb1_c[:, m:m + 1]).then_inc(fh_ready, 1)

            act.wait_ge(mix_done, MIX0 + NT // 2)
            steps = act.value_load(meta[0:1, 1:2], min_val=1, max_val=NGMAX // RG + 1)
            with act.Fori(0, steps) as i:
                for k in range(KB):
                    act.wait_ge(grp_mm, GRP0 + RG * i + 2 * k + 2)
                    act.wait_ge(acc_done, RG * i + 2 * k + 2)
                    A(sums[:, k, :], ps[:, GRP + k, :], ACT.Copy).then_inc(sums_ready, 1)

            act.wait_ge(grp_mm, GRP0 + RG * steps)
            ffn(0, 0)
            ffn(1, 1)
            with act.Fori(1, NT // 4) as i:
                for s in range(2):
                    act.wait_ge(fy_mm, 2 * i + s - 1)
                    ffn(2 * i + s, s)
            act.wait_ge(fy_mm, NT // 2 - 2)
            ffn(NT // 2 - 1, 0)

        @block.vector
        def _(dve):
            v = nc.vector
            chain = Chain(dve, dstep)
            v_link = chain.link

            def newton(var, y, t):
                v_link(v.tensor_scalar(t.bitcast(I32), var.bitcast(I32), 1, None, ALU.logical_shift_right))
                v_link(v.tensor_scalar(y.bitcast(I32), t.bitcast(I32), -1.0, 1597463007.0, ALU.mult, ALU.add))
                for _ in range(3):
                    v_link(v.scalar_tensor_tensor(t, y, -0.5, y, ALU.mult, ALU.mult))
                    v_link(v.tensor_tensor(t, t, var, ALU.mult))
                    v_link(v.scalar_tensor_tensor(y, t, 1.5, y, ALU.add, ALU.mult))

            dve.wait_ge(iotas, 8)
            v.tensor_scalar(ident[:, :], cols[:, :], lane[:, 0:1], None, ALU.is_equal).then_inc(consts, 1)
            v.tensor_scalar(ident_h[:, :], cols[:, :], lane[:, 0:1], None, ALU.is_equal).then_inc(consts, 1)
            v.tensor_scalar(ident_hi[:, :], cols[:, :], lane[:, 0:1], float(LOW), ALU.is_equal,
                            ALU.mult).then_inc(consts, 1)
            v.tensor_scalar(before[:, :], cols[:, :], lane[:, 0:1], None, ALU.is_gt).then_inc(consts, 1)
            v.tensor_scalar(maskc[:, NT - 1:NT], lane[:, 0:1], float(LASTROWS), None, ALU.is_lt).then_inc(consts, 1)
            units = newt[:, 2, 0:96].bitcast(I32).rearrange("p (a b) -> p a b", b=6)
            for k, unit in enumerate((1, 2, 3, 1, 3, 1)):
                v_link(v.memset(units[:, :, k], unit))
            v_link(v.tensor_tensor(bits[:, :, :], units, bits[:, :, :], ALU.logical_shift_left))
            v_link(v.tensor_scalar(minus_lane[:, :], lane[:, :], -1.0, None, ALU.mult))
            v_link(v.memset(one[:, :], 1.0))
            v_link(v.memset(onecol[:, :], 0.0))
            v_link(v.memset(onecol[:, EQ - 1:EQ], 1.0))
            v.sem_inc(oht_ready, OHT0)
            v.sem_inc(elu_v, ELUV0)
            v.sem_inc(rank_read, RREAD0)
            v.sem_inc(mix_done, MIX0)
            v.sem_inc(t_read, TREAD0)

            dve.wait_ge(raw_in, 64)
            si = rsrc.bitcast(I32)
            v.tensor_scalar(fbkt.bitcast(I32), si, 7, None, ALU.logical_shift_right).then_inc(raw_ready, 1)
            dve.wait_ge(raw_ready, 1)
            v.tensor_copy(fbkt, fbkt.bitcast(I32)).then_inc(raw_ready, 1)
            v.tensor_scalar(floc.bitcast(I32), si, P - 1, None, ALU.bitwise_and).then_inc(raw_ready, 1)
            dve.wait_ge(raw_ready, 3)
            v.tensor_copy(floc, floc.bitcast(I32)).then_inc(raw_ready, 1)
            v.tensor_copy(fdst, rdst.bitcast(I32)).then_inc(raw_ready, 1)
            rr = rrel[0:EQ, :].bitcast(I32).rearrange("p (k e) -> p k e", k=KB)
            v_link(v.tensor_tensor(rel[:, :].rearrange("p (k e) -> p k e", k=KB), rr,
                                   rr[:, :, 0:1].to_broadcast([EQ, KB, BE]), ALU.subtract))
            chain.inc(v.tensor_reduce(tk[0:EQ, 1:2], rel[:, :], AX.X, ALU.max))
            chain.inc(v.tensor_reduce(tk[0:EQ, 2:3], rel[:, :], AX.X, ALU.min))
            chain.wait()
            v_link(v.tensor_scalar(tk[0:EQ, 1:2], tk[0:EQ, 1:2], float(P - 1), None, ALU.is_gt))
            v_link(v.tensor_scalar(tk[0:EQ, 2:3], tk[0:EQ, 2:3], 0.0, None, ALU.is_lt))
            v.tensor_tensor(tk[0:EQ, 0:1], tk[0:EQ, 1:2], tk[0:EQ, 2:3], ALU.max).then_inc(viol_ready, 1)

            bidx = cols[:, 0:NT].unsqueeze(1).to_broadcast([P, BT, NT])

            def one_hot(b, k):
                return v.tensor_tensor(ohb[:, k, :].rearrange("p (t n) -> p t n", t=BT),
                                       bkt_t[:, ds(BT * b, BT)].unsqueeze(2).to_broadcast([P, BT, NT]), bidx,
                                       ALU.is_equal)

            dve.wait_ge(tab_read, TAB)
            for k in range(KB):
                one_hot(k, k).then_inc(hist_oh, 1)
            with dve.Fori(1, EQ) as i:
                for k in range(KB):
                    dve.wait_ge(hist_mm, KB * (i - 1) + k + 1)
                    one_hot(KB * i + k, k).then_inc(hist_oh, 1)

            dve.wait_ge(hist_mm, NB + 1)
            base4 = offs[:, 0, :].rearrange("p (t n) -> p t n", t=BT)
            h4 = offs[:, 8, :].rearrange("p (t n) -> p t n", t=BT)
            tot, grp, cs, cs2 = (offs[:, 2 + k, 0:NT] for k in range(4))
            v_link(v.tensor_scalar(beforef, cols[:, :], lane[:, 0:1], None, ALU.is_gt))
            v_link(v.tensor_copy(offs[0:EQ, 1, :], ps[0:EQ, RANK, 0:BT * NT]))
            v.sem_inc(base_ready, 1)
            dve.wait_ge(base_mm, 1)
            v_link(v.tensor_copy(offs[:, 8, :], ps[:, 1, 0:BT * NT]))
            v_link(v.tensor_tensor(tot, h4[:, 0, :], h4[:, 1, :], ALU.add))
            for t in range(2, BT):
                v_link(v.tensor_tensor(tot, tot, h4[:, t, :], ALU.add))
            v_link(v.tensor_scalar(grp.bitcast(I32), tot, float(GS - 1), None, ALU.add))
            v_link(v.tensor_scalar(grp.bitcast(I32), grp.bitcast(I32), 8, None, ALU.logical_shift_right))
            v_link(v.tensor_copy(grp, grp.bitcast(I32)))
            v_link(v.tensor_copy(cs, grp))
            a, b_, d = cs, cs2, 1
            while d < NT:
                v_link(v.tensor_copy(b_[:, 0:d], a[:, 0:d]))
                v_link(v.tensor_tensor(b_[:, d:NT], a[:, d:NT], a[:, 0:NT - d], ALU.add))
                a, b_, d = b_, a, 2 * d
            cs = a
            v_link(v.tensor_tensor(b_, cs, grp, ALU.subtract))
            v_link(v.tensor_scalar(base4[:, 0, :], b_, float(GS), float(GS), ALU.mult, ALU.add))
            for t in range(1, BT):
                v_link(v.tensor_tensor(base4[:, t, :], base4[:, t - 1, :], h4[:, t - 1, :], ALU.add))
            first, fpart = offs[0:EQ, 9, :].bitcast(I32), offs[0:EQ, 10, :].bitcast(I32)
            v_link(v.tensor_tensor(first, ps[0:EQ, 2, 0:BT * NT], offs[0:EQ, 0, :], ALU.add))
            v_link(v.tensor_scalar(fpart, first, LOW - 1, None, ALU.bitwise_and))
            v_link(v.tensor_copy(first_lo[:, :], fpart))
            v_link(v.tensor_scalar(fpart, first, 11, None, ALU.logical_shift_right))
            v_link(v.tensor_copy(first_hi[:, :], fpart))
            v_link(v.tensor_scalar(tk[:, 3:4], cs[:, NT - 1:NT], float(GS), float(GS), ALU.mult, ALU.add))
            v_link(v.tensor_scalar(pf_row[:, 0:NT], cs[0:1, :], float(GS), None, ALU.mult))
            v_link(v.tensor_scalar(pf_row[:, NT:], cols[0:1, 0:RG - 1], float(GS), tk[0:1, 3:4], ALU.mult, ALU.add))
            v_link(v.tensor_copy(meta[:, 0:1], cs[:, NT - 1:NT]))
            v_link(v.tensor_scalar(meta[:, 1:2], cs[:, NT - 1:NT], float(RG - 1), None, ALU.add))
            v_link(v.tensor_scalar(meta[:, 1:2], meta[:, 1:2], 3, None, ALU.logical_shift_right))
            v.sem_inc(meta_ready, 1)
            dve.wait_ge(viol_mm, 1)
            v.tensor_copy(meta[0:1, 2:3], ps[0:1, 3, 0:1]).then_inc(flag_ready, 1)
            gcol = offs[:, 6, 0:GJ]
            v_link(v.tensor_scalar(gcol, cols[:, 0:GJ], float(P), lane[:, 0:1], ALU.mult, ALU.add))
            v_link(v.tensor_tensor(bcmp, cs.unsqueeze(1).to_broadcast([P, GJ, NT]),
                                   gcol.unsqueeze(2).to_broadcast([P, GJ, NT]), ALU.is_lt))
            v_link(v.tensor_reduce(offs[:, 7, 0:GJ], bcmp, AX.X, ALU.add))
            v_link(v.tensor_scalar(gb_pj, offs[:, 7, 0:GJ], float(NT - 1), float(C), ALU.min, ALU.mult))
            v.sem_inc(gb_ready, 1)

            with dve.Fori(0, NG // 2) as i:
                chain.enter(i, 2 * (2 * G + 1 + NEWTON))
                for s in range(2):
                    dve.wait_ge(xg_in[s], 32 * (i + 1))
                    for t in range(G):
                        chain.inc(v.bn_stats(stats[:, t, :], x_g[s][:, t, :]))
                    chain.wait()
                    dve.sem_inc(passed, 1)
                    for t in range(G):
                        chain.inc(v.bn_aggr(mvs[:, t, :], stats[:, t, :]))
                    chain.wait()
                    v_link(v.tensor_scalar(newt[:, 1, 0:G], mvs[:, :, 1], EPS_LN, None, ALU.add))
                    newton(newt[:, 1, 0:G], rs[:, :], newt[:, 0, 0:G])
                    for t in range(G):
                        v.tensor_scalar(x_g[s][:, t, :], x_g[s][:, t, :], mvs[:, t, 0:1], rs[:, t:t + 1],
                                        ALU.subtract, ALU.mult).then_inc(xn_ready, 1)
                    dve.wait_ge(xn_ready, 2 * G * i + G * (s + 1))
            chain.leave(NG // 2)

            def make_oht(i, k):
                b = KB * i + k
                dve.wait_ge(relb_mm, b + 1)
                dve.wait_ge(main_mm, 2 * b + 6)
                v.tensor_scalar(oht[:, k % 2, :], ps[:, RELB, :], lane[:, 0:1], None,
                                ALU.is_equal).then_inc(oht_ready, 1)

            def make_ohb(i, k):
                dve.wait_ge(rank_mm, RANK0 + KB * i)
                one_hot(KB * i + k, k).then_inc(oh_ready, 1)

            def edges(i, k, more=True, oht_made=False):
                b = KB * i + k
                after = (i, k + 1) if k + 1 < KB else (i + 1, 0)
                if more and not oht_made:
                    make_oht(*after)
                dve.wait_ge(rank_mm, RANK0 + b + 1)
                dve.wait_ge(oh_ready, b + 1)
                for t in range(BT):
                    q = slice(t * NT, (t + 1) * NT)
                    v.tensor_tensor_reduce(out=scr[:, q], in0=ps[:, RANK, q], in1=ohb[:, k, q], scale=1.0, scalar=0.0,
                                           op0=ALU.mult, op1=ALU.add,
                                           accum_out=posf[:, BT * k + t:BT * k + t + 1]).then_inc(rank_read, 1)
                if more:
                    make_ohb(*after)
                dve.wait_ge(rows_left, b + 1)
                dve.wait_ge(rank_read, RREAD0 + BT * (b + 1))
                v.tensor_copy(posu[:, BT * k:BT * (k + 1)], posf[:, BT * k:BT * (k + 1)]).then_inc(pos_ready, 1)

            def elu(i, u):
                n = 2 * i + u
                dve.wait_ge(kv_acc, n + 1)
                v.tensor_copy(vext[:, u, :, P:P + 1],
                              maskc[:, ds(n, 1)].unsqueeze(1).to_broadcast([P, CC, 1])).then_inc(elu_v, 1)
                dve.wait_ge(elu_a, ELUA0 + 5 * n + 2)
                dve.wait_ge(q_free, i + 1)
                v.scalar_tensor_tensor(qTb[:, u, :], eq[:, u, :], 1.0, rq[:, u, :], ALU.min,
                                       ALU.add).then_inc(elu_v, 1)
                dve.wait_ge(elu_a, ELUA0 + 5 * n + 4)
                v.scalar_tensor_tensor(kk[:, u, :], ek[:, u, :], 1.0, rk[:, u, :], ALU.min,
                                       ALU.add).then_inc(elu_v, 1)

            for s in range(2):
                dve.wait_ge(xg_out[s], 48 * (NG // 2))
            make_oht(0, 0)
            make_ohb(0, 0)
            with dve.Fori(0, NT // 2) as i:
                edges(i, 0)
                edges(i, 1)
                elu(i, 0)
                edges(i, 2)
                elu(i, 1)
                edges(i, 3)

            dve.wait_ge(kv_acc, KVACC0 + NT + 1)
            for c in range(CC):
                for h in range(4):
                    q = slice(32 * h, 32 * h + 32)
                    chain.inc(v.tensor_copy(kvb[q, c, 32 * h:32 * h + 32],
                                            ps[q, KVA, c * (P + 1) + 32 * h:c * (P + 1) + 32 * h + 32]))
                    chain.inc(v.tensor_copy(kvb[q, c, P + h:P + h + 1],
                                            ps[q, KVA, c * (P + 1) + P:c * (P + 1) + P + 1]))
            chain.wait()
            v.sem_inc(kvb_ready, 1)
            dve.wait_ge(w_in, 16 * 12)
            dve.wait_ge(q_out, 16 * (NT // 2))

            def norm_stats(a, src2):
                for u in range(2):
                    chain.inc(v.bn_stats(stats[:, a + u, :], src2[:, u, :]))
                chain.wait()
                dve.sem_inc(passed, 1)
                for u in range(2):
                    chain.inc(v.bn_aggr(mvs[:, a + u, :], stats[:, a + u, :]))
                chain.wait()

            def norm_factors(a, n):
                v_link(v.tensor_scalar(newt[:, 1, a:a + n], mvs[:, a:a + n, 1], EPS_LN, None, ALU.add))
                newton(newt[:, 1, a:a + n], rs[:, a:a + n], newt[:, 0, a:a + n])

            def norm_apply(a, src2, out2, g_, b_, done):
                for u in range(2):
                    chain.inc(v.scalar_tensor_tensor(out2[:, u, :], src2[:, u, :], mvs[:, a + u, 0:1], vec[:, g_, :],
                                                     ALU.subtract, ALU.mult))
                chain.wait()
                for u in range(2):
                    done(v.scalar_tensor_tensor(out2[:, u, :], out2[:, u, :], rs[:, a + u:a + u + 1], vec[:, b_, :],
                                                ALU.mult, ALU.add))

            FRONT, BACK = 0, 2

            def attention(i):
                dve.wait_ge(t_mm, i + 1)
                den = ps[:, TPS:TPS + 2, 0:CC * (P + 4)].rearrange("p u (c f) -> p u c f", c=CC)
                for u in range(2):
                    chain.inc(v.tensor_scalar(rz[:, 8 * u:8 * u + 8].rearrange("p (c h) -> p c h", c=CC),
                                              den[:, u, :, P:P + 4], EPS_ATTN, None, ALU.add))
                chain.wait()
                v_link(v.reciprocal(rz[:, :], rz[:, :]))
                for u in range(2):
                    v.tensor_tensor(
                        tmp[:, u, :].rearrange("p (c h d) -> p c h d", c=CC, d=32),
                        den[:, u, :, 0:P].rearrange("p c (h d) -> p c h d", d=32),
                        rz[:, 8 * u:8 * u + 8].rearrange("p (c h) -> p c h", c=CC).unsqueeze(3).to_broadcast(
                            [P, CC, 4, 32]), ALU.mult).then_inc(t_read, 1)
                dve.wait_ge(t_read, TREAD0 + 2 * (i + 1))
                v.tensor_tensor(tmp, tmp, xnb, ALU.add).then_inc(xnb_read, 1)
                dve.wait_ge(xnb_read, i + 1)
                norm_stats(FRONT, tmp)

            def first_norm(i):
                norm_apply(FRONT, tmp, x1, LN1G, LN1B, lambda ins: ins.then_inc(x1_ready, 1))

            def residual(i):
                dve.wait_ge(y_mm, i + 1)
                dve.wait_ge(x1_ready, 2 * (i + 1))
                v_link(v.tensor_tensor(y2, ps[:, YPS, :].rearrange("p (u c) -> p u c", u=2), x1, ALU.add))
                norm_stats(BACK, y2)

            def second_norm(i):
                norm_apply(BACK, y2, y2, LN2G, LN2B, chain.inc)
                chain.wait()
                dve.wait_ge(x_in, 32 * (i + 1))
                v.tensor_tensor(acc[:, ds(2 * C * i, 2 * C)].rearrange("p (u c) -> p u c", u=2), y2, xb,
                                ALU.add).then_inc(mix_done, 1)

            def mix_step(i, front, back):
                e = NT // 2 + i
                edges(e, 0, oht_made=True)
                if front:
                    attention(i)
                edges(e, 1, oht_made=True)
                if back:
                    residual(i - 1)
                norm_factors(FRONT if front else BACK, 2 * (front + back))
                edges(e, 2, oht_made=True)
                if front:
                    first_norm(i)
                edges(e, 3, oht_made=True)
                if back:
                    second_norm(i - 1)

            mix_step(0, True, False)
            with dve.Fori(1, NT // 2) as i:
                chain.enter(i - 1, (3 + 4) + (1 + 4) + (1 + NEWTON) + 2 + 4)
                mix_step(i, True, True)
            chain.leave(NT // 2 - 1)
            mix_step(NT // 2, False, True)
            with dve.Fori(2 * (NT // 2) + 1, EQ - 1) as i:
                for k in range(KB):
                    edges(i, k)
            for k in range(KB):
                edges(EQ - 1, k, more=k + 1 < KB)

            dve.wait_ge(main_mm, MAIN0 + 2 * NB)
            steps = dve.value_load(meta[0:1, 1:2], min_val=1, max_val=NGMAX // RG + 1)

            with dve.Fori(0, steps) as i:
                for k in range(KB):
                    dve.wait_ge(r_in[k], 16 * (i + 1))
                    dve.wait_ge(grp_mm, RG * i + 2 * k + 6)
                    for s in range(BT):
                        r = BT * k + s
                        v.tensor_scalar(oht[:, k % 2, s * P:(s + 1) * P], cols[:, :], rowbuf[:, r, C + 1:C + 2],
                                        rowbuf[:, r, C:C + 1], ALU.is_equal, ALU.mult).then_inc(ohw_ready, 1)
            dve.wait_ge(acc_done, ACC0 + RG * steps)
            dve.sem_inc(passed, 1)

            with dve.Fori(0, NG) as i:
                chain.enter(i, 2 * G + 1)
                for t in range(G):
                    chain.inc(v.bn_stats(stats[:, t, :], acc[:, ds(i * GC + t * C, C)]))
                chain.wait()
                dve.sem_inc(passed, 1)
                for t in range(G):
                    chain.inc(v.bn_aggr(mvs[:, t, :], stats[:, t, :]))
                chain.wait()
                v_link(v.tensor_copy(mv[:, ds(G * i, G), :], mvs[:, :, :]))
            chain.leave(NG)
            v_link(v.tensor_scalar(newt[:, 1, :], mv[:, :, 1], EPS_LN, None, ALU.add))
            newton(newt[:, 1, :], rstd[:, :], newt[:, 0, :])

            def normed(out, col, tile):
                return v.tensor_scalar(out, acc[:, ds(col, C)], mv[:, ds(tile, 1), 0], rstd[:, ds(tile, 1)],
                                       ALU.subtract, ALU.mult)

            with dve.Fori(0, NG) as i:
                chain.enter(i, 2 * G + 1)
                for t in range(G):
                    chain.inc(normed(node[:, t * C:(t + 1) * C], i * GC + t * C, G * i + t))
                chain.wait()
                for t in range(G):
                    chain.inc(v.tensor_tensor_reduce(out=node[:, (G + t) * C:(G + t + 1) * C],
                                                     in0=node[:, t * C:(t + 1) * C], in1=vec[:, WR, :], scale=1.0,
                                                     scalar=0.0, op0=ALU.mult, op1=ALU.add,
                                                     accum_out=wcol[:, t:t + 1]))
                chain.wait()
                v_link(v.tensor_scalar(wts[:, ds(G * i, G)], wcol[:, :], br_c[:, 0:1], None, ALU.add))
            chain.leave(NG)

            wm, pen, hit = scr[:, 0:NT], scr[:, NT:2 * NT], scr[:, 2 * NT:3 * NT]
            v_link(v.tensor_scalar(pen, maskc[:, :], -1.0, 3.0e38, ALU.add, ALU.mult))
            v_link(v.tensor_tensor(wm, wts[:, :], maskc[:, :], ALU.mult))
            v_link(v.tensor_tensor(wm, wm, pen, ALU.add))
            key, taken = tki[:, 0:1], tki[:, 1:2]
            v_link(v.memset(key, 0))
            hits = node[:, 0:3 * NT].rearrange("p (k n) -> p k n", k=3)

            def decode(c, sign, thr):
                v_link(v.tensor_scalar(sign, c, 31, None, ALU.arith_shift_right))
                v_link(v.tensor_scalar(sign, sign, -1, SIGN, ALU.bitwise_xor, ALU.bitwise_or))
                v_link(v.tensor_tensor(thr, c, sign, ALU.bitwise_xor))

            with dve.Fori(0, 16) as i:
                chain.enter(i, 12)
                pair = bits[:, ds(15 - i, 1), 0:3].rearrange("p a k -> p (a k)")
                turn = bits[:, ds(15 - i, 1), 3:6].rearrange("p a k -> p (a k)")
                v_link(v.tensor_tensor(candi[:, 0, :], key.to_broadcast([P, 3]), pair, ALU.bitwise_or))
                decode(candi[:, 0, :], candi[:, 1, :], candi[:, 2, :])
                for k in range(3):
                    chain.inc(v.tensor_scalar(hits[:, k, :], wm, cands[:, 2, k:k + 1], None, ALU.is_ge))
                chain.wait()
                with nc.allow_low_precision("counts below 128"):
                    v.tensor_reduce(cntb[:, :], hits, AX.X, ALU.add).then_inc(cnt_ready, 1)
                dve.wait_ge(cnt_mm, i + 1)
                v_link(v.tensor_scalar(candi[:, 3, :], ps[:, 0, 0:3], float(KEEP), -1.0, ALU.is_ge, ALU.mult))
                v_link(v.tensor_tensor(candi[:, 3, :], candi[:, 3, :], turn, ALU.bitwise_and))
                for k in range(3):
                    v_link(v.tensor_tensor(key, key, candi[:, 3, k:k + 1], ALU.bitwise_xor))
            chain.leave(16)
            decode(key, taken, tki[:, 3:4])
            gt, eqm = ohb[:, 0, 0:NT], ohb[:, 1, 0:NT]
            v_link(v.tensor_scalar(gt, wm, tk[:, 3:4], None, ALU.is_gt))
            v.tensor_scalar(eqm, wm, tk[:, 3:4], None, ALU.is_equal).then_inc(final_cnt, 1)
            dve.wait_ge(final_mm, 1)
            v_link(v.tensor_reduce(tk[:, 4:5], ps[:, 0, 0:NT], AX.X, ALU.add))
            v_link(v.tensor_scalar(tk[:, 4:5], tk[:, 4:5], -1.0, float(KEEP), ALU.mult, ALU.add))
            a, b_, d = scr[:, NT:2 * NT], scr[:, 2 * NT:3 * NT], 1
            e0 = scr[:, 3 * NT:4 * NT]
            v_link(v.tensor_copy(e0, ps[:, 1, 0:NT]))
            v_link(v.tensor_copy(a, e0))
            while d < NT:
                v_link(v.tensor_copy(b_[:, 0:d], a[:, 0:d]))
                v_link(v.tensor_tensor(b_[:, d:NT], a[:, d:NT], a[:, 0:NT - d], ALU.add))
                a, b_, d = b_, a, 2 * d
            v_link(v.tensor_tensor(a, a, e0, ALU.subtract))
            v_link(v.tensor_tensor(a, a, ps[:, 2, 0:NT], ALU.add))
            v_link(v.tensor_scalar(a, a, tk[:, 4:5], None, ALU.is_lt))
            v_link(v.tensor_tensor(a, a, eqm, ALU.mult))
            v_link(v.tensor_tensor(a, a, gt, ALU.add))
            v_link(v.tensor_tensor(wts[:, :], wts[:, :], a, ALU.mult))

            def ffn_in(i, s):
                for u in range(2):
                    normed(x3[:, s, u * C:(u + 1) * C], 2 * i * C + u * C, 2 * i + u).then_inc(x3_ready, 1)

            def ffn_out(i, s):
                dve.wait_ge(fy_mm, i + 1)
                dve.wait_ge(x3_ready, 2 * (i + 1))
                for u in range(2):
                    chain.inc(v.scalar_tensor_tensor(fo[:, s, u * C:(u + 1) * C], ps[:, 4 + s, u * C:(u + 1) * C],
                                                     wts[:, ds(2 * i + u, 1)], x3[:, s, u * C:(u + 1) * C],
                                                     ALU.mult, ALU.add))
                chain.wait()
                v.tensor_tensor(fo[:, s, :], fo[:, s, :], acc[:, ds(2 * i * C, 2 * C)], ALU.add).then_inc(o_ready, 1)

            def ffn_step(i, then):
                for s in range(2):
                    dve.wait_ge(fo_free, 2 * i + s + 1)
                    ffn_out(2 * i + s, s)
                    if s < then:
                        ffn_in(2 * i + 2 + s, s)

            ffn_in(0, 0)
            ffn_in(1, 1)
            with dve.Fori(0, NT // 4 - 1) as i:
                chain.enter(i, 4)
                ffn_step(i, 2)
            chain.leave(NT // 4 - 1)
            ffn_step(NT // 4 - 1, 1)
            dve.wait_ge(fo_free, 2 * (NT // 4) + 1)
            ffn_out(NT // 2 - 1, 0)


class Chain:

    def __init__(self, eng, sem):
        self.eng, self.sem, self.n, self.i = eng, sem, 0, None

    def inc(self, ins):
        ins.then_inc(self.sem, 1)
        self.n += 1

    def enter(self, i, per):
        self.before, self.n, self.i, self.per = self.n, 0, i, per

    def leave(self, count):
        assert self.n == self.per, (self.n, self.per)
        self.n, self.i = self.before + count * self.per, None

    def wait(self):
        at = self.n if self.i is None else self.before + self.i * self.per + self.n
        self.eng.wait_ge(self.sem, at)

    def link(self, ins):
        self.inc(ins)
        self.wait()


_INS = ["x", "src", "dst", "edge_weight", "L0_gnn_weight", "L0_mix_Wqkv", "L0_mix_ln1_g", "L0_mix_ln1_b",
        "L0_mix_W1", "L0_mix_b1", "L0_mix_W2", "L0_mix_b2", "L0_mix_ln2_g", "L0_mix_ln2_b", "L0_ffn_wr",
        "L0_ffn_br", "L0_ffn_w1", "L0_ffn_b1", "L0_ffn_w2", "L0_ffn_b2"]


def kernel(**inputs):
    import numpy as _np
    import concourse.bacc as _bacc
    from concourse import mybir as _mybir
    from concourse.bass_utils import run_bass_kernel_spmd as _run

    nc = _bacc.Bacc("TRN2", target_bir_lowering=False, num_devices=1)
    arrays, args = {}, []
    for name in _INS:
        a = _np.ascontiguousarray(inputs[name])
        arrays[f"in_{name}"] = a
        args.append(nc.dram_tensor(f"in_{name}", a.shape, _mybir.dt.from_np(a.dtype), kind="ExternalInput").ap())
    args.append(nc.dram_tensor("out_rows", (N, C), _mybir.dt.float32, kind="ExternalOutput").ap())
    gps_layer_kernel(nc, *args)
    r = _run(nc, [arrays], core_ids=[0])
    return r.results[0]["out_rows"]
```

```python
import concourse.bass as bass
from concourse import mybir
from contextlib import ExitStack
import numpy as np

N, C, E, HEADS, HID, NQKV = 12500, 256, 212500, 8, 1024, 768
P = 128
CC = C // P
NT = (N + P - 1) // P
LASTROWS = N - (NT - 1) * P
KEEP = max(1, int(0.5 * N)) - 1
FP = -(-KEEP // (2 * P))
EPS_LN, EPS_ATTN = 1e-5, 1e-6

BT = 4
BE = BT * P
KB = 4
EQ = -(-E // (BE * KB))
NB = EQ * KB
ET = NB * BT
EJ = ET // P
EPAD = ET * P

GS = 256
RW = C + 2
RG = 8
NGMAX = (EPAD + NT * (GS - 1)) // GS
NGROUPS = 1 + NGMAX + RG + 1
GJ = -(-NGROUPS // P)

G = 7
NG = NT // G
CLEARS = (0, 39, 63, NT + RG - 1)


def gps_layer_kernel(nc, x, src, dst, edge_weight, gnn_w, wqkv, ln1_g, ln1_b, w1, b1, w2, b2,
                     ln2_g, ln2_b, wr, br, fw1, fb1, fw2, fb2, out):
    F32, BF16, F16, I32, U32 = (mybir.dt.float32, mybir.dt.bfloat16, mybir.dt.float16, mybir.dt.int32,
                                mybir.dt.uint32)
    ALU, ACT, AX = mybir.AluOpType, mybir.ActivationFunctionType, mybir.AxisListType
    ds = bass.ds
    SIGN = -2147483648
    LOW = 2048
    NEWTON = 2 + 3 * 3

    src_d = nc.dram_tensor("src_pad", [EPAD], I32).ap()
    dst_d = nc.dram_tensor("dst_pad", [EPAD], I32).ap()
    ew_d = nc.dram_tensor("weight_pad", [EPAD], F32).ap()
    xn_d = nc.dram_tensor("xn_rows", [NT * P, C], F32).ap()
    xnT_d = nc.dram_tensor("xn_transposed", [NT, P, C], F32).ap()
    sup_d = nc.dram_tensor("support_rows", [(NT + 1) * P, C], F32).ap()
    qT_d = nc.dram_tensor("q_transposed", [NT, P, C], F32).ap()
    rows_d = nc.dram_tensor("sorted_rows", [NGROUPS * GS, RW], F32).ap()
    gb_d = nc.dram_tensor("group_bucket", [GJ * P], I32).ap()

    with ExitStack() as ctx:
        def sb(name, shape, dt=F32):
            return ctx.enter_context(nc.sbuf_tensor(name, shape, dt))

        def sem(name):
            return ctx.enter_context(nc.semaphore(name))

        acc = sb("acc", [P, NT * C])
        tabs = sb("tabs", [P, 4 * ET])
        ws_t = tabs[:, 0:2 * ET].rearrange("p (t k) -> p t k", k=2)
        bkt_t = tabs[:, 2 * ET:3 * ET]
        dst_t = tabs[:, 3 * ET:4 * ET].bitcast(U32)
        fw1_s = tabs[:, 0:CC * HID].rearrange("p (c h) -> p c h", c=CC)
        fw2_s = tabs[:, CC * HID:2 * CC * HID].rearrange("p (k c) -> p k c", c=C)
        rel = sb("rel", [EQ, KB * BE], F16)
        d0_row = sb("d0_row", [1, NB], I32)
        wqkvT = sb("wqkvT", [P, CC, NQKV])
        gw_s = sb("gw_s", [P, CC, C])
        w1T = sb("w1T", [P, CC, C])
        w2T = sb("w2T", [P, CC, C])
        vec = sb("vec", [P, 7, C])
        LN1G, LN1B, LN2G, LN2B, B2, FB2, WR = range(7)
        b1_c = sb("b1_c", [P, CC])
        fb1_c = sb("fb1_c", [P, HID // P])
        br_c = sb("br_c", [P, 1])
        ident = sb("ident", [P, P])
        ident_h = sb("ident_h", [P, P], F16)
        ident_hi = sb("ident_hi", [P, P], F16)
        onecol = sb("onecol", [P, 2 * EQ], BF16)
        first_lo = sb("first_lo", [EQ, BT * NT], F16)
        first_hi = sb("first_hi", [EQ, BT * NT], F16)
        before = sb("before", [P, P], BF16)
        ones_b = sb("ones_b", [P, P], BF16)
        zeros_b = sb("zeros_b", [P, 512], BF16)
        onesf = sb("onesf", [P, P])
        lane = sb("lane", [P, 1])
        cols = sb("cols", [P, P])
        kvb = sb("kvb", [P, CC, P + 4])
        maskc = sb("maskc", [P, NT])
        meta = sb("meta", [P, 4], I32)
        gb_row = sb("gb_row", [1, GJ * P], I32)
        rowbuf = sb("rowbuf", [P, KB * BT, RW])
        oht = sb("oht", [P, 2, BE])
        win = sb("win", [P, KB, C])
        ohb = sb("ohb", [P, KB, BT * NT], BF16)
        posf = sb("posf", [P, KB * BT])
        posu = sb("posu", [P, KB * BT], U32)
        dsg = sb("dsg", [P, BT], U32)
        scr = sb("scr", [P, BT * NT])
        node = sb("node", [P, 14 * C])
        stats = sb("stats", [P, G, 6])
        mvs = sb("mvs", [P, G, 2])
        newt = sb("newt", [P, 3, NT])
        rs = sb("rs", [P, G])
        rz = sb("rz", [P, 2 * HEADS])
        wts = sb("wts", [P, NT])
        mv = sb("mv", [P, NT, 2])
        rstd = sb("rstd", [P, NT])
        tk = sb("tk", [P, 8])
        tki = tk[:, :].bitcast(I32)
        minus_lane = sb("minus_lane", [P, 1])
        one = sb("one", [P, 1])
        spare = sb("spare", [P, 1])
        idx = sb("idx", [P, NT])
        place = sb("place", [P, NT])
        idu = sb("idu", [P, 2, 2], U32)
        bits = sb("bits", [P, 16, 6], I32)
        cands = sb("cands", [P, 4, 3])
        candi = cands[:, :, :].bitcast(I32)
        cntb = sb("cntb", [P, 3], BF16)

        def part(at, *shape, of=acc):
            n = int(np.prod(shape))
            ap = of[:, at:at + n]
            if len(shape) == 1:
                return ap
            if len(shape) == 2:
                return ap.rearrange("p (a b) -> p a b", a=shape[0])
            return ap.rearrange("p (a b c) -> p a b c", a=shape[0], b=shape[1])

        GC = G * C
        x_g = [part(s * GC, G, C) for s in range(2)]
        xnT_g = [part((2 + s) * GC, G, C) for s in range(2)]
        sup_g = [part((4 + s) * GC, G, C) for s in range(2)]
        raw0 = 6 * GC
        rsrc, rdst, rew, fbkt, floc, fdst = (part(raw0 + k * ET, ET) for k in range(6))
        rrel = part(raw0 + 6 * ET, KB * BE)
        wraw = part(0, 10, C)
        offs = part(raw0, 16, BT * NT)
        bcmp = part(raw0 + 7000, GJ, NT)
        beforef = part(raw0 + 8000, P)
        xnT_b = [part(k * C, C) for k in range(2)]
        eq, rq, qTb, ek, rk, kk = (part((2 + 2 * k) * C, 2, C) for k in range(6))
        vext = part(14 * C, 2, CC, P + 1)
        qTm, xnb, xb, tmp, x1, x1T, hT = (part(2 * C * k, 2, C, of=node) for k in range(7))
        sums = part(0, KB, 2 * C, of=node)
        x3 = [part(s * GC, GC, of=node) for s in range(2)]
        prod = rowbuf[:, :, :].rearrange("p a b -> p (a b)")[:, 0:2 * GC].rearrange(
            "p (s t c) -> p s t c", s=2, t=G)
        x3T, fo, base, fy = (part(4 * C * k, 2, 2 * C) for k in range(4))
        xc = [part(16 * C + s * 2 * RW, 2, RW) for s in range(2)]
        y2 = wqkvT[:, 0, 0:2 * C].rearrange("p (u c) -> p u c", u=2)
        fhT = rowbuf[:, :, :].rearrange("p a b -> p (a b)")[:, 0:2 * 8 * 2 * P].rearrange(
            "p (s m r) -> p s m r", s=2, m=HID // P)
        zrow = node[:, 0:2 * RW]
        padi = node[0:1, 600:600 + EPAD - E].bitcast(I32)
        pf_row = node[0:1, 1200:1200 + NT + RG - 1].bitcast(I32)
        last_dst = node[0:1, 1420:1421].bitcast(I32)
        padj = node[0:1, 1500:1500 + EPAD - E].bitcast(I32)
        gb_pj = node[:, 1400:1400 + GJ].bitcast(I32)

        ps = ctx.enter_context(nc.psum_tensor("ps", [P, 8, 512], F32))
        RANK, RELB, MSG, KVA, QPS, KVPS = 0, 1, 2, 4, 5, 6
        TPS, XTPS, HPS, YPS = 4, 6, 7, 6
        GRP = 4

        (padsrc, padded, w_in, raw_in, wraw_in, d0_in, iotas, consts, dstep, pstep) = (sem(n) for n in (
            "padsrc", "padded", "w_in", "raw_in", "wraw_in", "d0_in", "iotas", "consts", "dstep", "pstep"))
        (raw_ready, tab_mm, tab_read, viol_ready, viol_mm, flag_ready) = (sem(n) for n in (
            "raw_ready", "tab_mm", "tab_read", "viol_ready", "viol_mm", "flag_ready"))
        (hist_oh, hist_mm, base_ready, base_mm, meta_ready, gb_ready, gb_out, gb_in) = (sem(n) for n in (
            "hist_oh", "hist_mm", "base_ready", "base_mm", "meta_ready", "gb_ready", "gb_out", "gb_in"))
        cleared = [sem(f"cleared{k}") for k in range(3)]
        xg_in = [sem(f"xg_in{s}") for s in range(2)]
        xg_out = [sem(f"xg_out{s}") for s in range(2)]
        (xn_ready, tr_mm, xnT_ready, sup_mm, sup_ready) = (sem(n) for n in (
            "xn_ready", "tr_mm", "xnT_ready", "sup_mm", "sup_ready"))
        (oh_ready, rank_mm, rank_read, relb_mm, oht_ready, main_mm, row_ready, pos_ready, ws_ready) = (
            sem(n) for n in ("oh_ready", "rank_mm", "rank_read", "relb_mm", "oht_ready", "main_mm",
                             "row_ready", "pos_ready", "ws_ready"))
        win_in = [sem(f"win_in{k}") for k in range(KB)]
        scat = [sem(f"scattered{k}") for k in range(KB)]
        dsg_ready, gath = sem("dsg_ready"), sem("gathered")
        xnTb_in = [sem(f"xnTb_in{u}") for u in range(2)]
        (q_mm, kv_mm, elu_a, elu_v, kv_acc, q_out, kvb_ready) = (sem(n) for n in (
            "q_mm", "kv_mm", "elu_parts", "elu_done", "kv_acc", "q_out", "kvb_ready"))
        (qxn_in, x_in, t_mm, x1_ready, x1T_mm, x1T_ready, h_mm, h_ready, y_mm, mix_done) = (sem(n) for n in (
            "qxn_in", "x_in", "t_mm", "x1_ready", "x1T_mm", "x1T_ready", "h_mm", "h_ready", "y_mm", "mix_done"))
        abs_done = sem("abs_done")
        fw_in, last_in, t_read, xnb_read = (sem(n) for n in ("fw_in", "last_in", "t_read", "xnb_read"))
        passed = sem("passed")
        r_in = [sem(f"rows_in{k}") for k in range(KB)]
        (ohw_ready, grp_mm, acc_done, cnt_ready, cnt_mm, final_cnt, final_mm) = (sem(n) for n in (
            "ohw_ready", "grp_mm", "acc_done", "cnt_ready", "cnt_mm", "final_cnt", "final_mm"))
        (x3_ready, x3T_mm, x3T_ready, fh_mm, fh_ready, fy_mm, o_ready) = (sem(n) for n in (
            "x3_ready", "x3T_mm", "x3T_ready", "fh_mm", "fh_ready", "fy_mm", "o_ready"))
        sums_ready = sem("sums_ready")
        q_free, rows_left = sem("q_free"), sem("rows_left")
        (rows_ready, base_out, base_free, take_ready, take_mm, sel_ready, sel_left, idu_ready,
         fo_out, fo_free) = (sem(n) for n in (
             "rows_ready", "base_out", "base_free", "take_ready", "take_mm", "sel_ready", "sel_left",
             "idu_ready", "fo_out", "fo_free"))
        prod_ready, prod_read = sem("prod_ready"), sem("prod_read")
        sel_out = [sem(f"sel_out{s}") for s in range(2)]
        xc_in = [sem(f"xc_in{s}") for s in range(2)]
        base_in = [sem(f"base_in{s}") for s in range(2)]

        MAIN0, ROW0, OHT0, RANK0, RREAD0, MIX0 = 2 * KB, 2, 1, 1, 1, 1
        ELUA0, ELUV0, KVACC0 = 10, 6, 2
        XNT0, SUP0 = 2, 2
        GRP0, SUM0, ACC0 = 2 * KB, KB, 2 * KB
        XT0, FH0 = 1, 2
        TREAD0, QFREE0, FO0, LEFT0, BASE0, SEL0, PROD0 = 2, 1, 2, KB, 2, 2, 2 * G
        TAB = 16 + 6

        block = ctx.enter_context(nc.Block())
        tiles_of = lambda d: d.rearrange("(t p) c -> t p c", p=P)
        lanes = lambda d: d.rearrange("t p c -> p t c")

        def clear(eng, part_):
            with eng.Fori(CLEARS[part_], CLEARS[part_ + 1]) as i:
                at = eng.value_load(pf_row[0:1, ds(i, 1)], min_val=0, max_val=(NGROUPS - 1) * GS)
                eng.dma_start(rows_d[ds(at, GS), :].rearrange("(p k) f -> p (k f)", p=P),
                              zrow[:, :]).then_inc(cleared[part_], 16)

        xr = tiles_of(x[0:(NT - 1) * P, :])

        @block.sync
        def _(sp):
            sp.sem_inc(q_free, QFREE0)
            sp.sem_inc(base_free, BASE0)
            row = lambda d: d.rearrange("(a b) -> a b", a=1)
            sp.dma_start(last_dst, row(dst[E - 1:E])).then_inc(last_in, 16)
            for k, (a, n) in enumerate(((wqkv, 6), (w1, 2), (w2, 2))):
                at = (0, 6, 8)[k]
                sp.dma_start(wraw[:, at:at + n, :], a.rearrange("(k p) c -> p k c", p=P)).then_inc(wraw_in, 16)
            sp.dma_start(src_d[0:E], src).then_inc(padded, 16)
            sp.dma_start(dst_d[0:E], dst).then_inc(padded, 16)
            sp.dma_start(ew_d[0:E], edge_weight).then_inc(padded, 16)
            sp.wait_ge(padsrc, 2)
            sp.dma_start(row(src_d[E:EPAD]), padi).then_inc(padded, 16)
            sp.dma_start(row(ew_d[E:EPAD]), zrow[0:1, 0:EPAD - E]).then_inc(padded, 16)
            sp.wait_ge(padsrc, 3)
            sp.dma_start(row(dst_d[E:EPAD]), padj).then_inc(padded, 16)
            sp.dma_start(sup_d[NT * P:, :], zrow[:, 0:C]).then_inc(w_in, 16)
            sp.dma_start(gw_s[:, :, :], gnn_w.rearrange("(k p) c -> p k c", p=P)).then_inc(w_in, 16)
            sp.wait_ge(padded, 96)
            for a, d in ((rsrc, src_d), (rdst, dst_d)):
                sp.dma_start(a.bitcast(I32).rearrange("r (j e) -> r j e", e=P),
                             d.rearrange("(j r e) -> r j e", r=P, e=P)).then_inc(raw_in, 16)
            sp.dma_start(rew.rearrange("r (j e) -> r j e", e=P),
                         ew_d.rearrange("(j r e) -> r j e", r=P, e=P)).then_inc(raw_in, 16)
            sp.dma_start(rrel[0:EQ, :].bitcast(I32), dst_d.rearrange("(q f) -> q f", q=EQ)).then_inc(raw_in, 16)
            sp.dma_start(d0_row[0:1, :], dst_d.rearrange("(a b e) -> a b e", a=1, e=BE)[:, :, 0],
                         allow_slow_non_contiguous=True).then_inc(d0_in, 16)
            for k, v in enumerate((ln1_g, ln1_b, ln2_g, ln2_b, b2, fb2, wr.rearrange("a b -> (a b)"))):
                sp.dma_start(vec[:, k, :], v.partition_broadcast(P)).then_inc(w_in, 16)
            sp.dma_start(b1_c[:, :], b1.rearrange("(k p) -> p k", p=P),
                         allow_slow_non_contiguous=True).then_inc(w_in, 16)
            sp.dma_start(fb1_c[:, :], fb1.rearrange("(k p) -> p k", p=P),
                         allow_slow_non_contiguous=True).then_inc(w_in, 16)
            sp.dma_start(br_c[:, :], br.partition_broadcast(P)).then_inc(w_in, 16)

            sp.wait_ge(tab_read, 6)

            def x_load(s, g):
                sp.dma_start(x_g[s][:, 0:G - 1, :], lanes(xr[ds(g * G, G - 1)])).then_inc(xg_in[s], 16)
                sp.dma_start(x_g[s][:, G - 1, :], x[ds((g * G + G - 1) * P, P), :]).then_inc(xg_in[s], 16)

            def x_load_last(s):
                sp.dma_start(x_g[s][:, 0:G - 1, :], lanes(xr[(NG - 1) * G:NT - 1])).then_inc(xg_in[s], 16)
                sp.dma_start(x_g[s][0:LASTROWS, G - 1, :], x[(NT - 1) * P:N, :]).then_inc(xg_in[s], 16)

            def stage_out(s, g):
                sp.wait_ge(xn_ready, G * (g + 1))
                sp.dma_start(lanes(tiles_of(xn_d)[ds(g * G, G)]), x_g[s]).then_inc(xg_out[s], 16)
                sp.wait_ge(xnT_ready, XNT0 + G * (g + 1))
                sp.dma_start(lanes(xnT_d[ds(g * G, G)]), xnT_g[s]).then_inc(xg_out[s], 16)
                sp.wait_ge(sup_ready, SUP0 + G * (g + 1))
                sp.dma_start(lanes(tiles_of(sup_d[0:NT * P])[ds(g * G, G)]), sup_g[s]).then_inc(xg_out[s], 16)

            x_load(0, 0)
            x_load(1, 1)
            with sp.Fori(0, NG // 2 - 2) as i:
                for s in range(2):
                    stage_out(s, 2 * i + s)
                    sp.wait_ge(xg_out[s], 48 * (i + 1))
                    x_load(s, 2 * i + 2 + s)
            for s in range(2):
                stage_out(s, NG - 4 + s)
                sp.wait_ge(xg_out[s], 48 * (NG // 2 - 1))
                if s == 0:
                    x_load(0, NG - 2)
                else:
                    x_load_last(1)
            for s in range(2):
                stage_out(s, NG - 2 + s)

            for s in range(2):
                sp.wait_ge(xg_out[s], 48 * (NG // 2))
            sp.wait_ge(d0_in, 16)

            def window(i, k):
                b = KB * i + k
                sp.wait_ge(main_mm, 2 * b + 2)
                first = sp.value_load(d0_row[0:1, ds(b, 1)], min_val=0, max_val=N - 1)
                sp.dma_start(win[:, k, :], sup_d[ds(first, P), :]).then_inc(win_in[k], 16)

            def att_load(u, n):
                sp.dma_start(xnT_b[u], xnT_d[ds(n, 1)].rearrange("a p c -> (a p) c")).then_inc(xnTb_in[u], 16)

            def att_step(i, more):
                for k in range(KB):
                    if k == 3:
                        sp.wait_ge(elu_v, ELUV0 + 6 * i + 5)
                        sp.dma_start(lanes(qT_d[ds(2 * i, 2)]), qTb).then_inc(q_out, 16)
                    window(i + 1, k)
                    if more and k < 2:
                        sp.wait_ge(kv_mm, 2 * i + k + 1)
                        att_load(k, 2 * i + 2 + k)
                sp.wait_ge(q_out, 16 * (i + 1))
                sp.sem_inc(q_free, 1)

            for k in range(KB):
                window(0, k)
                if k < 2:
                    att_load(k, k)
            sp.wait_ge(meta_ready, 1)
            clear(sp, 0)
            sp.wait_ge(gb_ready, 1)
            sp.dma_start(gb_d.rearrange("(j p) -> p j", p=P), gb_pj,
                         allow_slow_non_contiguous=True).then_inc(gb_out, 16)
            sp.wait_ge(gb_out, 16)
            sp.dma_start(gb_row[0:1, :], row(gb_d)).then_inc(gb_in, 16)
            with sp.Fori(0, NT // 2 - 1) as i:
                att_step(i, True)
            att_step(NT // 2 - 1, False)
            sp.wait_ge(q_out, 16 * (NT // 2))
            for k in range(3):
                sp.wait_ge(cleared[k], 16 * (CLEARS[k + 1] - CLEARS[k]))

            def front_load(i):
                sp.dma_start(qTm, lanes(qT_d[ds(2 * i, 2)])).then_inc(qxn_in, 16)
                sp.dma_start(xnb, lanes(tiles_of(xn_d)[ds(2 * i, 2)])).then_inc(qxn_in, 16)

            def x_back(i, last=False):
                sp.dma_start(xb[:, 0, :], x[ds(2 * P * i, P), :]).then_inc(x_in, 16)
                if last:
                    sp.dma_start(xb[0:LASTROWS, 1, :], x[(NT - 1) * P:N, :]).then_inc(x_in, 16)
                else:
                    sp.dma_start(xb[:, 1, :], x[ds(2 * P * i + P, P), :]).then_inc(x_in, 16)

            def mix_step(i, front=True, last=False):
                e = NT // 2 + i
                window(e + 1, 0)
                if front:
                    sp.wait_ge(t_mm, i + 1)
                    sp.wait_ge(xnb_read, i + 1)
                    front_load(i + 1)
                window(e + 1, 1)
                window(e + 1, 2)
                window(e + 1, 3)
                sp.wait_ge(mix_done, MIX0 + i)
                x_back(i, last)

            front_load(0)
            with sp.Fori(0, NT // 2 - 1) as i:
                mix_step(i)
            mix_step(NT // 2 - 1, front=False, last=True)
            with sp.Fori(2 * (NT // 2) + 1, EQ) as i:
                for k in range(KB):
                    window(i, k)

            for k in range(KB):
                sp.wait_ge(scat[k], 16 * BT * EQ)
            steps = sp.value_load(meta[0:1, 1:2], min_val=1, max_val=NGMAX // RG + 1)
            with sp.Fori(0, steps) as i:
                for k in range(KB):
                    sp.wait_ge(grp_mm, RG * i + 2 * k + 2)
                    sp.dma_start(rowbuf[:, k * BT:(k + 1) * BT, :].rearrange("p (g k) f -> p g (k f)", g=2),
                                 rows_d[ds((RG * i + 2 * k + 1) * GS, 2 * GS), :].rearrange(
                                     "(g p k) f -> p g (k f)", g=2, p=P)).then_inc(r_in[k], 16)

            sp.wait_ge(rank_mm, RANK0 + NB)
            sp.dma_start(fw1_s, fw1.rearrange("(k p) c -> p k c", p=P)).then_inc(fw_in, 16)
            sp.dma_start(fw2_s, fw2.rearrange("(k p) c -> p k c", p=P)).then_inc(fw_in, 16)

            def base_store(g, s, last=False):
                sp.wait_ge(rows_ready, g + 1)
                rows_ = x3[s].rearrange("p (t c) -> p t c", t=G)
                if last:
                    sp.dma_start(lanes(tiles_of(out[(NT - G) * P:(NT - 1) * P, :])), rows_[:, 0:G - 1, :]).then_inc(
                        base_out, 16)
                    sp.dma_start(out[(NT - 1) * P:N, :], rows_[0:LASTROWS, G - 1, :]).then_inc(base_out, 16)
                else:
                    sp.dma_start(lanes(tiles_of(out[0:(NT - 1) * P, :])[ds(G * g, G)]), rows_).then_inc(base_out, 16)
                    sp.wait_ge(base_out, 16 * (g + 1))
                    sp.sem_inc(base_free, 1)

            with sp.Fori(0, NG // 2 - 1) as i:
                for s in range(2):
                    base_store(2 * i + s, s)
            base_store(NG - 2, 0)
            base_store(NG - 1, 1, last=True)

            def served_load(i, s):
                sp.dma_start(xc[s], rows_d[ds(2 * P * i, 2 * P), :].rearrange("(u p) f -> p u f", p=P)).then_inc(
                    xc_in[s], 16)

            for s in range(2):
                sp.wait_ge(sel_out[s], 16 * G * (NG // 2))
            for s in range(2):
                served_load(s, s)
            with sp.Fori(0, FP // 2 - 1) as i:
                for s in range(2):
                    sp.wait_ge(o_ready, 2 * (2 * i + s + 1))
                    served_load(2 * i + s + 2, s)
            sp.wait_ge(o_ready, 2 * (FP - 2))
            served_load(FP - 1, 0)

        @block.gpsimd
        def _(pool):
            g = nc.gpsimd
            pool.sem_inc(rows_left, LEFT0)
            g.memset(zrow, 0.0).then_inc(padsrc, 1)
            g.memset(padi, NT * P - 1).then_inc(padsrc, 1)
            pool.wait_ge(last_in, 16)
            g.tensor_copy(padj, last_dst.to_broadcast([1, EPAD - E])).then_inc(padsrc, 1)
            g.iota(lane[:, :], [[0, 1]], base=0, channel_multiplier=1,
                   allow_small_or_imprecise_dtypes=True).then_inc(iotas, 1)
            g.iota(cols[:, :], [[1, P]], base=0, channel_multiplier=0,
                   allow_small_or_imprecise_dtypes=True).then_inc(iotas, 1)
            g.memset(zeros_b[:, :], 0.0).then_inc(iotas, 1)
            g.memset(ones_b[:, :], 1.0).then_inc(iotas, 1)
            g.memset(onesf[:, :], 1.0).then_inc(iotas, 1)
            g.memset(maskc[:, :], 1.0).then_inc(iotas, 1)
            g.memset(kvb[:, :, :], 0.0).then_inc(iotas, 1)
            g.iota(bits[:, :, :], [[2, 16], [0, 6]], base=0, channel_multiplier=0).then_inc(iotas, 1)

            pool.wait_ge(meta_ready, 1)
            clear(pool, 2)
            for k in range(3):
                pool.wait_ge(cleared[k], 16 * (CLEARS[k + 1] - CLEARS[k]))
            pool.wait_ge(flag_ready, 1)
            wide = pool.value_load(meta[0:1, 2:3], min_val=0, max_val=EQ)

            def scatter(i, k, first=False):
                b = KB * i + k
                pool.wait_ge(pos_ready, b + 1)
                pool.wait_ge(ws_ready, b + 1)
                pool.wait_ge(row_ready, ROW0 + 2 * b + 2)
                pool.sem_inc(passed, 1)
                with pool.If(wide > 0):
                    g.tensor_copy(dsg[:, :], dst_t[:, ds(BT * b, BT)]).then_inc(dsg_ready, 1)
                    pool.wait_ge(dsg_ready, b + 1)
                    pool.sem_inc(passed, 1)
                    for t in range(BT):
                        g.indirect_dma_start(rowbuf[:, BT * k + t, 0:C], None, sup_d,
                                             bass.IndirectOffsetOnAxis(dsg[:, t:t + 1], 0)).then_inc(gath, 16)
                    pool.wait_ge(gath, 16 * BT * (b + 1))
                    pool.sem_inc(passed, 1)
                for t in range(BT):
                    s = BT * k + t
                    g.indirect_dma_start(rows_d, bass.IndirectOffsetOnAxis(posu[:, s:s + 1], 0),
                                         rowbuf[:, s, :], None).then_inc(scat[k], 16)
                if not first:
                    pool.wait_ge(scat[(k - 1) % KB], 16 * BT * (i + (k > 0)))
                    pool.sem_inc(rows_left, 1)

            for k in range(KB):
                scatter(0, k, first=k == 0)
            with pool.Fori(1, EQ) as i:
                for k in range(KB):
                    scatter(i, k)

            pool.sem_inc(acc_done, ACC0)
            pool.wait_ge(gb_in, 16)
            pool.wait_ge(mix_done, MIX0 + NT // 2)
            steps = pool.value_load(meta[0:1, 1:2], min_val=1, max_val=NGMAX // RG + 1)
            with pool.Fori(0, steps) as i:
                for k in range(KB):
                    for h in range(2):
                        group = RG * i + 2 * k + h
                        at = pool.value_load(gb_row[0:1, ds(group + 1, 1)], min_val=0, max_val=(NT - 1) * C)
                        pool.wait_ge(sums_ready, SUM0 + KB * i + k + 1)
                        pool.wait_ge(acc_done, ACC0 + group)
                        g.tensor_tensor(acc[:, ds(at, C)], acc[:, ds(at, C)], sums[:, k, h * C:(h + 1) * C],
                                        ALU.add).then_inc(acc_done, 1)

            def sort_rows(i, s, first=False):
                pool.wait_ge(sel_ready, (G + 3) * (2 * i + s + 1))
                pool.sem_inc(passed, 1)
                for t in range(G):
                    g.indirect_dma_start(rows_d, bass.IndirectOffsetOnAxis(posu[:, s * G + t:s * G + t + 1], 0),
                                         rowbuf[:, s * G + t, :], None).then_inc(sel_out[s], 16)
                if not first:
                    pool.wait_ge(sel_out[1 - s], 16 * G * (i + s))
                    pool.sem_inc(sel_left, 1)

            pool.sem_inc(sel_left, SEL0)
            pool.sem_inc(fo_free, FO0)
            sort_rows(0, 0, first=True)
            sort_rows(0, 1)
            with pool.Fori(1, NG // 2) as i:
                for s in range(2):
                    sort_rows(i, s)

            def base_fetch(i, s):
                pool.wait_ge(idu_ready, i + 1)
                pool.sem_inc(passed, 1)
                for u in range(2):
                    g.indirect_dma_start(base[:, s, u * C:(u + 1) * C], None, out,
                                         bass.IndirectOffsetOnAxis(idu[:, s, u:u + 1], 0)).then_inc(base_in[s], 16)

            def rows_out(i, s):
                pool.wait_ge(o_ready, 2 * (i + 1))
                pool.sem_inc(passed, 1)
                for u in range(2):
                    g.indirect_dma_start(out, bass.IndirectOffsetOnAxis(idu[:, s, u:u + 1], 0),
                                         fo[:, s, u * C:(u + 1) * C], None).then_inc(fo_out, 16)
                pool.wait_ge(fo_out, 32 * (i + 1))
                pool.sem_inc(fo_free, 1)

            pool.wait_ge(base_out, 16 * (NG + 1))
            base_fetch(0, 0)
            with pool.Fori(0, FP // 2) as i:
                for s in range(2):
                    base_fetch(2 * i + s + 1, 1 - s)
                    rows_out(2 * i + s, s)
            rows_out(FP - 1, 0)
            pool.wait_ge(fo_out, 32 * FP)

        @block.tensor
        def _(pe):
            mm, tp = nc.tensor.matmul, nc.tensor.transpose
            pe.sem_inc(main_mm, MAIN0)
            pe.sem_inc(rank_mm, RANK0)
            pe.sem_inc(kv_acc, KVACC0)
            pe.sem_inc(grp_mm, GRP0)
            pe.wait_ge(consts, 5)
            pe.wait_ge(iotas, 8)

            def blocks(job, items):
                if job >= 8:
                    pe.wait_ge(tab_read, job - 7)
                for k, a in enumerate(items):
                    last = tp(ps[:, job % 8, k * P:(k + 1) * P], a, ident[:, :])
                last.then_inc(tab_mm, 1)

            pe.wait_ge(wraw_in, 48)
            for job, (rows, c) in enumerate((([0, 1, 2, 3], 0), ([4, 5], 0), ([0, 1, 2, 3], 1), ([4, 5], 1))):
                blocks(job, [wraw[:, r, c * P:(c + 1) * P] for r in rows])
            for job, at in ((4, 6), (5, 8)):
                blocks(job, [wraw[:, at + r, c * P:(c + 1) * P] for c in range(CC) for r in range(2)])
            pe.wait_ge(raw_in, 64)
            for k, tab in enumerate((fbkt, floc, rew, fdst)):
                pe.wait_ge(raw_ready, (2, 4, 4, 5)[k])
                for q in range(4):
                    n = min(4, EJ - 4 * q)
                    blocks(6 + 4 * k + q, [tab[:, (4 * q + r) * P:(4 * q + r + 1) * P] for r in range(n)])
            pe.wait_ge(tab_read, TAB)
            pe.wait_ge(viol_ready, 1)
            mm(ps[0:1, 3, 0:1], tk[0:EQ, 0:1], onesf[0:EQ, 0:1], start=True, stop=True).then_inc(viol_mm, 1)

            hist = ps[0:EQ, RANK, 0:BT * NT]
            mm(hist, zeros_b[:, 0:EQ], zeros_b[:, 0:BT * NT], start=True, stop=False)
            pe.wait_ge(w_in, 16 * 12)

            def count(i):
                for k in range(KB):
                    pe.wait_ge(hist_oh, KB * i + k + 1)
                    pe.sem_inc(passed, 1)
                    mm(hist, onecol[:, ds(EQ - 1 - i, EQ)], ohb[:, k, :], start=False, stop=False).then_inc(hist_mm, 1)

            with pe.Fori(0, NG // 2) as i:
                for n in range(2 * G):
                    s, t = n // G, n % G
                    tile = 2 * G * i + n
                    pe.wait_ge(xn_ready, tile + 1)
                    pe.wait_ge(xnT_ready, tile + 1)
                    for c in range(CC):
                        last = tp(ps[:, 4 + n % 2, c * P:(c + 1) * P], x_g[s][:, t, c * P:(c + 1) * P], ident[:, :])
                    last.then_inc(tr_mm, 1)
                    count(tile)
                    pe.wait_ge(xnT_ready, XNT0 + tile + 1)
                    pe.wait_ge(sup_ready, tile + 1)
                    for c in range(CC):
                        last = mm(ps[:, 6 + n % 2, 0:C], xnT_g[s][:, t, c * P:(c + 1) * P], gw_s[:, c, :],
                                  start=c == 0, stop=c == CC - 1)
                    last.then_inc(sup_mm, 1)
            with pe.Fori(NT, EQ) as i:
                count(i)
            mm(hist, zeros_b[:, 0:EQ], zeros_b[:, 0:BT * NT], start=False, stop=True).then_inc(hist_mm, 1)
            pe.wait_ge(base_ready, 1)
            mm(ps[:, 1, 0:BT * NT], onesf[0:EQ, :], offs[0:EQ, 1, :], start=True, stop=True)
            mm(ps[0:EQ, 2, 0:BT * NT], beforef[0:EQ, 0:EQ], offs[0:EQ, 1, :], start=True, stop=True).then_inc(base_mm, 1)

            pe.wait_ge(flag_ready, 1)
            pe.wait_ge(meta_ready, 1)
            pe.wait_ge(sup_ready, SUP0 + NT)
            mm(ps[:, KVA, 0:CC * (P + 1)], zeros_b[:, 0:P], zeros_b[:, 0:CC * (P + 1)], start=True, stop=False)

            def relb(i, k):
                pe.wait_ge(oht_ready, KB * i + k + 1)
                mm(ps[:, RELB, :], ident_h[0:EQ, ds(i, 1)].to_broadcast([EQ, P]), rel[:, k * BE:(k + 1) * BE],
                   start=True, stop=True).then_inc(relb_mm, 1)

            def ranks(i, k, more=True):
                b = KB * i + k
                pe.wait_ge(oht_ready, OHT0 + b + 1)
                if more:
                    relb(*((i, k + 1) if k + 1 < KB else (i + 1, 0)))
                pe.wait_ge(rank_read, RREAD0 + BT * b)
                rank = ps[:, RANK, 0:BT * NT]
                mm(rank, ident_h[0:EQ, ds(i, 1)].to_broadcast([EQ, P]), first_lo[:, :], start=True, stop=False)
                mm(rank, ident_hi[0:EQ, ds(i, 1)].to_broadcast([EQ, P]), first_hi[:, :], start=False, stop=False)
                for j in range(k):
                    mm(rank, ones_b[:, :], ohb[:, j, :], start=False, stop=False)
                pe.wait_ge(oh_ready, b + 1)
                mm(rank, before[:, :], ohb[:, k, :], start=False, stop=True).then_inc(rank_mm, 1)

            def messages(i, k):
                b = KB * i + k
                pe.wait_ge(win_in[k], 16 * (i + 1))
                for h in range(2):
                    pe.wait_ge(row_ready, 2 * b + h + 1)
                    for t in range(2):
                        last = mm(ps[:, MSG + h, t * C:(t + 1) * C], oht[:, k % 2, (2 * h + t) * P:(2 * h + t + 1) * P],
                                  win[:, k, :], start=True, stop=True)
                    last.then_inc(main_mm, 1)

            def edges(i, k, more=True):
                ranks(i, k, more)
                messages(i, k)

            def qkv(i, u):
                n = 2 * i + u
                pe.wait_ge(xnTb_in[u], 16 * (i + 1))
                pe.wait_ge(elu_a, 5 * n + 7)
                for m in range(CC):
                    for c in range(CC):
                        last = mm(ps[:, QPS, u * C + m * P:u * C + (m + 1) * P], wqkvT[:, c, m * P:(m + 1) * P],
                                  xnT_b[u][:, c * P:(c + 1) * P], start=c == 0, stop=c == CC - 1)
                last.then_inc(q_mm, 1)
                for c in range(CC):
                    last = mm(ps[:, KVPS + u, :], xnT_b[u][:, c * P:(c + 1) * P], wqkvT[:, c, C:3 * C],
                              start=c == 0, stop=c == CC - 1)
                last.then_inc(kv_mm, 1)

            def kv_sum(i, u):
                n = 2 * i + u
                pe.wait_ge(elu_v, ELUV0 + 3 * n + 3)
                pe.wait_ge(elu_a, ELUA0 + 5 * n + 5)
                for c in range(CC):
                    last = mm(ps[:, KVA, c * (P + 1):(c + 1) * (P + 1)], kk[:, u, c * P:(c + 1) * P],
                              vext[:, u, c, :], start=False, stop=False)
                last.then_inc(kv_acc, 1)

            relb(0, 0)
            with pe.Fori(0, NT // 2) as i:
                edges(i, 0)
                qkv(i, 0)
                edges(i, 1)
                qkv(i, 1)
                edges(i, 2)
                kv_sum(i, 0)
                edges(i, 3)
                kv_sum(i, 1)
            mm(ps[:, KVA, 0:CC * (P + 1)], zeros_b[:, 0:P], zeros_b[:, 0:CC * (P + 1)], start=False,
               stop=True).then_inc(kv_acc, 1)
            pe.wait_ge(kvb_ready, 1)
            pe.wait_ge(elu_a, ELUA0 + 5 * NT)
            pe.wait_ge(w_in, 16 * 12)

            def attend(i):
                pe.wait_ge(qxn_in, 32 * (i + 1))
                pe.wait_ge(t_read, 2 * i + 2)
                for u in range(2):
                    for c in range(CC):
                        last = mm(ps[:, TPS + u, c * (P + 4):(c + 1) * (P + 4)], qTm[:, u, c * P:(c + 1) * P],
                                  kvb[:, c, :], start=True, stop=True)
                last.then_inc(t_mm, 1)

            def x1_transpose(i):
                pe.wait_ge(x1_ready, 2 * (i + 1))
                for c in range(CC):
                    for u in range(2):
                        last = tp(ps[:, XTPS, (2 * c + u) * P:(2 * c + u + 1) * P], x1[:, u, c * P:(c + 1) * P],
                                  ident[:, :])
                last.then_inc(x1T_mm, 1)

            def mlp_up(i):
                pe.wait_ge(x1T_ready, i + 1)
                for m in range(CC):
                    for c in range(CC):
                        last = mm(ps[:, HPS, m * C:(m + 1) * C], w1T[:, c, m * P:(m + 1) * P], x1T[:, c, :],
                                  start=c == 0, stop=c == CC - 1)
                last.then_inc(h_mm, 1)

            def mlp_down(i):
                pe.wait_ge(h_ready, 2 * (i + 1))
                for u in range(2):
                    for m in range(CC):
                        mm(ps[:, YPS, u * C:(u + 1) * C], hT[:, m, u * P:(u + 1) * P], w2T[:, m, :],
                           start=m == 0, stop=False)
                    last = mm(ps[:, YPS, u * C:(u + 1) * C], onesf[0:1, :], vec[0:1, B2, :], start=False, stop=True)
                last.then_inc(y_mm, 1)

            def mix_step(i, front, back):
                e = NT // 2 + i
                ranks(e, 0)
                if front:
                    attend(i)
                if back:
                    mlp_up(i - 1)
                messages(e, 0)
                ranks(e, 1)
                if back:
                    mlp_down(i - 1)
                messages(e, 1)
                edges(e, 2)
                edges(e, 3)
                if front:
                    x1_transpose(i)

            mix_step(0, True, False)
            with pe.Fori(1, NT // 2) as i:
                mix_step(i, True, True)
            mix_step(NT // 2, False, True)
            with pe.Fori(2 * (NT // 2) + 1, EQ - 1) as i:
                for k in range(KB):
                    edges(i, k)
            for k in range(KB):
                edges(EQ - 1, k, more=k + 1 < KB)

            pe.wait_ge(mix_done, MIX0 + NT // 2)
            pe.wait_ge(row_ready, ROW0 + 2 * NB)
            steps = pe.value_load(meta[0:1, 1:2], min_val=1, max_val=NGMAX // RG + 1)
            with pe.Fori(0, steps) as i:
                for k in range(KB):
                    pe.wait_ge(r_in[k], 16 * (i + 1))
                    pe.wait_ge(sums_ready, KB * i + k + 1)
                    for h in range(2):
                        grp = RG * i + 2 * k + h
                        for t in range(2):
                            pe.wait_ge(ohw_ready, 2 * grp + t + 1)
                            s = 2 * h + t
                            last = mm(ps[:, GRP + k, h * C:(h + 1) * C], oht[:, k % 2, s * P:(s + 1) * P],
                                      rowbuf[:, BT * k + s, 0:C], start=t == 0, stop=t == 1)
                        last.then_inc(grp_mm, 1)

            with pe.Fori(0, 16) as i:
                pe.wait_ge(cnt_ready, i + 1)
                mm(ps[:, 0, 0:3], ones_b[:, :], cntb[:, :], start=True, stop=True).then_inc(cnt_mm, 1)
            pe.wait_ge(final_cnt, 1)
            mm(ps[:, 0, 0:NT], ones_b[:, :], ohb[:, 0, 0:NT], start=True, stop=True)
            mm(ps[:, 1, 0:NT], ones_b[:, :], ohb[:, 1, 0:NT], start=True, stop=True)
            mm(ps[:, 2, 0:NT], before[:, :], ohb[:, 1, 0:NT], start=True, stop=True).then_inc(final_mm, 1)

            pe.wait_ge(take_ready, 1)
            mm(ps[:, 3, 0:NT], ones_b[:, :], ohb[:, 2, 0:NT], start=True, stop=True)
            mm(ps[:, 3, NT:2 * NT], before[:, :], ohb[:, 2, 0:NT], start=True, stop=True).then_inc(take_mm, 1)

            pe.wait_ge(fw_in, 32)
            pe.wait_ge(sel_ready, G + 3)

            def served_transpose(i, s, turn):
                pe.wait_ge(xc_in[s], 16 * (turn + 1))
                pe.wait_ge(x3T_ready, i + 1)
                for c in range(CC):
                    for u in range(2):
                        last = tp(ps[:, 0, (2 * c + u) * P:(2 * c + u + 1) * P], xc[s][:, u, c * P:(c + 1) * P],
                                  ident[:, :])
                last.then_inc(x3T_mm, 1)

            def ffn_up(i, s):
                pe.wait_ge(x3T_ready, XT0 + i + 1)
                for m in range(HID // P):
                    pe.wait_ge(fh_ready, 8 * i + m + 1)
                    for c in range(CC):
                        last = mm(ps[:, 2 + m % 2, 0:C], fw1_s[:, c, m * P:(m + 1) * P],
                                  x3T[:, s, c * 2 * P:(c + 1) * 2 * P], start=c == 0, stop=c == CC - 1)
                    last.then_inc(fh_mm, 1)

            def ffn_down(i, s, first=False):
                pe.wait_ge(fh_ready, FH0 + 8 * (i + 1))
                if not first:
                    pe.wait_ge(o_ready, 2 * (i - 1))
                for u in range(2):
                    for m in range(HID // P):
                        last = mm(ps[:, 4 + s, u * C:(u + 1) * C], fhT[:, s, m, u * P:(u + 1) * P], fw2_s[:, m, :],
                                  start=m == 0, stop=m == HID // P - 1)
                last.then_inc(fy_mm, 1)

            def ffn_pairs(i, first=False):
                ffn_up(2 * i, 0)
                served_transpose(2 * i + 1, 1, i)
                ffn_down(2 * i, 0, first)
                ffn_up(2 * i + 1, 1)
                served_transpose(2 * i + 2, 0, i + 1)
                ffn_down(2 * i + 1, 1, first)

            served_transpose(0, 0, 0)
            ffn_pairs(0, first=True)
            with pe.Fori(1, FP // 2) as i:
                ffn_pairs(i)
            ffn_up(FP - 1, 0)
            ffn_down(FP - 1, 0)

        @block.scalar
        def _(act):
            A = nc.scalar.activation
            act.sem_inc(xnT_ready, XNT0)
            act.sem_inc(sup_ready, SUP0)
            act.sem_inc(row_ready, ROW0)
            act.sem_inc(elu_a, ELUA0)
            act.sem_inc(x3T_ready, XT0)
            act.sem_inc(fh_ready, FH0)
            act.sem_inc(sums_ready, SUM0)
            act.sem_inc(prod_read, PROD0)
            outs = [wqkvT[:, 0, 0:512], wqkvT[:, 0, 512:768], wqkvT[:, 1, 0:512], wqkvT[:, 1, 512:768],
                    w1T[:, :, :].rearrange("p c o -> p (c o)"), w2T[:, :, :].rearrange("p c o -> p (c o)")]
            for tab in (bkt_t, ws_t[:, :, 1], ws_t[:, :, 0], dst_t):
                for q in range(4):
                    outs.append(tab[:, 4 * q * P:min(4 * q + 4, EJ) * P])
            for job, o in enumerate(outs):
                act.wait_ge(tab_mm, job + 1)
                A(o, ps[:, job % 8, 0:o.shape[1]], ACT.Copy).then_inc(tab_read, 1)
            with act.Fori(0, NG // 2) as i:
                for n in range(2 * G):
                    s, t = n // G, n % G
                    tile = 2 * G * i + n
                    act.wait_ge(tr_mm, tile + 1)
                    A(xnT_g[s][:, t, :], ps[:, 4 + n % 2, 0:C], ACT.Copy).then_inc(xnT_ready, 1)
                    act.wait_ge(sup_mm, tile + 1)
                    A(sup_g[s][:, t, :], ps[:, 6 + n % 2, 0:C], ACT.Copy).then_inc(sup_ready, 1)

            act.wait_ge(meta_ready, 1)
            clear(act, 1)

            def rows(i, k):
                b = KB * i + k
                act.wait_ge(rows_left, b + 1)
                for h in range(2):
                    act.wait_ge(main_mm, MAIN0 + 2 * b + h + 1)
                    s = BT * k + 2 * h
                    A(rowbuf[:, s:s + 2, 0:C], ps[:, MSG + h, :].rearrange("p (t c) -> p t c", t=2),
                      ACT.Copy).then_inc(row_ready, 1)
                A(rowbuf[:, BT * k:BT * (k + 1), C:RW], ws_t[:, ds(BT * b, BT), :], ACT.Copy).then_inc(ws_ready, 1)

            def elu_parts(i, u):
                n = 2 * i + u
                act.wait_ge(elu_v, 3 * n + 3)
                act.wait_ge(q_mm, n + 1)
                A(eq[:, u, :], ps[:, QPS, u * C:(u + 1) * C], ACT.Exp).then_inc(elu_a, 1)
                A(rq[:, u, :], ps[:, QPS, u * C:(u + 1) * C], ACT.Relu).then_inc(elu_a, 1)
                act.wait_ge(kv_mm, n + 1)
                A(ek[:, u, :], ps[:, KVPS + u, 0:C], ACT.Exp).then_inc(elu_a, 1)
                A(rk[:, u, :], ps[:, KVPS + u, 0:C], ACT.Relu).then_inc(elu_a, 1)
                act.wait_ge(kv_acc, n + 1)
                A(vext[:, u, :, 0:P], ps[:, KVPS + u, C:2 * C].rearrange("p (c f) -> p c f", c=CC), ACT.Copy,
                  scale=maskc[:, ds(n, 1)]).then_inc(elu_a, 1)

            act.wait_ge(consts, 5)
            for s in range(2):
                act.wait_ge(xg_out[s], 48 * (NG // 2))
            with act.Fori(0, NT // 2) as i:
                rows(i, 0)
                elu_parts(i, 0)
                rows(i, 1)
                elu_parts(i, 1)
                rows(i, 2)
                rows(i, 3)
            act.wait_ge(w_in, 16 * 12)

            def make_oht(i, k):
                b = KB * i + k
                act.wait_ge(relb_mm, b + 1)
                act.wait_ge(main_mm, 2 * b + 6)
                A(oht[:, k % 2, :], ps[:, RELB, :], ACT.Abs, bias=minus_lane[:, :]).then_inc(abs_done, 1)
                act.wait_ge(abs_done, b - KB * (NT // 2))
                A(oht[:, k % 2, :], oht[:, k % 2, :], ACT.Relu, bias=one[:, :], scale=-1.0).then_inc(oht_ready, 1)

            def mix_step(i, front, back):
                e = NT // 2 + i
                for k in range(KB):
                    make_oht(*((e, k + 1) if k + 1 < KB else (e + 1, 0)))
                    if back and k == 0:
                        act.wait_ge(h_mm, i)
                        for m in range(CC):
                            A(hT[:, m, :], ps[:, HPS, m * C:(m + 1) * C], ACT.Gelu,
                              bias=b1_c[:, m:m + 1]).then_inc(h_ready, 1)
                    rows(e, k)
                if front:
                    act.wait_ge(x1T_mm, i + 1)
                    A(x1T.rearrange("p c r -> p (c r)"), ps[:, XTPS, :], ACT.Copy).then_inc(x1T_ready, 1)

            mix_step(0, True, False)
            A(spare[:, :], one[:, :], ACT.Gelu).then_inc(passed, 1)
            with act.Fori(1, NT // 2) as i:
                mix_step(i, True, True)
            mix_step(NT // 2, False, True)
            with act.Fori(2 * (NT // 2) + 1, EQ) as i:
                for k in range(KB):
                    rows(i, k)

            def served_copy(i, s):
                act.wait_ge(x3T_mm, i + 1)
                A(x3T[:, s, :], ps[:, 0, :], ACT.Copy).then_inc(x3T_ready, 1)

            def hidden(i, s):
                for m in range(HID // P):
                    act.wait_ge(fh_mm, 8 * i + m + 1)
                    A(fhT[:, s, m, :], ps[:, 2 + m % 2, 0:C], ACT.Gelu_apprx_tanh,
                      bias=fb1_c[:, m:m + 1]).then_inc(fh_ready, 1)

            act.wait_ge(mix_done, MIX0 + NT // 2)
            steps = act.value_load(meta[0:1, 1:2], min_val=1, max_val=NGMAX // RG + 1)
            with act.Fori(0, steps) as i:
                for k in range(KB):
                    act.wait_ge(grp_mm, GRP0 + RG * i + 2 * k + 2)
                    act.wait_ge(acc_done, RG * i + 2 * k + 2)
                    A(sums[:, k, :], ps[:, GRP + k, :], ACT.Copy).then_inc(sums_ready, 1)

            with act.Fori(0, NG // 2) as i:
                for s in range(2):
                    act.wait_ge(prod_ready, 2 * i + s + 1)
                    for t in range(G):
                        A(prod[:, s, t, :], prod[:, s, t, :], ACT.Copy,
                          accum_out=wts[:, ds(2 * G * i + G * s + t, 1)]).then_inc(prod_read, 1)

            act.wait_ge(grp_mm, GRP0 + RG * steps)
            served_copy(0, 0)
            hidden(0, 0)
            served_copy(1, 1)
            hidden(1, 1)
            served_copy(2, 0)
            with act.Fori(1, FP // 2) as i:
                for s in range(2):
                    act.wait_ge(fy_mm, 2 * i + s - 1)
                    hidden(2 * i + s, s)
                    served_copy(2 * i + s + 1, 1 - s)
            act.wait_ge(fy_mm, FP - 2)
            hidden(FP - 1, 0)

        @block.vector
        def _(dve):
            v = nc.vector
            chain = Chain(dve, dstep)
            v_link = chain.link

            def newton(var, y, t):
                v_link(v.tensor_scalar(t.bitcast(I32), var.bitcast(I32), 1, None, ALU.logical_shift_right))
                v_link(v.tensor_scalar(y.bitcast(I32), t.bitcast(I32), -1.0, 1597463007.0, ALU.mult, ALU.add))
                for _ in range(3):
                    v_link(v.scalar_tensor_tensor(t, y, -0.5, y, ALU.mult, ALU.mult))
                    v_link(v.tensor_tensor(t, t, var, ALU.mult))
                    v_link(v.scalar_tensor_tensor(y, t, 1.5, y, ALU.add, ALU.mult))

            dve.wait_ge(iotas, 8)
            v.tensor_scalar(ident[:, :], cols[:, :], lane[:, 0:1], None, ALU.is_equal).then_inc(consts, 1)
            v.tensor_scalar(ident_h[:, :], cols[:, :], lane[:, 0:1], None, ALU.is_equal).then_inc(consts, 1)
            v.tensor_scalar(ident_hi[:, :], cols[:, :], lane[:, 0:1], float(LOW), ALU.is_equal,
                            ALU.mult).then_inc(consts, 1)
            v.tensor_scalar(before[:, :], cols[:, :], lane[:, 0:1], None, ALU.is_gt).then_inc(consts, 1)
            v.tensor_scalar(maskc[:, NT - 1:NT], lane[:, 0:1], float(LASTROWS), None, ALU.is_lt).then_inc(consts, 1)
            units = newt[:, 2, 0:96].bitcast(I32).rearrange("p (a b) -> p a b", b=6)
            for k, unit in enumerate((1, 2, 3, 1, 3, 1)):
                v_link(v.memset(units[:, :, k], unit))
            v_link(v.tensor_tensor(bits[:, :, :], units, bits[:, :, :], ALU.logical_shift_left))
            v_link(v.tensor_scalar(minus_lane[:, :], lane[:, :], -1.0, None, ALU.mult))
            v_link(v.memset(one[:, :], 1.0))
            v_link(v.memset(onecol[:, :], 0.0))
            v_link(v.memset(onecol[:, EQ - 1:EQ], 1.0))
            v.sem_inc(oht_ready, OHT0)
            v.sem_inc(elu_v, ELUV0)
            v.sem_inc(rank_read, RREAD0)
            v.sem_inc(mix_done, MIX0)
            v.sem_inc(t_read, TREAD0)

            dve.wait_ge(raw_in, 64)
            si = rsrc.bitcast(I32)
            v.tensor_scalar(fbkt.bitcast(I32), si, 7, None, ALU.logical_shift_right).then_inc(raw_ready, 1)
            dve.wait_ge(raw_ready, 1)
            v.tensor_copy(fbkt, fbkt.bitcast(I32)).then_inc(raw_ready, 1)
            v.tensor_scalar(floc.bitcast(I32), si, P - 1, None, ALU.bitwise_and).then_inc(raw_ready, 1)
            dve.wait_ge(raw_ready, 3)
            v.tensor_copy(floc, floc.bitcast(I32)).then_inc(raw_ready, 1)
            v.tensor_copy(fdst, rdst.bitcast(I32)).then_inc(raw_ready, 1)
            rr = rrel[0:EQ, :].bitcast(I32).rearrange("p (k e) -> p k e", k=KB)
            v_link(v.tensor_tensor(rel[:, :].rearrange("p (k e) -> p k e", k=KB), rr,
                                   rr[:, :, 0:1].to_broadcast([EQ, KB, BE]), ALU.subtract))
            chain.inc(v.tensor_reduce(tk[0:EQ, 1:2], rel[:, :], AX.X, ALU.max))
            chain.inc(v.tensor_reduce(tk[0:EQ, 2:3], rel[:, :], AX.X, ALU.min))
            chain.wait()
            v_link(v.tensor_scalar(tk[0:EQ, 1:2], tk[0:EQ, 1:2], float(P - 1), None, ALU.is_gt))
            v_link(v.tensor_scalar(tk[0:EQ, 2:3], tk[0:EQ, 2:3], 0.0, None, ALU.is_lt))
            v.tensor_tensor(tk[0:EQ, 0:1], tk[0:EQ, 1:2], tk[0:EQ, 2:3], ALU.max).then_inc(viol_ready, 1)

            bidx = cols[:, 0:NT].unsqueeze(1).to_broadcast([P, BT, NT])

            def one_hot(b, k):
                return v.tensor_tensor(ohb[:, k, :].rearrange("p (t n) -> p t n", t=BT),
                                       bkt_t[:, ds(BT * b, BT)].unsqueeze(2).to_broadcast([P, BT, NT]), bidx,
                                       ALU.is_equal)

            dve.wait_ge(tab_read, TAB)
            for k in range(KB):
                one_hot(k, k).then_inc(hist_oh, 1)

            def count(i):
                for k in range(KB):
                    dve.wait_ge(hist_mm, KB * (i - 1) + k + 1)
                    one_hot(KB * i + k, k).then_inc(hist_oh, 1)

            with dve.Fori(0, NG // 2) as i:
                chain.enter(i, 2 * (2 * G + 1 + NEWTON))
                for s in range(2):
                    dve.wait_ge(xg_in[s], 32 * (i + 1))
                    for t in range(G):
                        chain.inc(v.bn_stats(stats[:, t, :], x_g[s][:, t, :]))
                    chain.wait()
                    dve.sem_inc(passed, 1)
                    for t in range(G):
                        chain.inc(v.bn_aggr(mvs[:, t, :], stats[:, t, :]))
                    chain.wait()
                    v_link(v.tensor_scalar(newt[:, 1, 0:G], mvs[:, :, 1], EPS_LN, None, ALU.add))
                    newton(newt[:, 1, 0:G], rs[:, :], newt[:, 0, 0:G])
                    for t in range(G):
                        v.tensor_scalar(x_g[s][:, t, :], x_g[s][:, t, :], mvs[:, t, 0:1], rs[:, t:t + 1],
                                        ALU.subtract, ALU.mult).then_inc(xn_ready, 1)
                    dve.wait_ge(xn_ready, 2 * G * i + G * (s + 1))
                    for t in range(G):
                        count(G * (2 * i + s) + t + 1)
            chain.leave(NG // 2)
            with dve.Fori(NT + 1, EQ) as i:
                count(i)

            dve.wait_ge(hist_mm, NB + 1)
            base4 = offs[:, 0, :].rearrange("p (t n) -> p t n", t=BT)
            h4 = offs[:, 8, :].rearrange("p (t n) -> p t n", t=BT)
            tot, grp, cs, cs2 = (offs[:, 2 + k, 0:NT] for k in range(4))
            v_link(v.tensor_scalar(beforef, cols[:, :], lane[:, 0:1], None, ALU.is_gt))
            v_link(v.tensor_copy(offs[0:EQ, 1, :], ps[0:EQ, RANK, 0:BT * NT]))
            v.sem_inc(base_ready, 1)
            dve.wait_ge(base_mm, 1)
            v_link(v.tensor_copy(offs[:, 8, :], ps[:, 1, 0:BT * NT]))
            v_link(v.tensor_tensor(tot, h4[:, 0, :], h4[:, 1, :], ALU.add))
            for t in range(2, BT):
                v_link(v.tensor_tensor(tot, tot, h4[:, t, :], ALU.add))
            v_link(v.tensor_scalar(grp.bitcast(I32), tot, float(GS - 1), None, ALU.add))
            v_link(v.tensor_scalar(grp.bitcast(I32), grp.bitcast(I32), 8, None, ALU.logical_shift_right))
            v_link(v.tensor_copy(grp, grp.bitcast(I32)))
            v_link(v.tensor_copy(cs, grp))
            a, b_, d = cs, cs2, 1
            while d < NT:
                v_link(v.tensor_copy(b_[:, 0:d], a[:, 0:d]))
                v_link(v.tensor_tensor(b_[:, d:NT], a[:, d:NT], a[:, 0:NT - d], ALU.add))
                a, b_, d = b_, a, 2 * d
            cs = a
            v_link(v.tensor_tensor(b_, cs, grp, ALU.subtract))
            v_link(v.tensor_scalar(base4[:, 0, :], b_, float(GS), float(GS), ALU.mult, ALU.add))
            for t in range(1, BT):
                v_link(v.tensor_tensor(base4[:, t, :], base4[:, t - 1, :], h4[:, t - 1, :], ALU.add))
            first, fpart = offs[0:EQ, 9, :].bitcast(I32), offs[0:EQ, 10, :].bitcast(I32)
            v_link(v.tensor_tensor(first, ps[0:EQ, 2, 0:BT * NT], offs[0:EQ, 0, :], ALU.add))
            v_link(v.tensor_scalar(fpart, first, LOW - 1, None, ALU.bitwise_and))
            v_link(v.tensor_copy(first_lo[:, :], fpart))
            v_link(v.tensor_scalar(fpart, first, 11, None, ALU.logical_shift_right))
            v_link(v.tensor_copy(first_hi[:, :], fpart))
            v_link(v.tensor_scalar(tk[:, 3:4], cs[:, NT - 1:NT], float(GS), float(GS), ALU.mult, ALU.add))
            v_link(v.tensor_scalar(pf_row[:, 0:NT], cs[0:1, :], float(GS), None, ALU.mult))
            v_link(v.tensor_scalar(pf_row[:, NT:], cols[0:1, 0:RG - 1], float(GS), tk[0:1, 3:4], ALU.mult, ALU.add))
            v_link(v.tensor_copy(meta[:, 0:1], cs[:, NT - 1:NT]))
            v_link(v.tensor_scalar(meta[:, 1:2], cs[:, NT - 1:NT], float(RG - 1), None, ALU.add))
            v_link(v.tensor_scalar(meta[:, 1:2], meta[:, 1:2], 3, None, ALU.logical_shift_right))
            v.sem_inc(meta_ready, 1)
            dve.wait_ge(viol_mm, 1)
            v.tensor_copy(meta[0:1, 2:3], ps[0:1, 3, 0:1]).then_inc(flag_ready, 1)
            gcol = offs[:, 6, 0:GJ]
            v_link(v.tensor_scalar(gcol, cols[:, 0:GJ], float(P), lane[:, 0:1], ALU.mult, ALU.add))
            v_link(v.tensor_tensor(bcmp, cs.unsqueeze(1).to_broadcast([P, GJ, NT]),
                                   gcol.unsqueeze(2).to_broadcast([P, GJ, NT]), ALU.is_lt))
            v_link(v.tensor_reduce(offs[:, 7, 0:GJ], bcmp, AX.X, ALU.add))
            v_link(v.tensor_scalar(gb_pj, offs[:, 7, 0:GJ], float(NT - 1), float(C), ALU.min, ALU.mult))
            v.sem_inc(gb_ready, 1)

            def make_oht(i, k):
                b = KB * i + k
                dve.wait_ge(relb_mm, b + 1)
                dve.wait_ge(main_mm, 2 * b + 6)
                v.tensor_scalar(oht[:, k % 2, :], ps[:, RELB, :], lane[:, 0:1], None,
                                ALU.is_equal).then_inc(oht_ready, 1)

            def make_ohb(i, k):
                dve.wait_ge(rank_mm, RANK0 + KB * i)
                one_hot(KB * i + k, k).then_inc(oh_ready, 1)

            def edges(i, k, more=True, oht_made=False):
                b = KB * i + k
                after = (i, k + 1) if k + 1 < KB else (i + 1, 0)
                if more and not oht_made:
                    make_oht(*after)
                dve.wait_ge(rank_mm, RANK0 + b + 1)
                dve.wait_ge(oh_ready, b + 1)
                for t in range(BT):
                    q = slice(t * NT, (t + 1) * NT)
                    v.tensor_tensor_reduce(out=scr[:, q], in0=ps[:, RANK, q], in1=ohb[:, k, q], scale=1.0, scalar=0.0,
                                           op0=ALU.mult, op1=ALU.add,
                                           accum_out=posf[:, BT * k + t:BT * k + t + 1]).then_inc(rank_read, 1)
                if more:
                    make_ohb(*after)
                dve.wait_ge(rows_left, b + 1)
                dve.wait_ge(rank_read, RREAD0 + BT * (b + 1))
                v.tensor_copy(posu[:, BT * k:BT * (k + 1)], posf[:, BT * k:BT * (k + 1)]).then_inc(pos_ready, 1)

            def elu(i, u):
                n = 2 * i + u
                dve.wait_ge(kv_acc, n + 1)
                v.tensor_copy(vext[:, u, :, P:P + 1],
                              maskc[:, ds(n, 1)].unsqueeze(1).to_broadcast([P, CC, 1])).then_inc(elu_v, 1)
                dve.wait_ge(elu_a, ELUA0 + 5 * n + 2)
                dve.wait_ge(q_free, i + 1)
                v.scalar_tensor_tensor(qTb[:, u, :], eq[:, u, :], 1.0, rq[:, u, :], ALU.min,
                                       ALU.add).then_inc(elu_v, 1)
                dve.wait_ge(elu_a, ELUA0 + 5 * n + 4)
                v.scalar_tensor_tensor(kk[:, u, :], ek[:, u, :], 1.0, rk[:, u, :], ALU.min,
                                       ALU.add).then_inc(elu_v, 1)

            for s in range(2):
                dve.wait_ge(xg_out[s], 48 * (NG // 2))
            make_oht(0, 0)
            make_ohb(0, 0)
            with dve.Fori(0, NT // 2) as i:
                edges(i, 0)
                edges(i, 1)
                elu(i, 0)
                edges(i, 2)
                elu(i, 1)
                edges(i, 3)

            dve.wait_ge(kv_acc, KVACC0 + NT + 1)
            for c in range(CC):
                for h in range(4):
                    q = slice(32 * h, 32 * h + 32)
                    chain.inc(v.tensor_copy(kvb[q, c, 32 * h:32 * h + 32],
                                            ps[q, KVA, c * (P + 1) + 32 * h:c * (P + 1) + 32 * h + 32]))
                    chain.inc(v.tensor_copy(kvb[q, c, P + h:P + h + 1],
                                            ps[q, KVA, c * (P + 1) + P:c * (P + 1) + P + 1]))
            chain.wait()
            v.sem_inc(kvb_ready, 1)
            dve.wait_ge(w_in, 16 * 12)
            dve.wait_ge(q_out, 16 * (NT // 2))

            def norm_stats(a, src2):
                for u in range(2):
                    chain.inc(v.bn_stats(stats[:, a + u, :], src2[:, u, :]))
                chain.wait()
                dve.sem_inc(passed, 1)
                for u in range(2):
                    chain.inc(v.bn_aggr(mvs[:, a + u, :], stats[:, a + u, :]))
                chain.wait()

            def norm_factors(a, n):
                v_link(v.tensor_scalar(newt[:, 1, a:a + n], mvs[:, a:a + n, 1], EPS_LN, None, ALU.add))
                newton(newt[:, 1, a:a + n], rs[:, a:a + n], newt[:, 0, a:a + n])

            def norm_apply(a, src2, out2, g_, b_, done):
                for u in range(2):
                    chain.inc(v.scalar_tensor_tensor(out2[:, u, :], src2[:, u, :], mvs[:, a + u, 0:1], vec[:, g_, :],
                                                     ALU.subtract, ALU.mult))
                chain.wait()
                for u in range(2):
                    done(v.scalar_tensor_tensor(out2[:, u, :], out2[:, u, :], rs[:, a + u:a + u + 1], vec[:, b_, :],
                                                ALU.mult, ALU.add))

            FRONT, BACK = 0, 2

            def attention(i):
                dve.wait_ge(t_mm, i + 1)
                den = ps[:, TPS:TPS + 2, 0:CC * (P + 4)].rearrange("p u (c f) -> p u c f", c=CC)
                for u in range(2):
                    chain.inc(v.tensor_scalar(rz[:, 8 * u:8 * u + 8].rearrange("p (c h) -> p c h", c=CC),
                                              den[:, u, :, P:P + 4], EPS_ATTN, None, ALU.add))
                chain.wait()
                v_link(v.reciprocal(rz[:, :], rz[:, :]))
                for u in range(2):
                    v.tensor_tensor(
                        tmp[:, u, :].rearrange("p (c h d) -> p c h d", c=CC, d=32),
                        den[:, u, :, 0:P].rearrange("p c (h d) -> p c h d", d=32),
                        rz[:, 8 * u:8 * u + 8].rearrange("p (c h) -> p c h", c=CC).unsqueeze(3).to_broadcast(
                            [P, CC, 4, 32]), ALU.mult).then_inc(t_read, 1)
                dve.wait_ge(t_read, TREAD0 + 2 * (i + 1))
                v.tensor_tensor(tmp, tmp, xnb, ALU.add).then_inc(xnb_read, 1)
                dve.wait_ge(xnb_read, i + 1)
                norm_stats(FRONT, tmp)

            def first_norm(i):
                norm_apply(FRONT, tmp, x1, LN1G, LN1B, lambda ins: ins.then_inc(x1_ready, 1))

            def residual(i):
                dve.wait_ge(y_mm, i + 1)
                dve.wait_ge(x1_ready, 2 * (i + 1))
                v_link(v.tensor_tensor(y2, ps[:, YPS, :].rearrange("p (u c) -> p u c", u=2), x1, ALU.add))
                norm_stats(BACK, y2)

            def second_norm(i):
                norm_apply(BACK, y2, y2, LN2G, LN2B, chain.inc)
                chain.wait()
                dve.wait_ge(x_in, 32 * (i + 1))
                v.tensor_tensor(acc[:, ds(2 * C * i, 2 * C)].rearrange("p (u c) -> p u c", u=2), y2, xb,
                                ALU.add).then_inc(mix_done, 1)

            def mix_step(i, front, back):
                e = NT // 2 + i
                edges(e, 0, oht_made=True)
                if front:
                    attention(i)
                edges(e, 1, oht_made=True)
                if back:
                    residual(i - 1)
                norm_factors(FRONT if front else BACK, 2 * (front + back))
                edges(e, 2, oht_made=True)
                if front:
                    first_norm(i)
                edges(e, 3, oht_made=True)
                if back:
                    second_norm(i - 1)

            mix_step(0, True, False)
            with dve.Fori(1, NT // 2) as i:
                chain.enter(i - 1, (3 + 4) + (1 + 4) + (1 + NEWTON) + 2 + 4)
                mix_step(i, True, True)
            chain.leave(NT // 2 - 1)
            mix_step(NT // 2, False, True)
            with dve.Fori(2 * (NT // 2) + 1, EQ - 1) as i:
                for k in range(KB):
                    edges(i, k)
            for k in range(KB):
                edges(EQ - 1, k, more=k + 1 < KB)

            dve.wait_ge(main_mm, MAIN0 + 2 * NB)
            steps = dve.value_load(meta[0:1, 1:2], min_val=1, max_val=NGMAX // RG + 1)

            with dve.Fori(0, steps) as i:
                for k in range(KB):
                    dve.wait_ge(r_in[k], 16 * (i + 1))
                    dve.wait_ge(grp_mm, RG * i + 2 * k + 6)
                    for s in range(BT):
                        r = BT * k + s
                        v.tensor_scalar(oht[:, k % 2, s * P:(s + 1) * P], cols[:, :], rowbuf[:, r, C + 1:C + 2],
                                        rowbuf[:, r, C:C + 1], ALU.is_equal, ALU.mult).then_inc(ohw_ready, 1)
            dve.wait_ge(acc_done, ACC0 + RG * steps)
            dve.sem_inc(passed, 1)

            wr_ = vec[:, WR:WR + 1, :].to_broadcast([P, G, C])
            with dve.Fori(0, NG // 2) as i:
                chain.enter(i, 2 * (2 * G + 1))
                for s in range(2):
                    n = 2 * i + s
                    for t in range(G):
                        chain.inc(v.bn_stats(stats[:, t, :], acc[:, ds(n * GC + t * C, C)]))
                    dve.wait_ge(prod_read, G * (n + 1))
                    v.tensor_tensor(prod[:, s, :, :], acc[:, ds(n * GC, GC)].rearrange("p (t c) -> p t c", t=G), wr_,
                                    ALU.mult).then_inc(prod_ready, 1)
                    chain.wait()
                    dve.sem_inc(passed, 1)
                    for t in range(G):
                        chain.inc(v.bn_aggr(mvs[:, t, :], stats[:, t, :]))
                    chain.wait()
                    v_link(v.tensor_copy(mv[:, ds(G * n, G), :], mvs[:, :, :]))
            chain.leave(NG // 2)
            dve.wait_ge(prod_read, PROD0 + NT)
            v_link(v.tensor_scalar(newt[:, 1, :], mv[:, :, 1], EPS_LN, None, ALU.add))
            newton(newt[:, 1, :], rstd[:, :], newt[:, 0, :])
            v_link(v.tensor_reduce(tk[:, 5:6], vec[:, WR, :], AX.X, ALU.add))
            v_link(v.tensor_scalar(scr[:, 0:NT], mv[:, :, 0], tk[:, 5:6], None, ALU.mult))
            v_link(v.tensor_tensor(wts[:, :], wts[:, :], scr[:, 0:NT], ALU.subtract))
            v_link(v.tensor_tensor(wts[:, :], wts[:, :], rstd[:, :], ALU.mult))
            v_link(v.tensor_scalar(wts[:, :], wts[:, :], br_c[:, 0:1], None, ALU.add))

            def normed(out, col, tile):
                return v.tensor_scalar(out, acc[:, ds(col, C)], mv[:, ds(tile, 1), 0], rstd[:, ds(tile, 1)],
                                       ALU.subtract, ALU.mult)

            wm, pen = scr[:, 0:NT], scr[:, NT:2 * NT]
            v_link(v.tensor_scalar(pen, maskc[:, :], -1.0, 3.0e38, ALU.add, ALU.mult))
            v_link(v.tensor_tensor(wm, wts[:, :], maskc[:, :], ALU.mult))
            v_link(v.tensor_tensor(wm, wm, pen, ALU.add))
            key, taken = tki[:, 0:1], tki[:, 1:2]
            v_link(v.memset(key, 0))
            hits = x3[0][:, 0:3 * NT].rearrange("p (k n) -> p k n", k=3)

            def decode(c, sign, thr):
                v_link(v.tensor_scalar(sign, c, 31, None, ALU.arith_shift_right))
                v_link(v.tensor_scalar(sign, sign, -1, SIGN, ALU.bitwise_xor, ALU.bitwise_or))
                v_link(v.tensor_tensor(thr, c, sign, ALU.bitwise_xor))

            with dve.Fori(0, 16) as i:
                chain.enter(i, 12)
                pair = bits[:, ds(15 - i, 1), 0:3].rearrange("p a k -> p (a k)")
                turn = bits[:, ds(15 - i, 1), 3:6].rearrange("p a k -> p (a k)")
                v_link(v.tensor_tensor(candi[:, 0, :], key.to_broadcast([P, 3]), pair, ALU.bitwise_or))
                decode(candi[:, 0, :], candi[:, 1, :], candi[:, 2, :])
                for k in range(3):
                    chain.inc(v.tensor_scalar(hits[:, k, :], wm, cands[:, 2, k:k + 1], None, ALU.is_ge))
                chain.wait()
                with nc.allow_low_precision("counts below 128"):
                    v.tensor_reduce(cntb[:, :], hits, AX.X, ALU.add).then_inc(cnt_ready, 1)
                dve.wait_ge(cnt_mm, i + 1)
                v_link(v.tensor_scalar(candi[:, 3, :], ps[:, 0, 0:3], float(KEEP), -1.0, ALU.is_ge, ALU.mult))
                v_link(v.tensor_tensor(candi[:, 3, :], candi[:, 3, :], turn, ALU.bitwise_and))
                for k in range(3):
                    v_link(v.tensor_tensor(key, key, candi[:, 3, k:k + 1], ALU.bitwise_xor))
            chain.leave(16)
            decode(key, taken, tki[:, 3:4])
            gt, eqm = ohb[:, 0, 0:NT], ohb[:, 1, 0:NT]
            v_link(v.tensor_scalar(gt, wm, tk[:, 3:4], None, ALU.is_gt))
            v.tensor_scalar(eqm, wm, tk[:, 3:4], None, ALU.is_equal).then_inc(final_cnt, 1)
            dve.wait_ge(final_mm, 1)
            v_link(v.tensor_reduce(tk[:, 4:5], ps[:, 0, 0:NT], AX.X, ALU.add))
            v_link(v.tensor_scalar(tk[:, 4:5], tk[:, 4:5], -1.0, float(KEEP), ALU.mult, ALU.add))

            def prefix(total, low, e0):
                a, b_, d = scr[:, NT:2 * NT], scr[:, 2 * NT:3 * NT], 1
                v_link(v.tensor_copy(e0, total))
                v_link(v.tensor_copy(a, e0))
                while d < NT:
                    v_link(v.tensor_copy(b_[:, 0:d], a[:, 0:d]))
                    v_link(v.tensor_tensor(b_[:, d:NT], a[:, d:NT], a[:, 0:NT - d], ALU.add))
                    a, b_, d = b_, a, 2 * d
                v_link(v.tensor_tensor(a, a, e0, ALU.subtract))
                v_link(v.tensor_tensor(a, a, low, ALU.add))
                return a, b_

            e0 = scr[:, 3 * NT:4 * NT]
            a, _ = prefix(ps[:, 1, 0:NT], ps[:, 2, 0:NT], e0)
            v_link(v.tensor_scalar(a, a, tk[:, 4:5], None, ALU.is_lt))
            v_link(v.tensor_tensor(a, a, eqm, ALU.mult))
            v_link(v.tensor_tensor(a, a, gt, ALU.add))
            v_link(v.tensor_tensor(wts[:, :], wts[:, :], a, ALU.mult))

            take, other = ohb[:, 2, 0:NT], scr[:, 0:NT]
            v_link(v.tensor_copy(take, a))
            v.sem_inc(take_ready, 1)
            v_link(v.tensor_scalar(other, a, -1.0, 1.0, ALU.mult, ALU.add))
            v_link(v.tensor_scalar(idx[:, :], cols[:, 0:NT], float(P), lane[:, 0:1], ALU.mult, ALU.add))
            dve.wait_ge(take_mm, 1)
            a, b_ = prefix(ps[:, 3, 0:NT], ps[:, 3, NT:2 * NT], e0)
            v_link(v.scalar_tensor_tensor(b_, a, -2.0, idx[:, :], ALU.mult, ALU.add))
            v_link(v.scalar_tensor_tensor(b_, b_, float(KEEP), other, ALU.add, ALU.mult))
            v_link(v.tensor_tensor(place[:, :], a, b_, ALU.add))

            with dve.Fori(0, NG // 2) as i:
                for s in range(2):
                    n = 2 * i + s
                    dve.wait_ge(sel_left, n + 1)
                    for t in range(G):
                        normed(rowbuf[:, s * G + t, 0:C], n * GC + t * C, G * n + t).then_inc(sel_ready, 1)
                    for k, col in enumerate((wts, idx)):
                        v.tensor_copy(rowbuf[:, s * G:(s + 1) * G, C + k], col[:, ds(G * n, G)]).then_inc(sel_ready, 1)
                    v.tensor_copy(posu[:, s * G:(s + 1) * G], place[:, ds(G * n, G)]).then_inc(sel_ready, 1)
                    dve.wait_ge(sel_ready, (G + 3) * n + G)
                    dve.wait_ge(base_free, n + 1)
                    v.tensor_tensor(x3[s].rearrange("p (t c) -> p t c", t=G), rowbuf[:, s * G:(s + 1) * G, 0:C],
                                    acc[:, ds(n * GC, GC)].rearrange("p (t c) -> p t c", t=G),
                                    ALU.add).then_inc(rows_ready, 1)

            def numbers(i, s, turn):
                dve.wait_ge(fo_free, i + 1)
                dve.wait_ge(xc_in[s], 16 * (turn + 1))
                v.tensor_copy(idu[:, s, :], xc[s][:, :, C + 1]).then_inc(idu_ready, 1)

            def ffn_out(i, s, turn):
                dve.wait_ge(fy_mm, i + 1)
                v_link(v.tensor_tensor(fy[:, s, :].rearrange("p (u c) -> p u c", u=2),
                                       ps[:, 4 + s, :].rearrange("p (u c) -> p u c", u=2),
                                       vec[:, FB2:FB2 + 1, :].to_broadcast([P, 2, C]), ALU.add))
                dve.wait_ge(base_in[s], 32 * (turn + 1))
                for u in range(2):
                    q = slice(u * C, (u + 1) * C)
                    v.scalar_tensor_tensor(fo[:, s, q], fy[:, s, q], xc[s][:, u, C:C + 1], base[:, s, q],
                                           ALU.mult, ALU.add).then_inc(o_ready, 1)

            numbers(0, 0, 0)
            with dve.Fori(0, FP // 2) as i:
                chain.enter(i, 2)
                numbers(2 * i + 1, 1, i)
                ffn_out(2 * i, 0, i)
                numbers(2 * i + 2, 0, i + 1)
                ffn_out(2 * i + 1, 1, i)
            chain.leave(FP // 2)
            ffn_out(FP - 1, 0, FP // 2)


class Chain:

    def __init__(self, eng, sem):
        self.eng, self.sem, self.n, self.i = eng, sem, 0, None

    def inc(self, ins):
        ins.then_inc(self.sem, 1)
        self.n += 1

    def enter(self, i, per):
        self.before, self.n, self.i, self.per = self.n, 0, i, per

    def leave(self, count):
        assert self.n == self.per, (self.n, self.per)
        self.n, self.i = self.before + count * self.per, None

    def wait(self):
        at = self.n if self.i is None else self.before + self.i * self.per + self.n
        self.eng.wait_ge(self.sem, at)

    def link(self, ins):
        self.inc(ins)
        self.wait()


_INS = ["x", "src", "dst", "edge_weight", "L0_gnn_weight", "L0_mix_Wqkv", "L0_mix_ln1_g", "L0_mix_ln1_b",
        "L0_mix_W1", "L0_mix_b1", "L0_mix_W2", "L0_mix_b2", "L0_mix_ln2_g", "L0_mix_ln2_b", "L0_ffn_wr",
        "L0_ffn_br", "L0_ffn_w1", "L0_ffn_b1", "L0_ffn_w2", "L0_ffn_b2"]


def kernel(**inputs):
    import numpy as _np
    import concourse.bacc as _bacc
    from concourse import mybir as _mybir
    from concourse.bass_utils import run_bass_kernel_spmd as _run

    nc = _bacc.Bacc("TRN2", target_bir_lowering=False, num_devices=1)
    arrays, args = {}, []
    for name in _INS:
        a = _np.ascontiguousarray(inputs[name])
        arrays[f"in_{name}"] = a
        args.append(nc.dram_tensor(f"in_{name}", a.shape, _mybir.dt.from_np(a.dtype), kind="ExternalInput").ap())
    args.append(nc.dram_tensor("out_rows", (N, C), _mybir.dt.float32, kind="ExternalOutput").ap())
    gps_layer_kernel(nc, *args)
    r = _run(nc, [arrays], core_ids=[0])
    return r.results[0]["out_rows"]
```
